# Optimizing a Trainium2 kernel written in Bass

```python
import numpy as np
import jax
import jax.numpy as jnp

def _softmax(x, axis=-1):
    return jax.nn.softmax(x, axis=axis)

def _gelu(x):
    return jax.nn.gelu(x, approximate=True)

def _silu(x):
    return jax.nn.silu(x)

def _sigmoid(x):
    return jax.nn.sigmoid(x)

def _layernorm(x, axis=-1, eps=1e-05):
    m = jnp.mean(x, axis=axis, keepdims=True)
    v = jnp.var(x, axis=axis, keepdims=True)
    return (x - m) / jnp.sqrt(v + eps)

def _scatter_add(tgt, idx, src, axis=0):
    return tgt.at[idx].add(src)

def _segment_sum(src, seg, n):
    return jax.ops.segment_sum(src, seg, n)
kernel_name = 'mk_flamingo_gated_d2_seqx_r8_dcee32'

def setup_inputs(seed: int=0):
    np.random.seed(seed)
    _w = jnp.asarray

    def _rec_inputs():
        import jax
        import jax.numpy as jnp
        _rk = jax.random.key(seed)
        x = -0.0002928 + 1 * jax.random.normal(jax.random.fold_in(_rk, 1), (8, 256, 128), jnp.float32)
        _lenS = 256 - jax.random.randint(jax.random.fold_in(_rk, 7), (8,), 0, max(1, 256 // 4) + 1, jnp.int32)
        _lenS2 = 256 - jax.random.randint(jax.random.fold_in(_rk, 8), (8,), 0, max(1, 256 // 4) + 1, jnp.int32)
        _ctx_512P = jax.random.normal(jax.random.fold_in(_rk, 11), (8, 16, 64), jnp.float32)
        _ctx_512c = jax.random.dirichlet(jax.random.fold_in(_rk, 511), 0.3 * jnp.ones((16,), jnp.float32), (8, 256))
        _ctx_512t = jnp.einsum('bsk,bkd->bsd', _ctx_512c, _ctx_512P)
        _ctx_512t = _ctx_512t * jax.lax.rsqrt(jnp.mean(jnp.square(_ctx_512t)) + 1e-12) * 0.953939
        ctx_512 = 0.00222621 + 0.99962 * (_ctx_512t + 0.3 * jax.random.normal(jax.random.fold_in(_rk, 611), (8, 256, 64), jnp.float32))
        _g = jax.random.normal(jax.random.fold_in(_rk, 9001), (2, 2), jnp.float32)
        _g = jnp.sign(_g) * jnp.maximum(jnp.abs(_g), 1.0) + (_g == 0) * 1.0
        g_xattn = _g[0]
        g_ffn = _g[1]
        return (x, ctx_512, g_xattn, g_ffn)
    x, ctx_512, g_xattn, g_ffn = _rec_inputs()

    def _L0_xattn_setup():
        import jax, jax.numpy as jnp
        import numpy as np
        B, T, TC, C, CC, H = (2, 256, 64, 128, 64, 16)
        D = C // H

        def _heads(t):
            b, l, _ = t.shape
            return t.reshape(b, l, H, D).transpose(0, 2, 1, 3)
        key = jax.random.key(seed)
        ks = jax.random.split(key, 18)
        w = lambda k, i, o: jax.random.normal(k, (i, o), jnp.float32) / np.sqrt(i).astype(np.float32)
        return {'x': jax.random.normal(ks[0], (B, T, C), jnp.float32), 'cross_input': jax.random.normal(ks[1], (B, TC, CC), jnp.float32), 'Wk': w(ks[2], C, C), 'bk': jnp.zeros((C,), jnp.float32), 'Wq': w(ks[3], C, C), 'bq': jnp.zeros((C,), jnp.float32), 'Wv': w(ks[4], C, C), 'bv': jnp.zeros((C,), jnp.float32), 'Wck': w(ks[5], CC, C), 'bck': jnp.zeros((C,), jnp.float32), 'Wcq': w(ks[6], C, C), 'bcq': jnp.zeros((C,), jnp.float32), 'Wcv': w(ks[7], CC, C), 'bcv': jnp.zeros((C,), jnp.float32), 'Wp': w(ks[8], C, C), 'bp': jnp.zeros((C,), jnp.float32)}
    _L0_xattn_all = _L0_xattn_setup()
    _L0_xattn_in = {k: v for k, v in _L0_xattn_all.items() if k in ('Wk', 'bk', 'Wq', 'bq', 'Wv', 'bv', 'Wck', 'bck', 'Wcq', 'bcq', 'Wcv', 'bcv', 'Wp', 'bp')}
    del _L0_xattn_all

    def _L0_ffn_setup():
        import jax, jax.numpy as jnp
        import numpy as np
        N_EMBED = 128
        FFN_HIDDEN = 512
        NUM_EXPERTS = 8
        TOP_K = 2
        key = jax.random.key(seed)
        ks = jax.random.split(key, 8)
        d, f, E = (N_EMBED, FFN_HIDDEN, NUM_EXPERTS)
        s_d = 1.0 / np.sqrt(d)
        s_f = 1.0 / np.sqrt(f)
        return {'x': jax.random.normal(ks[0], (2, 256, d), dtype=jnp.float32), 'Wg': jax.random.uniform(ks[1], (d, E), jnp.float32, -s_d, s_d), 'bg': jax.random.uniform(ks[2], (E,), jnp.float32, -s_d, s_d), 'W1': jax.random.uniform(ks[3], (E, d, f), jnp.float32, -s_d, s_d), 'b1': jax.random.uniform(ks[4], (E, f), jnp.float32, -s_d, s_d), 'W2': jax.random.uniform(ks[5], (E, f, d), jnp.float32, -s_f, s_f), 'b2': jax.random.uniform(ks[6], (E, d), jnp.float32, -s_f, s_f)}
    _L0_ffn_all = _L0_ffn_setup()
    _L0_ffn_in = {k: v for k, v in _L0_ffn_all.items() if k in ('Wg', 'bg', 'W1', 'b1', 'W2', 'b2')}
    del _L0_ffn_all

    def _L1_xattn_setup():
        import jax, jax.numpy as jnp
        import numpy as np
        B, LQ, LK = (8, 256, 256)
        QD, KD, VD = (128, 64, 64)
        key = jax.random.key(seed)
        ks = jax.random.split(key, 9)
        s = 0.02
        return {'query': jax.random.normal(ks[0], (B, LQ, QD), jnp.float32), 'key': jax.random.normal(ks[1], (B, LK, KD), jnp.float32), 'value': jax.random.normal(ks[2], (B, LK, VD), jnp.float32), 'Wq': jax.random.normal(ks[3], (QD, QD), jnp.float32) * s, 'bq': jnp.zeros((QD,), jnp.float32), 'Wk': jax.random.normal(ks[4], (KD, QD), jnp.float32) * s, 'bk': jnp.zeros((QD,), jnp.float32), 'Wv': jax.random.normal(ks[5], (VD, QD), jnp.float32) * s, 'bv': jnp.zeros((QD,), jnp.float32)}
    _L1_xattn_all = _L1_xattn_setup()
    _L1_xattn_in = {k: v for k, v in _L1_xattn_all.items() if k in ('Wq', 'bq', 'Wk', 'bk', 'Wv', 'bv')}
    del _L1_xattn_all

    def _L1_ffn_setup():
        import jax, jax.numpy as jnp
        import numpy as np
        EPS = 1e-06
        LN_EPS = 1e-05

        def _absmean_core(W):
            gamma = jnp.mean(jnp.abs(W)) + EPS
            Ws = W / gamma
            Wq = jnp.sign(Ws) * jnp.minimum(jnp.round(jnp.abs(Ws)), 1.0)
            return (Wq, gamma)

        @jax.custom_vjp
        def absmean(W):
            return _absmean_core(W)[0]

        def _absmean_fwd(W):
            Wq, gamma = _absmean_core(W)
            return (Wq, gamma)

        def _absmean_bwd(gamma, g):
            return (g / gamma,)
        absmean.defvjp(_absmean_fwd, _absmean_bwd)

        def layernorm(x, w, b, eps=LN_EPS):
            mu = jnp.mean(x, axis=-1, keepdims=True)
            var = jnp.mean((x - mu) ** 2, axis=-1, keepdims=True)
            return (x - mu) * jax.lax.rsqrt(var + eps) * w + b
        key = jax.random.key(seed)
        k1, k2, k3 = jax.random.split(key, 3)
        d, h = (128, 512)
        B, T = (8, 256)
        return {'x': jax.random.normal(k1, (B, T, d), jnp.float32), 'W_fc': jax.random.normal(k2, (h, d), jnp.float32), 'ln_w': jnp.ones((h,), jnp.float32), 'ln_b': jnp.zeros((h,), jnp.float32), 'W_proj': jax.random.normal(k3, (d, h), jnp.float32)}
    _L1_ffn_all = _L1_ffn_setup()
    _L1_ffn_in = {k: v for k, v in _L1_ffn_all.items() if k in ('W_fc', 'ln_w', 'ln_b', 'W_proj')}
    del _L1_ffn_all
    return {'x': x, 'ctx_512': ctx_512, 'g_xattn': g_xattn, 'g_ffn': g_ffn, 'L0_xattn_Wk': _L0_xattn_in['Wk'], 'L0_xattn_bk': _L0_xattn_in['bk'], 'L0_xattn_Wq': _L0_xattn_in['Wq'], 'L0_xattn_bq': _L0_xattn_in['bq'], 'L0_xattn_Wv': _L0_xattn_in['Wv'], 'L0_xattn_bv': _L0_xattn_in['bv'], 'L0_xattn_Wck': _L0_xattn_in['Wck'], 'L0_xattn_bck': _L0_xattn_in['bck'], 'L0_xattn_Wcq': _L0_xattn_in['Wcq'], 'L0_xattn_bcq': _L0_xattn_in['bcq'], 'L0_xattn_Wcv': _L0_xattn_in['Wcv'], 'L0_xattn_bcv': _L0_xattn_in['bcv'], 'L0_xattn_Wp': _L0_xattn_in['Wp'], 'L0_xattn_bp': _L0_xattn_in['bp'], 'L0_ffn_Wg': _L0_ffn_in['Wg'], 'L0_ffn_bg': _L0_ffn_in['bg'], 'L0_ffn_W1': _L0_ffn_in['W1'], 'L0_ffn_b1': _L0_ffn_in['b1'], 'L0_ffn_W2': _L0_ffn_in['W2'], 'L0_ffn_b2': _L0_ffn_in['b2'], 'L1_xattn_Wq': _L1_xattn_in['Wq'], 'L1_xattn_bq': _L1_xattn_in['bq'], 'L1_xattn_Wk': _L1_xattn_in['Wk'], 'L1_xattn_bk': _L1_xattn_in['bk'], 'L1_xattn_Wv': _L1_xattn_in['Wv'], 'L1_xattn_bv': _L1_xattn_in['bv'], 'L1_ffn_W_fc': _L1_ffn_in['W_fc'], 'L1_ffn_ln_w': _L1_ffn_in['ln_w'], 'L1_ffn_ln_b': _L1_ffn_in['ln_b'], 'L1_ffn_W_proj': _L1_ffn_in['W_proj']}

def reference(x, ctx_512, g_xattn, g_ffn, L0_xattn_Wk, L0_xattn_bk, L0_xattn_Wq, L0_xattn_bq, L0_xattn_Wv, L0_xattn_bv, L0_xattn_Wck, L0_xattn_bck, L0_xattn_Wcq, L0_xattn_bcq, L0_xattn_Wcv, L0_xattn_bcv, L0_xattn_Wp, L0_xattn_bp, L0_ffn_Wg, L0_ffn_bg, L0_ffn_W1, L0_ffn_b1, L0_ffn_W2, L0_ffn_b2, L1_xattn_Wq, L1_xattn_bq, L1_xattn_Wk, L1_xattn_bk, L1_xattn_Wv, L1_xattn_bv, L1_ffn_W_fc, L1_ffn_ln_w, L1_ffn_ln_b, L1_ffn_W_proj):
    import jax
    import jax.numpy as jnp

    def _L0_xattn_ref(x, cross_input, Wk, bk, Wq, bq, Wv, bv, Wck, bck, Wcq, bcq, Wcv, bcv, Wp, bp):
        import jax, jax.numpy as jnp
        import numpy as np
        B, T, TC, C, CC, H = (2, 256, 64, 128, 64, 16)
        D = C // H

        def _heads(t):
            b, l, _ = t.shape
            return t.reshape(b, l, H, D).transpose(0, 2, 1, 3)
        scale = np.float32(1.0 / np.sqrt(D))
        q = _heads(x @ Wq + bq)
        k = _heads(x @ Wk + bk)
        v = _heads(x @ Wv + bv)
        att = jnp.einsum('bhqd,bhkd->bhqk', q, k) * scale
        causal = jnp.tril(jnp.ones((T, T), bool))
        att = jnp.where(causal[None, None], att, -jnp.inf)
        y = jnp.einsum('bhqk,bhkd->bhqd', jax.nn.softmax(att, axis=-1), v)
        qc = _heads(x @ Wcq + bcq)
        kc = _heads(cross_input @ Wck + bck)
        vc = _heads(cross_input @ Wcv + bcv)
        attc = jnp.einsum('bhqd,bhkd->bhqk', qc, kc) * scale
        y = y + jnp.einsum('bhqk,bhkd->bhqd', jax.nn.softmax(attc, axis=-1), vc)
        y = y.transpose(0, 2, 1, 3).reshape(x.shape[0], T, C)
        return y @ Wp + bp

    def _L0_ffn_ref(x, Wg, bg, W1, b1, W2, b2):
        import jax, jax.numpy as jnp
        import numpy as np
        N_EMBED = 128
        FFN_HIDDEN = 512
        NUM_EXPERTS = 8
        TOP_K = 2
        gate_scores = jax.nn.softmax(x @ Wg + bg, axis=-1)
        topk_scores, topk_idx = jax.lax.top_k(gate_scores, TOP_K)
        topk_scores = topk_scores / (jnp.sum(topk_scores, axis=-1, keepdims=True) + 1e-08)
        onehot = jax.nn.one_hot(topk_idx, NUM_EXPERTS, dtype=x.dtype)
        combine_w = jnp.einsum('bsk,bske->bse', topk_scores, onehot)
        output = jnp.zeros_like(x)
        for e in range(NUM_EXPERTS):
            h = jax.nn.gelu(x @ W1[e] + b1[e])
            y = h @ W2[e] + b2[e]
            output = output + y * combine_w[..., e:e + 1]
        return output

    def _L1_xattn_ref(query, key, value, Wq, bq, Wk, bk, Wv, bv):
        import jax, jax.numpy as jnp
        import numpy as np
        B, LQ, LK = (8, 256, 256)
        QD, KD, VD = (128, 64, 64)
        q = jnp.einsum('bld,de->ble', query, Wq) + bq
        k = jnp.einsum('bld,de->ble', key, Wk) + bk
        v = jnp.einsum('bld,de->ble', value, Wv) + bv
        scores = jnp.einsum('bqe,bke->bqk', q, k)
        attn = jax.nn.softmax(scores, axis=-1)
        out = jnp.einsum('bqk,bke->bqe', attn, v)
        return out

    def _L1_ffn_ref(x, W_fc, ln_w, ln_b, W_proj):
        import jax, jax.numpy as jnp
        import numpy as np
        EPS = 1e-06
        LN_EPS = 1e-05

        def _absmean_core(W):
            gamma = jnp.mean(jnp.abs(W)) + EPS
            Ws = W / gamma
            Wq = jnp.sign(Ws) * jnp.minimum(jnp.round(jnp.abs(Ws)), 1.0)
            return (Wq, gamma)

        @jax.custom_vjp
        def absmean(W):
            return _absmean_core(W)[0]

        def _absmean_fwd(W):
            Wq, gamma = _absmean_core(W)
            return (Wq, gamma)

        def _absmean_bwd(gamma, g):
            return (g / gamma,)
        absmean.defvjp(_absmean_fwd, _absmean_bwd)

        def layernorm(x, w, b, eps=LN_EPS):
            mu = jnp.mean(x, axis=-1, keepdims=True)
            var = jnp.mean((x - mu) ** 2, axis=-1, keepdims=True)
            return (x - mu) * jax.lax.rsqrt(var + eps) * w + b
        h = jnp.einsum('btd,hd->bth', x, absmean(W_fc))
        h = jax.nn.gelu(h, approximate=False)
        h = layernorm(h, ln_w, ln_b)
        return jnp.einsum('bth,dh->btd', h, absmean(W_proj))
    x = x + jnp.tanh(g_xattn[0]) * _L0_xattn_ref(_layernorm(x, axis=-1), ctx_512, L0_xattn_Wk, L0_xattn_bk, L0_xattn_Wq, L0_xattn_bq, L0_xattn_Wv, L0_xattn_bv, L0_xattn_Wck, L0_xattn_bck, L0_xattn_Wcq, L0_xattn_bcq, L0_xattn_Wcv, L0_xattn_bcv, L0_xattn_Wp, L0_xattn_bp)
    x = x + jnp.tanh(g_ffn[0]) * _L0_ffn_ref(_layernorm(x, axis=-1), L0_ffn_Wg, L0_ffn_bg, L0_ffn_W1, L0_ffn_b1, L0_ffn_W2, L0_ffn_b2)
    x = x + jnp.tanh(g_xattn[1]) * _L1_xattn_ref(_layernorm(x, axis=-1), ctx_512, ctx_512, L1_xattn_Wq, L1_xattn_bq, L1_xattn_Wk, L1_xattn_bk, L1_xattn_Wv, L1_xattn_bv)
    x = x + jnp.tanh(g_ffn[1]) * _L1_ffn_ref(_layernorm(x, axis=-1), L1_ffn_W_fc, L1_ffn_ln_w, L1_ffn_ln_b, L1_ffn_W_proj)
    return x

_drawn_inputs = setup_inputs


def setup_inputs(seed=0):
    import zlib

    import numpy as np

    out = dict(_drawn_inputs(seed))
    spreads = {'g_ffn': (-1.0, 0.2),
     'L0_xattn_bk': (0.0, 0.8),
     'L0_xattn_bq': (0.0, 0.392),
     'L0_xattn_bv': (0.0, 0.1),
     'L0_xattn_bck': (0.0, 0.8),
     'L0_xattn_bcq': (0.0, 0.342),
     'L0_xattn_bcv': (0.0, 0.1),
     'L0_xattn_bp': (0.0, 0.1),
     'L1_xattn_bq': (0.0, 0.8),
     'L1_xattn_bk': (0.0, 0.8),
     'L1_xattn_bv': (0.0, 0.1),
     'L1_ffn_ln_w': (1.0, 0.2),
     'L1_ffn_ln_b': (0.0, 0.1)}
    factors = {'L0_ffn_b1': 5.221, 'L0_ffn_b2': 3.766, 'L1_xattn_Wq': 4.092, 'L1_xattn_Wk': 4.024}
    for name, (base, spread) in spreads.items():
        noise = np.random.default_rng([zlib.crc32(name.encode()), seed]).standard_normal(out[name].shape)
        drawn = base * np.exp(spread * noise) if base else spread * noise
        out[name] = jnp.asarray(drawn.astype(out[name].dtype))
    for name, factor in factors.items():
        out[name] = (out[name] * factor).astype(out[name].dtype)
    return out
```

```python
from contextlib import ExitStack

import concourse.bass as bass
from concourse import mybir

F32 = mybir.dt.float32
F16 = mybir.dt.float16
BF16 = mybir.dt.bfloat16
ALU = mybir.AluOpType
ACT = mybir.ActivationFunctionType
AX = mybir.AxisListType

P = 128
B, T, C = 8, 256, 128
CC = 64
H, D = 16, 8
E, F = 8, 512
TT = T // P
FC = F // P
SH = 4
SLOT = P // SH
ONES = 3 * D
LN_EPS = 1e-5
MASKED = -1e30
SHIFT_MAX = 60000.0

PER_BATCH = dict(
    x_in=16, ctx_in=16,
    a_stats=TT, a_mv=TT, a_var=1, a_rstd=1, a_xn=TT, a_tr=1, a_ctx_tr=1, a_xT=1, a_cT=1,
    stack_ps=4, stack_hi=4, stack=4, qm_self=H, qm_cross=H, v_ps=1, v_pad=2,
    max_ps=14, max_out=14, maxT_ps=2, shift=2, shift_self_in=16, shift_cross_in=16,
    score_ps=14, probs=14, probs_masked=6, pv=14,
    o_sb=2, oT_ps=1, o_rec=1, o_num=1, y=1, yT_ps=1, yT=1, wp_ps=1, xb=1, x1=1,
    b_stats=TT, b_mv=TT, b_var=1, b_rstd=1, b_xn=TT, b_tr=1, b_xT=1,
    gate_ps=1, gate=17, gate_e=1, gate_w=1, wT_ps=1, wT=1, b2_ps=1,
    h_ps=E, h=E, y_ps=E, acc=2 * E + 1,
    ctxb_in=16,
    c_stats=TT, c_mv=TT, c_var=1, c_rstd=1, c_xn=TT, c_tr=1, c_xT=1, cb_tr=1, cb_cT=1,
    q1_ps=1, q1=1, v1_ps=1, v1=1, s1_ps=1, s1_max=1, p1=2, p1T_ps=1, p1T=1, s1_rec=1, s1_scale=1, o1_ps=1, x3=2,
    d_stats=TT, d_mv=TT, d_var=1, d_rstd=1, d_xn=TT, d_tr=1, d_xT=1,
    f_ps=1, f=1, g_stats=TT, g_mv=TT, g_var=1, g_rstd=1, z=TT, zT_ps=1, zT=1, f2_ps=1, x3b=1, xo=1, out=16,
)
SETUP = ["w_in", "ctxw_in", "w1_in", "w2_in", "raw_zero", "ctxw_zero", "consts", "masks", "cen_ps", "cen", "bias_in", "expand",
         "ones_in", "gates", "fold", "bp_in", "lnw_in", "wf_in", "absum", "gamma_ps", "gamma", "tern", "ternT_ps", "ternT",
         "cb_ps", "cb", "zeros", "link",
         "pool_passed", "dve_passed"]


def flamingo(nc, x, ctx_512, g_xattn, g_ffn, L0_xattn_Wk, L0_xattn_bk, L0_xattn_Wq, L0_xattn_bq, L0_xattn_Wv, L0_xattn_bv,
             L0_xattn_Wck, L0_xattn_bck, L0_xattn_Wcq, L0_xattn_bcq, L0_xattn_Wcv, L0_xattn_bcv, L0_xattn_Wp, L0_xattn_bp,
             L0_ffn_Wg, L0_ffn_bg, L0_ffn_W1, L0_ffn_b1, L0_ffn_W2, L0_ffn_b2, L1_xattn_Wq, L1_xattn_bq, L1_xattn_Wk,
             L1_xattn_bk, L1_xattn_Wv, L1_xattn_bv, L1_ffn_W_fc, L1_ffn_ln_w, L1_ffn_ln_b, L1_ffn_W_proj, out):
    with ExitStack() as ctx:
        def sb(name, shape, dt=F32):
            return ctx.enter_context(nc.sbuf_tensor(name, shape, dt))

        def row(ap):
            return ap.rearrange("(a n) -> a n", a=1)

        sems = {name: ctx.enter_context(nc.semaphore("s_" + name)) for name in [*PER_BATCH, *SETUP]}

        ident = sb("ident", [P, P])
        identb = sb("identb", [P, P], BF16)
        causal = sb("causal", [P, P], BF16)
        center = sb("center", [P, P])
        raw = sb("raw", [P, 6, P])
        cw = sb("cw", [P, 6, P])
        cxw = sb("cxw", [P, 4, P])
        w1raw = sb("w1raw", [P, E * F])
        w1 = sb("w1", [P, E, FC, P])
        w2 = sb("w2", [P, E, FC, P])
        b2 = sb("b2", [P, P])
        wstack = sb("wstack", [P, 4, H // SH, SH, SLOT])
        lo_q = sb("lo_q", [P, 1])
        lo_k = sb("lo_k", [P, 1])
        head_mask = sb("head_mask", [P, SH])
        low8 = sb("low8", [P, 2, SH])
        wp = sb("wp", [P, P])
        bp = sb("bp", [P, P])
        graw = sb("graw", [P, 4])
        gates = sb("gates", [P, 4])
        onesrow = sb("onesrow", [1, H])
        spare = sb("spare", [P, 1])
        rank = sb("rank", [P, E])
        minus_half = sb("minus_half", [P, TT])
        eps = sb("eps", [P, TT])
        wfc_raw = sb("wfc_raw", [P, FC, P])
        wpr_raw = sb("wpr_raw", [P, F])
        absum = sb("absum", [P, 2])
        ones = sb("ones", [P, P])
        thr = sb("thr", [P, 2, 2])
        tern = sb("tern", [P, 2, F])
        tneg = sb("tneg", [P, F])
        wfcT = sb("wfcT", [P, F])
        wprT = sb("wprT", [P, FC, P])
        wprT0 = sb("wprT0", [P, FC, P])
        lnw = sb("lnw", [P, FC])
        lnwg = sb("lnwg", [P, FC])
        lnb = sb("lnb", [P, FC])
        lnbb = sb("lnbb", [P, FC, P])
        cb = sb("cb", [P, P])

        xin = sb("xin", [P, TT, C])
        cin = sb("cin", [P, TT, P])
        xn = {k: sb("xn_" + k, [P, TT, C]) for k in "abcd"}
        stats = {k: sb("stats_" + k, [P, TT, 6]) for k in "abcdg"}
        mv = {k: sb("mv_" + k, [P, TT, 2]) for k in "abcdg"}
        var = {k: sb("var_" + k, [P, TT]) for k in "abcdg"}
        rstd = {k: sb("rstd_" + k, [P, TT]) for k in "abcdg"}
        xT = {k: sb("xT_" + k, [P, T]) for k in "abcd"}
        cT = sb("cT", [P, T])
        hi = sb("hi", [P, 4, H // SH, T], F16)
        stack = sb("stack", [P, 4, H // SH, T], F16)
        qm = sb("qm", [P, 2 * H, T], F16)
        vpad = sb("vpad", [P, 2, TT, H, 32])
        smax = sb("smax", [P, 2, TT, H])
        shift = sb("shift", [H, 2, T], F16)
        probs = [sb(f"probs{n}", [P, 1024]) for n in range(3)]
        o_sb = sb("o_sb", [P, 2, 2, T])
        o_rec = sb("o_rec", [P, 2 * TT, H, 1])
        o_num = sb("o_num", [P, 2 * TT, H, D])
        y = sb("y", [P, TT, C])
        yT = sb("yT", [P, T])
        xb = sb("xb", [P, TT, C])
        x1 = sb("x1", [P, TT, C])
        gt = sb("gt", [P, 12, TT, E])
        gs = sb("gs", [P, 8, TT, 1])
        gw = sb("gw", [P, TT, P])
        wT = sb("wT", [P, T])
        h = [sb(f"h{n}", [P, FC, T]) for n in range(2)]
        acc = sb("acc", [P, TT, C])
        cinb = sb("cinb", [P, TT, P])
        cTb = sb("cTb", [P, T])
        q1 = sb("q1", [P, 2, T])
        v1 = sb("v1", [P, TT, C])
        s1max = sb("s1max", [P, TT])
        s1sum = sb("s1sum", [P, TT])
        s1rec = sb("s1rec", [P, TT])
        s1scale = sb("s1scale", [P, TT])
        p1 = sb("p1", [P, TT, T])
        p1T = sb("p1T", [P, TT, T])
        x3 = sb("x3", [P, TT, C])
        x3b = sb("x3b", [P, TT, C])
        fh = sb("fh", [P, TT, F])
        z = sb("z", [P, TT, F])
        zT = sb("zT", [P, FC, T])
        xo = sb("xo", [P, TT, C])

        ps = ctx.enter_context(nc.psum_tensor("ps", [P, 8, 512], F32))
        WK = [ps[:, 0:2, :].rearrange("p a n -> p (a n)"), ps[:, 2:4, :].rearrange("p a n -> p (a n)")]
        HB = ps[:, 4:6, :].rearrange("p a n -> p (a n)")
        PO = ps[:, 6, :]
        MS = ps[:, 7, :]

        def count(name, b, k=None):
            return b * PER_BATCH[name] + (PER_BATCH[name] if k is None else k)

        def before(name, b):
            return b * PER_BATCH[name]

        MAX_UNITS = [("s0", n) for n in range(2)] + [("s1", n) for n in range(4)] + [("c", n) for n in range(8)]
        GROUPS = [[8 * r + 2 * j + s for j in range(4)] for r in range(2) for s in range(2)]
        EXP_UNITS = ([(0, 0, [(hd, j * T, 0, T) for j, hd in enumerate(g)]) for g in GROUPS]
                     + [(0, 1, [(hd, (4 * k + j) * P, P, P) for k in range(2) for j, hd in enumerate(GROUPS[2 * u + k])])
                        for u in range(2)]
                     + [(1, kb, [(hd, j * T, 0, T) for j, hd in enumerate(g)]) for kb in range(2) for g in GROUPS])

        block = ctx.enter_context(nc.Block())

        @block.sync
        def _(sp):
            sp.wait_ge(sems["raw_zero"], 1)
            for n, w in enumerate([L0_xattn_Wq, L0_xattn_Wk, L0_xattn_Wcq, L0_xattn_Wv, L1_xattn_Wq]):
                sp.dma_start(raw[:, n, :], w).then_inc(sems["w_in"], 16)
            sp.dma_start(raw[:, 5, 0:E], L0_ffn_Wg).then_inc(sems["w_in"], 16)
            sp.dma_start(w1raw[:].rearrange("p (e f) -> p e f", e=E), L0_ffn_W1.rearrange("e d f -> d e f")).then_inc(sems["w1_in"], 16)
            sp.wait_ge(sems["ctxw_zero"], 1)
            for n, (w, b) in enumerate([(L0_xattn_Wck, L0_xattn_bck), (L0_xattn_Wcv, L0_xattn_bcv),
                                        (L1_xattn_Wk, L1_xattn_bk), (L1_xattn_Wv, L1_xattn_bv)]):
                sp.dma_start(cxw[0:CC, n, :], w).then_inc(sems["ctxw_in"], 16)
                sp.dma_start(cxw[CC:CC + 1, n, :], row(b)).then_inc(sems["ctxw_in"], 16)
            sp.dma_start(wp[:], L0_xattn_Wp).then_inc(sems["bp_in"], 16)
            sp.dma_start(bp[:], row(L0_xattn_bp).broadcast_to([P, C])).then_inc(sems["bp_in"], 16)
            sp.dma_start(graw[:, 0:2], row(g_xattn).broadcast_to([P, 2])).then_inc(sems["bp_in"], 16)
            sp.dma_start(graw[:, 2:4], row(g_ffn).broadcast_to([P, 2])).then_inc(sems["bp_in"], 16)
            sp.dma_start(w2[:], L0_ffn_W2.rearrange("e (c h) d -> h e c d", h=P)).then_inc(sems["w2_in"], 16)
            sp.dma_start(b2[0:E, :], L0_ffn_b2).then_inc(sems["w2_in"], 16)
            sp.dma_start(wfc_raw[:], L1_ffn_W_fc.rearrange("(c h) d -> h c d", h=P)).then_inc(sems["wf_in"], 16)
            sp.dma_start(wpr_raw[:], L1_ffn_W_proj).then_inc(sems["wf_in"], 16)
            with nc.allow_non_contiguous_dma(reason="512 values"):
                sp.dma_start(lnw[:], L1_ffn_ln_w.rearrange("(c h) -> h c", h=P)).then_inc(sems["lnw_in"], 16)
                sp.dma_start(lnb[:], L1_ffn_ln_b.rearrange("(c h) -> h c", h=P)).then_inc(sems["lnw_in"], 16)
            sp.wait_ge(sems["cen"], 10)
            for n, b in enumerate([L0_xattn_bq, L0_xattn_bk, L0_xattn_bcq, L0_xattn_bv, L1_xattn_bq]):
                sp.dma_start(cw[P - 1:P, n, :], row(b)).then_inc(sems["bias_in"], 16)
            sp.dma_start(cw[P - 1:P, 5, 0:E], row(L0_ffn_bg)).then_inc(sems["bias_in"], 16)
            sp.dma_start(w1[P - 1:P, :, :, :].rearrange("p e c f -> p (e c f)"),
                         L0_ffn_b1.rearrange("(a e) f -> a (e f)", a=1)).then_inc(sems["bias_in"], 16)
            sp.wait_ge(sems["expand"], 13)
            sp.wait_ge(sems["consts"], 1)
            with nc.allow_non_contiguous_dma(reason="16 values"):
                for r, op in ((P - 1, 1), (CC, 3)):
                    sp.dma_start(wstack[r:r + 1, op, :, :, ONES:ONES + 1].rearrange("p o g s -> p (o g s)"),
                                 onesrow[:]).then_inc(sems["ones_in"], 16)
            sp.wait_ge(sems["zeros"], 1)
            def batch(b):
                sp.wait_ge(sems["a_xn"], before("a_xn", b))
                sp.wait_ge(sems["xb"], before("xb", b))
                sp.dma_start(xin[:], x[b].rearrange("(t p) c -> p t c", p=P)).then_inc(sems["x_in"], 16)
                sp.wait_ge(sems["a_ctx_tr"], before("a_ctx_tr", b))
                sp.dma_start(cin[:, :, 0:CC], ctx_512[b].rearrange("(t p) c -> p t c", p=P)).then_inc(sems["ctx_in"], 16)
                sp.wait_ge(sems["cb_tr"], before("cb_tr", b))
                sp.dma_start(cinb[:, :, 0:CC], ctx_512[b].rearrange("(t p) c -> p t c", p=P)).then_inc(sems["ctxb_in"], 16)
                for kind in range(2):
                    sp.wait_ge(sems["shift"], count("shift", b, kind + 1))
                    sp.dma_start(qm[ONES:ONES + 1, kind * H:(kind + 1) * H, :], shift[:, kind, :])\
                        .then_inc(sems[("shift_self_in", "shift_cross_in")[kind]], 16)
                sp.wait_ge(sems["xo"], count("xo", b))
                sp.dma_start(out[b].rearrange("(t p) c -> p t c", p=P), xo[:]).then_inc(sems["out"], 16)

            batch(0)
            with sp.Fori(1, B) as b:
                batch(b)
            sp.wait_ge(sems["out"], 16 * B)

        @block.gpsimd
        def _(pool):
            g = nc.gpsimd
            g.memset(raw[:, 5, :], 0.0)
            g.memset(b2[:], 0.0).then_inc(sems["raw_zero"], 1)
            g.memset(cxw[:], 0.0).then_inc(sems["ctxw_zero"], 1)
            linked = [0]

            def link(ins):
                linked[0] += 1
                ins.then_inc(sems["masks"], 1)
                pool.wait_ge(sems["masks"], linked[0])

            g.memset(onesrow[:], 1.0).then_inc(sems["consts"], 1)
            g.memset(ones[:], 1.0)
            g.memset(minus_half[:], -0.5)
            g.memset(eps[:], LN_EPS)
            for e in range(E):
                g.memset(rank[:, e:e + 1], float(E - e))
            link(g.memset(ident[:], 0.0))
            link(g.affine_select(out=ident[:], in_=ident[:], compare_op=ALU.not_equal, fill=1.0, base=0,
                                 pattern=[[-1, P]], channel_multiplier=1))
            link(g.tensor_copy(identb[:], ident[:]))
            link(g.affine_select(out=center[:], in_=ident[:], compare_op=ALU.not_equal, fill=-1.0, base=-(P - 1),
                                 pattern=[[0, P]], channel_multiplier=1))
            link(g.memset(center[:, P - 1:P], 0.0))
            link(g.memset(causal[:], 0.0))
            link(g.affine_select(out=causal[:], in_=causal[:], compare_op=ALU.is_ge, fill=MASKED, base=0,
                                 pattern=[[-1, P]], channel_multiplier=1))
            for t, first, rows in ((head_mask[:], 0, SLOT), (low8[:, 0, :], 2 * D, D), (low8[:, 1, :], D, D)):
                link(g.memset(t, 1.0))
                link(g.affine_select(out=t, in_=t, compare_op=ALU.is_ge, fill=0.0, base=-first,
                                     pattern=[[-SLOT, SH]], channel_multiplier=1))
                link(g.affine_select(out=t, in_=t, compare_op=ALU.is_ge, fill=0.0, base=first + rows - 1,
                                     pattern=[[SLOT, SH]], channel_multiplier=-1))
            g.memset(cin[:], 0.0)
            g.memset(cinb[:], 0.0)
            g.memset(vpad[:], 0.0)
            for k in "abc":
                g.memset(xn[k][:, :, C - 1:C], 1.0)
            link(g.memset(gw[:], 0.0))
            g.memset(cin[:, :, CC:CC + 1], 1.0)
            g.memset(cinb[:, :, CC:CC + 1], 1.0)
            for s in range(2):
                g.memset(vpad[:].rearrange("p k t (j s) c -> p (k t j) s c", s=2)[:, :, s, 16 * s + D:16 * s + D + 1], 1.0)
            link(g.memset(tneg[:], 0.0))
            g.memset(spare[:], 0.0).then_inc(sems["zeros"], 1)

            def variance(k, b):
                pool.wait_ge(sems[k + "_mv"], count(k + "_mv", b))
                g.tensor_tensor(var[k][:], mv[k][:, :, 1], eps[:], ALU.add).then_inc(sems[k + "_var"], 1)
                pool.wait_ge(sems[k + "_var"], count(k + "_var", b))
                g.tensor_tensor(rstd[k][:], var[k][:], minus_half[:], ALU.pow).then_inc(sems[k + "_rstd"], 1)

            def batch(b):
                variance("a", b)
                pool.wait_ge(sems["x_in"], count("x_in", b))
                pool.wait_ge(sems["x1"], before("x1", b))
                g.tensor_tensor(xb[:], xin[:], bp[:].rearrange("p (a c) -> p a c", a=1).broadcast_to([P, TT, C]),
                                ALU.add).then_inc(sems["xb"], 1)
                pool.wait_ge(sems["stack"], count("stack", b))
                pool.wait_ge(sems["score_ps"], before("score_ps", b))
                pool.sem_inc(sems["pool_passed"], 1)
                for n in range(H):
                    g.tensor_scalar(qm[:, H + n, :], stack[:, 2, n // SH, :], head_mask[:, n % SH:n % SH + 1], None,
                                    ALU.mult).then_inc(sems["qm_cross"], 1)
                for u in range(6):
                    pool.wait_ge(sems["probs"], count("probs", b, u + 1))
                    pool.sem_inc(sems["pool_passed"], 1)
                    p = probs[u % 3][:]
                    if u < 4:
                        p = p.rearrange("p (h q) -> p h q", q=T)[:, :, 0:P]
                    else:
                        p = p.rearrange("p (h q) -> p h q", q=P)
                    g.affine_select(out=p, in_=p, compare_op=ALU.is_ge, fill=0.0, base=0,
                                    pattern=[[0, 4 if u < 4 else 8], [1, P]], channel_multiplier=-1).then_inc(sems["probs_masked"], 1)
                variance("b", b)
                variance("c", b)
                variance("d", b)
                pool.wait_ge(sems["x3"], count("x3", b))
                g.tensor_tensor(x3b[:], x3[:], cb[:].rearrange("p (a c) -> p a c", a=1).broadcast_to([P, TT, C]),
                                ALU.add).then_inc(sems["x3b"], 1)
                variance("g", b)

            batch(0)
            with pool.Fori(1, B) as b:
                batch(b)

        @block.tensor
        def _(pe):
            mm = nc.tensor.matmul
            pe.wait_ge(sems["masks"], 7)
            pe.wait_ge(sems["w1_in"], 16)
            for e in range(E):
                mm(ps[:, e, :], center[:], w1raw[:, e * F:(e + 1) * F], start=True, stop=True).then_inc(sems["cen_ps"], 1)
            pe.wait_ge(sems["w_in"], 96)
            pe.wait_ge(sems["cen"], 2)
            r = raw[:].rearrange("p n c -> p (n c)")
            mm(ps[:, 0, :], center[:], r[:, 0:512], start=True, stop=True).then_inc(sems["cen_ps"], 1)
            mm(ps[:, 1, 0:256], center[:], r[:, 512:768], start=True, stop=True).then_inc(sems["cen_ps"], 1)
            pe.wait_ge(sems["absum"], 2)
            pe.wait_ge(sems["cen"], 3)
            mm(ps[:, 2, 0:2], ones[:], absum[:], start=True, stop=True).then_inc(sems["gamma_ps"], 1)
            pe.wait_ge(sems["tern"], 4)
            pe.wait_ge(sems["cen"], 8)
            for m in range(2):
                for c in range(FC):
                    t = nc.tensor.transpose(ps[:, 4 + m, c * P:(c + 1) * P], tern[:, m, c * P:(c + 1) * P], ident[:])
                t.then_inc(sems["ternT_ps"], 1)
            pe.wait_ge(sems["ternT"], 2)
            pe.wait_ge(sems["fold"], 4)
            pe.wait_ge(sems["gamma"], 2)
            for c in range(FC):
                t = mm(ps[:, 3, 0:P], lnbb[:, c, :], wprT0[:, c, :], start=(c == 0), stop=(c == FC - 1))
            t.then_inc(sems["cb_ps"], 1)
            pe.wait_ge(sems["bias_in"], 112)
            pe.wait_ge(sems["ones_in"], 32)
            pe.wait_ge(sems["ctxw_in"], 128)
            pe.wait_ge(sems["w2_in"], 32)
            pe.wait_ge(sems["cen"], 10)
            pe.wait_ge(sems["cb"], 1)
            pe.wait_ge(sems["zeros"], 1)
            pe.wait_ge(sems["fold"], 9)

            def transposes(dst, src, need_name, b, done):
                pe.wait_ge(sems[need_name], count(need_name, b))
                for t in range(TT):
                    ins = nc.tensor.transpose(dst[:, t * P:(t + 1) * P], src[:, t, :], ident[:])
                ins.then_inc(sems[done], 1)

            def batch(b):
                pe.wait_ge(sems["x1"], before("x1", b))
                pe.wait_ge(sems["acc"], before("acc", b))
                transposes(PO[:, 0:T], xn["a"], "a_xn", b, "a_tr")
                transposes(PO[:, T:2 * T], cin, "ctx_in", b, "a_ctx_tr")
                pe.wait_ge(sems["a_xT"], count("a_xT", b))
                pe.wait_ge(sems["a_cT"], count("a_cT", b))
                pe.wait_ge(sems["probs"], before("probs", b))
                for op in range(4):
                    if op >= 2:
                        pe.wait_ge(sems["stack"], count("stack", b, op - 1))
                    for n in range(H // SH):
                        ins = mm(WK[op % 2][:, n * T:(n + 1) * T], wstack[:, op, n, :, :].rearrange("p g s -> p (g s)"),
                                 (cT if op == 3 else xT["a"])[:], start=True, stop=True)
                    ins.then_inc(sems["stack_ps"], 1)
                for t in range(TT):
                    mm(PO[:, t * P:(t + 1) * P], xT["a"][:, t * P:(t + 1) * P], cw[:, 3, :], start=True, stop=True)
                for t in range(TT):
                    ins = mm(PO[:, T + t * P:T + (t + 1) * P], cT[:, t * P:(t + 1) * P], cxw[:, 1, :], start=True, stop=True)
                ins.then_inc(sems["v_ps"], 1)
                pe.wait_ge(sems["stack"], count("stack", b))
                for u, (kind, n) in enumerate(MAX_UNITS):
                    wk = WK[u % 2]
                    if u >= 2:
                        pe.wait_ge(sems["max_out"], count("max_out", b, u - 1))
                    if kind == "s0":
                        for half in range(2):
                            for k in range(4):
                                hd = 8 * n + 4 * half + k
                                pe.wait_ge(sems["qm_self"], count("qm_self", b, hd + 1))
                                mm(wk[:, (4 * half + k) * P:(4 * half + k + 1) * P], qm[:, hd, 0:P],
                                   stack[:, 1, hd // SH, 0:P], start=(k == 0), stop=False, skip_group_check=True)
                            ins = mm(wk[:, half * 512:(half + 1) * 512].rearrange("p (k n) -> p k n", k=4), identb[:],
                                     causal[:].rearrange("p (a n) -> p a n", a=1).broadcast_to([P, 4, P]),
                                     start=False, stop=True, skip_group_check=True)
                    elif kind == "s1":
                        for half in range(2):
                            for k in range(2):
                                hd = 4 * n + 2 * half + k
                                at = half * 512 + k * T
                                mm(wk[:, at:at + T], qm[:, hd, P:T], stack[:, 1, hd // SH, :], start=(k == 0), stop=False,
                                   skip_group_check=True)
                            ins = mm(wk[:, half * 512:(half + 1) * 512].rearrange("p (k n) -> p k n", k=2)[:, :, P:T], identb[:],
                                     causal[:].rearrange("p (a n) -> p a n", a=1).broadcast_to([P, 2, P]),
                                     start=False, stop=True, skip_group_check=True)
                    else:
                        for k in range(4):
                            hd = 4 * (n % 4) + k
                            pe.wait_ge(sems["qm_cross"], count("qm_cross", b, hd + 1))
                            t = n // 4
                            ins = mm(wk[:, k * T:(k + 1) * T], qm[:, H + hd, t * P:(t + 1) * P], stack[:, 3, hd // SH, :],
                                     start=True, stop=True)
                    ins.then_inc(sems["max_ps"], 1)
                    if u in (8, 13):
                        kind2 = 0 if u == 8 else 1
                        pe.wait_ge(sems["max_out"], count("max_out", b, 6 if u == 8 else 14))
                        pe.wait_ge(sems["v_pad"], count("v_pad", b))
                        for t in range(TT):
                            ins = nc.tensor.transpose(PO[0:H, kind2 * T + t * P:kind2 * T + (t + 1) * P],
                                                      smax[:, kind2, t, :], ident[:])
                        ins.then_inc(sems["maxT_ps"], 1)
                def scores(u):
                    kind, kb, parts = EXP_UNITS[u]
                    if u == 0:
                        pe.wait_ge(sems["shift_self_in"], count("shift_self_in", b))
                    if u == 6:
                        pe.wait_ge(sems["shift_cross_in"], count("shift_cross_in", b))
                    if u < 2:
                        pe.wait_ge(sems["max_out"], count("max_out", b))
                    else:
                        pe.wait_ge(sems["probs"], count("probs", b, u - 1))
                    for hd, at, q0, nq in parts:
                        ins = mm(WK[u % 2][:, at:at + nq], stack[:, 1 + 2 * kind, hd // SH, kb * P:(kb + 1) * P],
                                 qm[:, kind * H + hd, q0:q0 + nq], start=True, stop=True)
                    ins.then_inc(sems["score_ps"], 1)

                def values(u):
                    kind, kb, parts = EXP_UNITS[u]
                    if u < 6:
                        pe.wait_ge(sems["probs_masked"], count("probs_masked", b, u + 1))
                    else:
                        pe.wait_ge(sems["probs"], count("probs", b, u + 1))
                    if u == 0:
                        pe.wait_ge(sems["shift"], count("shift", b))
                    if u == 6:
                        pe.wait_ge(sems["o_sb"], count("o_sb", b, 1))
                    for hd, at, q0, nq in parts:
                        j, col = hd % 8 // 2, hd // 8 * T + q0
                        ins = mm(PO[32 * j:32 * j + 32, col:col + nq], vpad[:, kind, kb, hd, :],
                                 probs[u % 3][:, at:at + nq], start=(u in (0, 6)), stop=(u in (5, 13)), skip_group_check=True)
                    ins.then_inc(sems["pv"], 1)

                scores(0)
                scores(1)
                for u in range(14):
                    values(u)
                    if u + 2 < 14:
                        scores(u + 2)
                pe.wait_ge(sems["o_sb"], count("o_sb", b))
                for n in range(4 * TT):
                    kind, t, half = n // 4, n // 2 % 2, n % 2
                    ins = nc.tensor.transpose(WK[0][:, n * P:(n + 1) * P], o_sb[:, kind, half, t * P:(t + 1) * P], ident[:])
                ins.then_inc(sems["oT_ps"], 1)
                transposes(PO[:, 0:T], y, "y", b, "yT_ps")
                pe.wait_ge(sems["yT"], count("yT", b))
                for t in range(TT):
                    ins = mm(PO[:, t * P:(t + 1) * P], yT[:, t * P:(t + 1) * P], wp[:], start=True, stop=True)
                ins.then_inc(sems["wp_ps"], 1)
                pe.wait_ge(sems["xo"], before("xo", b))
                transposes(MS[:, 0:T], xn["b"], "b_xn", b, "b_tr")
                pe.wait_ge(sems["b_xT"], count("b_xT", b))
                for t in range(TT):
                    ins = mm(MS[:, t * P:(t + 1) * P], xT["b"][:, t * P:(t + 1) * P], cw[:, 5, :], start=True, stop=True)
                ins.then_inc(sems["gate_ps"], 1)

                def hidden(e):
                    if e:
                        pe.wait_ge(sems["h"], count("h", b, e))
                    else:
                        pe.wait_ge(sems["zT"], before("zT", b))
                    for c in range(FC):
                        ins = mm(HB[:, c * T:(c + 1) * T], w1[:, e, c, :], xT["b"][:], start=True, stop=True)
                    ins.then_inc(sems["h_ps"], 1)

                def expert_out(e):
                    pe.wait_ge(sems["h"], count("h", b, e + 1))
                    if e >= 2:
                        pe.wait_ge(sems["acc"], count("acc", b, 2 * (e - 1) + 1))
                    for t in range(TT):
                        for c in range(FC):
                            ins = mm([MS, PO][e % 2][:, t * P:(t + 1) * P], h[e % 2][:, c, t * P:(t + 1) * P], w2[:, e, c, :],
                                     start=(c == 0), stop=(c == FC - 1))
                    ins.then_inc(sems["y_ps"], 1)

                hidden(0)
                transposes(MS[:, 0:T], gw, "gate_w", b, "wT_ps")
                pe.wait_ge(sems["wT"], count("wT", b))
                for t in range(TT):
                    ins = mm(MS[:, t * P:(t + 1) * P], wT[:, t * P:(t + 1) * P], b2[:], start=True, stop=True)
                ins.then_inc(sems["b2_ps"], 1)
                hidden(1)
                pe.wait_ge(sems["acc"], count("acc", b, 1))
                for e in range(E):
                    expert_out(e)
                    if e + 2 < E:
                        hidden(e + 2)
                pe.wait_ge(sems["acc"], count("acc", b))
                transposes(MS[:, 0:T], xn["c"], "c_xn", b, "c_tr")
                transposes(MS[:, T:2 * T], cinb, "ctxb_in", b, "cb_tr")
                pe.wait_ge(sems["c_xT"], count("c_xT", b))
                pe.wait_ge(sems["cb_cT"], count("cb_cT", b))
                mm(MS[:, 0:T], cw[:, 4, :], xT["c"][:], start=True, stop=True)
                mm(MS[:, T:2 * T], cxw[:, 2, :], cTb[:], start=True, stop=True).then_inc(sems["q1_ps"], 1)
                pe.wait_ge(sems["q1"], count("q1", b))
                for t in range(TT):
                    ins = mm(MS[:, t * P:(t + 1) * P], cTb[:, t * P:(t + 1) * P], cxw[:, 3, :], start=True, stop=True)
                ins.then_inc(sems["v1_ps"], 1)
                pe.wait_ge(sems["h"], count("h", b))
                for t in range(TT):
                    ins = mm(HB[:, t * T:(t + 1) * T], q1[:, 0, t * P:(t + 1) * P], q1[:, 1, :], start=True, stop=True)
                ins.then_inc(sems["s1_ps"], 1)
                pe.wait_ge(sems["p1"], count("p1", b))
                pe.wait_ge(sems["v1"], count("v1", b))
                for kb in range(TT):
                    for t in range(TT):
                        ins = nc.tensor.transpose(MS[:, kb * T + t * P:kb * T + (t + 1) * P], p1[:, t, kb * P:(kb + 1) * P], ident[:])
                ins.then_inc(sems["p1T_ps"], 1)
                pe.wait_ge(sems["p1T"], count("p1T", b))
                for t in range(TT):
                    for kb in range(TT):
                        ins = mm(MS[:, t * P:(t + 1) * P], p1T[:, kb, t * P:(t + 1) * P], v1[:, kb, :], start=(kb == 0), stop=(kb == TT - 1))
                ins.then_inc(sems["o1_ps"], 1)
                pe.wait_ge(sems["x3"], count("x3", b))
                transposes(MS[:, 0:T], xn["d"], "d_xn", b, "d_tr")
                pe.wait_ge(sems["d_xT"], count("d_xT", b))
                for t in range(TT):
                    ins = mm(HB[:, t * F:(t + 1) * F], xT["d"][:, t * P:(t + 1) * P], wfcT[:], start=True, stop=True)
                ins.then_inc(sems["f_ps"], 1)
                pe.wait_ge(sems["z"], count("z", b))
                for c in range(FC):
                    for t in range(TT):
                        ins = nc.tensor.transpose(HB[:, c * T + t * P:c * T + (t + 1) * P], z[:, t, c * P:(c + 1) * P], ident[:])
                ins.then_inc(sems["zT_ps"], 1)
                pe.wait_ge(sems["zT"], count("zT", b))
                for t in range(TT):
                    for c in range(FC):
                        ins = mm(MS[:, t * P:(t + 1) * P], zT[:, c, t * P:(t + 1) * P], wprT[:, c, :], start=(c == 0), stop=(c == FC - 1))
                ins.then_inc(sems["f2_ps"], 1)

            batch(0)
            with pe.Fori(1, B) as b:
                batch(b)

        @block.scalar
        def _(act):
            sc = nc.scalar
            act.wait_ge(sems["bp_in"], 64)
            sc.activation(gates[:], graw[:], ACT.Tanh).then_inc(sems["gates"], 1)
            for e in range(0, E, 2):
                act.wait_ge(sems["cen_ps"], e + 2)
                for k in range(2):
                    sc.copy(w1[:, e + k, :, :].rearrange("p c f -> p (c f)"), ps[:, e + k, :]).then_inc(sems["cen"], 1)
            act.wait_ge(sems["cen_ps"], 10)
            c6 = cw[:].rearrange("p n c -> p (n c)")
            sc.copy(c6[:, 0:512], ps[:, 0, :]).then_inc(sems["cen"], 1)
            sc.copy(c6[:, 512:768], ps[:, 1, 0:256]).then_inc(sems["cen"], 1)
            def batch(b):
                act.wait_ge(sems["a_ctx_tr"], count("a_ctx_tr", b))
                act.wait_ge(sems["v_ps"], before("v_ps", b))
                sc.copy(xT["a"][:], PO[:, 0:T]).then_inc(sems["a_xT"], 1)
                sc.copy(cT[:], PO[:, T:2 * T]).then_inc(sems["a_cT"], 1)
                act.wait_ge(sems["stack"], before("stack", b))
                for op in range(4):
                    act.wait_ge(sems["stack_ps"], count("stack_ps", b, op + 1))
                    sc.copy(hi[:, op, :, :].rearrange("p o t -> p (o t)"), WK[op % 2]).then_inc(sems["stack_hi"], 1)
                act.wait_ge(sems["v_ps"], count("v_ps", b))
                act.wait_ge(sems["pv"], before("pv", b))
                for s in range(2):
                    dst = vpad[:].rearrange("p k t (j s) c -> p s (k t j) c", s=2)[:, s, :, 16 * s:16 * s + D]
                    sc.copy(dst, PO.rearrange("p (n s d) -> p s n d", s=2, d=D)[:, s]).then_inc(sems["v_pad"], 1)
                for u, (kind, kb, parts) in enumerate(EXP_UNITS):
                    act.wait_ge(sems["score_ps"], count("score_ps", b, u + 1))
                    if u >= 3:
                        act.wait_ge(sems["pv"], count("pv", b, u - 2))
                    sc.activation(probs[u % 3][:], WK[u % 2], ACT.Exp, scale=D ** -0.5).then_inc(sems["probs"], 1)
                    if u in (7, 13):
                        kind = int(u == 13)
                        act.wait_ge(sems["pv"], count("pv", b, 14 if kind else 6))
                        act.wait_ge(sems["oT_ps"], before("oT_ps", b))
                        sc.copy(o_sb[:, kind, :, :].rearrange("p r t -> p (r t)"), PO).then_inc(sems["o_sb"], 1)
                act.wait_ge(sems["yT_ps"], count("yT_ps", b))
                sc.copy(yT[:], PO[:, 0:T]).then_inc(sems["yT"], 1)
                act.wait_ge(sems["b_tr"], count("b_tr", b))
                sc.copy(xT["b"][:], MS[:, 0:T]).then_inc(sems["b_xT"], 1)
                act.wait_ge(sems["gate"], count("gate", b, 2))
                sc.activation(gt[:, 1, :, :], gt[:, 0, :, :], ACT.Exp).then_inc(sems["gate_e"], 1)
                act.wait_ge(sems["wT_ps"], count("wT_ps", b))
                sc.copy(wT[:], MS[:, 0:T]).then_inc(sems["wT"], 1)
                for e in range(E):
                    act.wait_ge(sems["h_ps"], count("h_ps", b, e + 1))
                    if e >= 2:
                        act.wait_ge(sems["y_ps"], count("y_ps", b, e - 1))
                    sc.activation(h[e % 2][:].rearrange("p c t -> p (c t)"), HB, ACT.Gelu_apprx_tanh).then_inc(sems["h"], 1)
                act.wait_ge(sems["cb_tr"], count("cb_tr", b))
                sc.copy(xT["c"][:], MS[:, 0:T]).then_inc(sems["c_xT"], 1)
                sc.copy(cTb[:], MS[:, T:2 * T]).then_inc(sems["cb_cT"], 1)
                act.wait_ge(sems["q1_ps"], count("q1_ps", b))
                sc.copy(q1[:].rearrange("p a t -> p (a t)"), MS).then_inc(sems["q1"], 1)
                act.wait_ge(sems["v1_ps"], count("v1_ps", b))
                sc.copy(v1[:].rearrange("p t c -> p (t c)"), MS[:, 0:T]).then_inc(sems["v1"], 1)
                act.wait_ge(sems["s1_max"], count("s1_max", b))
                for t in range(TT):
                    sc.activation(p1[:, t, :], HB[:, t * T:(t + 1) * T], ACT.Exp, bias=s1max[:, t:t + 1],
                                  accum_out=s1sum[:, t:t + 1]).then_inc(sems["p1"], 1)
                act.wait_ge(sems["p1T_ps"], count("p1T_ps", b))
                sc.copy(p1T[:].rearrange("p k t -> p (k t)"), MS).then_inc(sems["p1T"], 1)
                act.wait_ge(sems["d_tr"], count("d_tr", b))
                sc.copy(xT["d"][:], MS[:, 0:T]).then_inc(sems["d_xT"], 1)
                act.wait_ge(sems["f_ps"], count("f_ps", b))
                sc.activation(fh[:].rearrange("p t f -> p (t f)"), HB, ACT.Gelu).then_inc(sems["f"], 1)
                act.wait_ge(sems["zT_ps"], count("zT_ps", b))
                sc.copy(zT[:].rearrange("p c t -> p (c t)"), HB).then_inc(sems["zT"], 1)

            batch(0)
            with act.Fori(1, B) as b:
                batch(b)

        @block.vector
        def _(dve):
            v = nc.vector
            dve.wait_ge(sems["masks"], 16)
            v.tensor_reduce(lo_q[:], low8[:, 0, :], AX.X, ALU.add, negate=True)
            v.tensor_reduce(lo_k[:], low8[:, 1, :], AX.X, ALU.add, negate=True).then_inc(sems["gamma"], 1)
            v.memset(wstack[:], 0.0).then_inc(sems["expand"], 1)
            dve.wait_ge(sems["wf_in"], 32)
            v.tensor_reduce(absum[:, 0:1], wfc_raw[:].rearrange("p c d -> p (c d)"), AX.X, ALU.add,
                            apply_absolute_value=True).then_inc(sems["absum"], 1)
            v.tensor_reduce(absum[:, 1:2], wpr_raw[:], AX.X, ALU.add, apply_absolute_value=True).then_inc(sems["absum"], 1)
            dve.wait_ge(sems["gates"], 1)
            v.tensor_scalar(wp[:], wp[:], gates[:, 0:1], None, ALU.mult).then_inc(sems["fold"], 1)
            v.tensor_scalar(bp[:], bp[:], gates[:, 0:1], None, ALU.mult).then_inc(sems["fold"], 1)
            dve.wait_ge(sems["lnw_in"], 32)
            v.tensor_scalar(lnwg[:], lnw[:], gates[:, 3:4], None, ALU.mult).then_inc(sems["fold"], 1)
            dve.wait_ge(sems["masks"], 18)
            v.tensor_copy(lnbb[:], lnb[:].rearrange("p (c a) -> p c a", a=1).broadcast_to([P, FC, P])).then_inc(sems["fold"], 1)
            dve.wait_ge(sems["gamma_ps"], 1)
            v.tensor_scalar(thr[:, 0, :], ps[:, 2, 0:2], 0.5 / (F * C), 0.5e-6, ALU.mult, ALU.add).then_inc(sems["gamma"], 1)
            dve.wait_ge(sems["gamma"], 2)
            v.tensor_scalar(thr[:, 1, :], thr[:, 0, :], -1.0, None, ALU.mult).then_inc(sems["link"], 1)
            dve.wait_ge(sems["link"], 1)
            for m, w in enumerate((wfc_raw[:].rearrange("p c d -> p (c d)"), wpr_raw[:])):
                v.tensor_scalar(tneg[:], w, thr[:, 1, m:m + 1], None, ALU.is_lt).then_inc(sems["tern"], 1)
                dve.wait_ge(sems["tern"], 2 * m + 1)
                v.scalar_tensor_tensor(out=tern[:, m, :], in0=w, scalar=thr[:, 0, m:m + 1], in1=tneg[:], op0=ALU.is_gt,
                                       op1=ALU.subtract).then_inc(sems["tern"], 1)
                dve.wait_ge(sems["tern"], 2 * m + 2)
            dve.wait_ge(sems["ternT_ps"], 2)
            v.tensor_copy(wfcT[:], ps[:, 4, :]).then_inc(sems["ternT"], 1)
            v.tensor_copy(wprT0[:].rearrange("p c d -> p (c d)"), ps[:, 5, :]).then_inc(sems["ternT"], 1)
            dve.wait_ge(sems["ternT"], 2)
            dve.wait_ge(sems["fold"], 3)
            for c in range(FC):
                v.tensor_scalar(wprT[:, c, :], wprT0[:, c, :], lnwg[:, c:c + 1], None, ALU.mult).then_inc(sems["fold"], 1)
            dve.wait_ge(sems["expand"], 1)
            dve.wait_ge(sems["bias_in"], 112)
            dve.wait_ge(sems["ctxw_in"], 128)
            for op, w in enumerate((cw[:, 0, :], cw[:, 1, :], cw[:, 2, :], cxw[:, 0, :])):
                for r in range(3):
                    v.tensor_copy(wstack[:, op, :, :, r * D:(r + 1) * D].rearrange("p o g d -> p (o g) d"),
                                  w.rearrange("p (h d) -> p h d", d=D)).then_inc(sems["expand"], 1)
            v.memset(qm[0:1, 0, 0:1], 0.0).then_inc(sems["fold"], 1)
            dve.wait_ge(sems["cb_ps"], 1)
            v.tensor_scalar(cb[:], ps[:, 3, 0:P], gates[:, 3:4], None, ALU.mult).then_inc(sems["cb"], 1)
            dve.wait_ge(sems["zeros"], 1)

            def statistics(k, src, b):
                for t in range(TT):
                    v.bn_stats(stats[k][:, t, :], src[:, t, :]).then_inc(sems[k + "_stats"], 1)
                for t in range(TT):
                    dve.wait_ge(sems[k + "_stats"], count(k + "_stats", b, t + 1))
                    dve.sem_inc(sems["dve_passed"], 1)
                    v.bn_aggr(mv[k][:, t, :], stats[k][:, t, :]).then_inc(sems[k + "_mv"], 1)

            def normalise(k, src, dst, width, done, b):
                dve.wait_ge(sems[k + "_rstd"], count(k + "_rstd", b))
                for t in range(TT):
                    v.tensor_scalar(dst[:, t, 0:width], src[:, t, 0:width], mv[k][:, t, 0:1], rstd[k][:, t:t + 1],
                                    ALU.subtract, ALU.mult).then_inc(sems[done], 1)

            def batch(b):
                dve.wait_ge(sems["x_in"], count("x_in", b))
                statistics("a", xin, b)
                dve.wait_ge(sems["a_tr"], before("a_tr", b))
                normalise("a", xin, xn["a"], C - 1, "a_xn", b)
                dve.wait_ge(sems["score_ps"], before("score_ps", b))
                for op in range(4):
                    dve.wait_ge(sems["stack_hi"], count("stack_hi", b, op + 1))
                    v.scalar_tensor_tensor(out=stack[:, op, :, :].rearrange("p o t -> p (o t)"),
                                           in0=hi[:, op, :, :].rearrange("p o t -> p (o t)"), scalar=(lo_k if op % 2 else lo_q)[:, 0:1],
                                           in1=WK[op % 2], op0=ALU.mult, op1=ALU.add).then_inc(sems["stack"], 1)
                dve.wait_ge(sems["stack"], count("stack", b))
                for n in range(H):
                    v.tensor_scalar(qm[:, n, :], stack[:, 0, n // SH, :], head_mask[:, n % SH:n % SH + 1], None,
                                    ALU.mult).then_inc(sems["qm_self"], 1)
                dve.wait_ge(sems["maxT_ps"], before("maxT_ps", b))
                for u, (kind, n) in enumerate(MAX_UNITS):
                    dve.wait_ge(sems["max_ps"], count("max_ps", b, u + 1))
                    wk = WK[u % 2]
                    if kind == "s0":
                        o, i = smax[:, 0, 0, 8 * n:8 * n + 8], wk.rearrange("p (h k) -> p h k", k=P)
                    elif kind == "s1":
                        o, i = smax[:, 0, 1, 4 * n:4 * n + 4], wk.rearrange("p (h k) -> p h k", k=T)
                    else:
                        o, i = smax[:, 1, n // 4, 4 * (n % 4):4 * (n % 4) + 4], wk.rearrange("p (h k) -> p h k", k=T)
                    v.tensor_reduce(o, i, AX.X, ALU.max).then_inc(sems["max_out"], 1)
                    if u in (10, 13):
                        k2 = 0 if u == 10 else 1
                        dve.wait_ge(sems["maxT_ps"], count("maxT_ps", b, k2 + 1))
                        name = ("shift_self_in", "shift_cross_in")[k2]
                        dve.wait_ge(sems[name], before(name, b))
                        v.tensor_scalar(shift[:, k2, :], PO[0:H, k2 * T:(k2 + 1) * T], -1.0, -SHIFT_MAX, ALU.mult,
                                        ALU.max).then_inc(sems["shift"], 1)
                dve.wait_ge(sems["oT_ps"], count("oT_ps", b))
                o = WK[0].rearrange("p (n h r) -> p n h r", n=2 * TT, r=16)
                v.reciprocal(o_rec[:], o[:, :, :, D:D + 1]).then_inc(sems["o_rec"], 1)
                dve.wait_ge(sems["o_rec"], count("o_rec", b))
                v.tensor_tensor(o_num[:], o[:, :, :, 0:D], o_rec[:].broadcast_to([P, 2 * TT, H, D]), ALU.mult)\
                    .then_inc(sems["o_num"], 1)
                dve.wait_ge(sems["o_num"], count("o_num", b))
                dve.wait_ge(sems["yT_ps"], before("yT_ps", b))
                v.tensor_tensor(y[:], o_num[:, 0:TT].rearrange("p t h d -> p t (h d)"),
                                o_num[:, TT:2 * TT].rearrange("p t h d -> p t (h d)"), ALU.add).then_inc(sems["y"], 1)
                dve.wait_ge(sems["wp_ps"], count("wp_ps", b))
                dve.wait_ge(sems["xb"], count("xb", b))
                dve.wait_ge(sems["acc"], before("acc", b))
                v.tensor_tensor(x1[:], PO[:, 0:T].rearrange("p (t c) -> p t c", t=TT), xb[:], ALU.add).then_inc(sems["x1"], 1)
                dve.wait_ge(sems["x1"], count("x1", b))
                statistics("b", x1, b)
                dve.wait_ge(sems["b_tr"], before("b_tr", b))
                normalise("b", x1, xn["b"], C - 1, "b_xn", b)
                dve.wait_ge(sems["gate_ps"], count("gate_ps", b))
                dve.wait_ge(sems["gate_w"], before("gate_w", b))
                lg = MS[:, 0:T].rearrange("p (t e) -> p t e", t=TT)[:, :, 0:E]
                step = [0]

                def gate(ins):
                    step[0] += 1
                    ins.then_inc(sems["gate"], 1)
                    dve.wait_ge(sems["gate"], count("gate", b, step[0]))

                def wide(n):
                    return gs[:, n, :, :].broadcast_to([P, TT, E])

                rk = rank[:].rearrange("p (a e) -> p a e", a=1).broadcast_to([P, TT, E])
                gate(v.tensor_reduce(gs[:, 0, :, 0], lg, AX.X, ALU.max))
                gate(v.tensor_tensor(gt[:, 0], lg, wide(0), ALU.subtract))
                last = gt[:, 0]
                for k in range(2):
                    if k:
                        gate(v.tensor_reduce(gs[:, 1, :, 0], last, AX.X, ALU.max))
                        gate(v.tensor_tensor(gt[:, 3], last, wide(1), ALU.is_equal))
                        gate(v.tensor_tensor(gt[:, 4], gt[:, 3], rk, ALU.mult))
                    else:
                        gate(v.scalar_tensor_tensor(out=gt[:, 4], in0=last, scalar=0.0, in1=rk, op0=ALU.is_equal, op1=ALU.mult))
                    gate(v.tensor_reduce(gs[:, 2 + k, :, 0], gt[:, 4], AX.X, ALU.max))
                    gate(v.tensor_tensor(gt[:, 5 + k], rk, wide(2 + k), ALU.is_equal))
                    if k == 0:
                        gate(v.scalar_tensor_tensor(out=gt[:, 7], in0=gt[:, 5], scalar=MASKED, in1=gt[:, 0], op0=ALU.mult, op1=ALU.add))
                        last = gt[:, 7]
                gate(v.tensor_tensor(gt[:, 8], gt[:, 5], gt[:, 6], ALU.add))
                dve.wait_ge(sems["gate_e"], count("gate_e", b))
                gate(v.tensor_tensor(gt[:, 9], gt[:, 1], gt[:, 8], ALU.mult))
                gate(v.tensor_reduce(gs[:, 4, :, 0], gt[:, 9], AX.X, ALU.add))
                gate(v.tensor_reduce(gs[:, 5, :, 0], gt[:, 1], AX.X, ALU.add))
                gate(v.scalar_tensor_tensor(out=gs[:, 6], in0=gs[:, 5], scalar=1e-8, in1=gs[:, 4], op0=ALU.mult, op1=ALU.add))
                gate(v.reciprocal(gs[:, 7], gs[:, 6]))
                v.scalar_tensor_tensor(out=gw[:, :, 0:E], in0=gt[:, 9], scalar=gates[:, 2:3], in1=wide(7), op0=ALU.mult,
                                       op1=ALU.mult).then_inc(sems["gate_w"], 1)
                dve.wait_ge(sems["b2_ps"], count("b2_ps", b))
                dve.wait_ge(sems["x3"], before("x3", b))
                v.tensor_tensor(acc[:], MS[:, 0:T].rearrange("p (t c) -> p t c", t=TT), x1[:], ALU.add).then_inc(sems["acc"], 1)
                for e in range(E):
                    dve.wait_ge(sems["y_ps"], count("y_ps", b, e + 1))
                    dve.wait_ge(sems["acc"], count("acc", b, 2 * e + 1))
                    for t in range(TT):
                        v.scalar_tensor_tensor(out=acc[:, t, :], in0=[MS, PO][e % 2][:, t * P:(t + 1) * P], scalar=gw[:, t, e:e + 1], in1=acc[:, t, :],
                                               op0=ALU.mult, op1=ALU.add).then_inc(sems["acc"], 1)
                dve.wait_ge(sems["acc"], count("acc", b))
                statistics("c", acc, b)
                dve.wait_ge(sems["c_tr"], before("c_tr", b))
                normalise("c", acc, xn["c"], C - 1, "c_xn", b)
                dve.wait_ge(sems["s1_ps"], count("s1_ps", b))
                v.tensor_reduce(s1max[:], HB[:, 0:TT * T].rearrange("p (t k) -> p t k", t=TT), AX.X, ALU.max, negate=True)\
                    .then_inc(sems["s1_max"], 1)
                dve.wait_ge(sems["p1"], count("p1", b))
                v.reciprocal(s1rec[:], s1sum[:]).then_inc(sems["s1_rec"], 1)
                dve.wait_ge(sems["s1_rec"], count("s1_rec", b))
                v.tensor_scalar(s1scale[:], s1rec[:], gates[:, 1:2], None, ALU.mult).then_inc(sems["s1_scale"], 1)
                dve.wait_ge(sems["s1_scale"], count("s1_scale", b))
                dve.wait_ge(sems["o1_ps"], count("o1_ps", b))
                dve.wait_ge(sems["x3b"], before("x3b", b))
                for t in range(TT):
                    v.scalar_tensor_tensor(out=x3[:, t, :], in0=MS[:, t * P:(t + 1) * P], scalar=s1scale[:, t:t + 1],
                                           in1=acc[:, t, :], op0=ALU.mult, op1=ALU.add).then_inc(sems["x3"], 1)
                dve.wait_ge(sems["x3"], count("x3", b))
                statistics("d", x3, b)
                dve.wait_ge(sems["d_tr"], before("d_tr", b))
                normalise("d", x3, xn["d"], C, "d_xn", b)
                dve.wait_ge(sems["f"], count("f", b))
                statistics("g", fh, b)
                dve.wait_ge(sems["zT_ps"], before("zT_ps", b))
                normalise("g", fh, z, F, "z", b)
                dve.wait_ge(sems["f2_ps"], count("f2_ps", b))
                dve.wait_ge(sems["x3b"], count("x3b", b))
                dve.wait_ge(sems["out"], before("out", b))
                v.tensor_tensor(xo[:], MS[:, 0:T].rearrange("p (t c) -> p t c", t=TT), x3b[:], ALU.add).then_inc(sems["xo"], 1)

            batch(0)
            with dve.Fori(1, B) as b:
                batch(b)
_INS = ["x", "ctx_512", "g_xattn", "g_ffn", "L0_xattn_Wk", "L0_xattn_bk", "L0_xattn_Wq", "L0_xattn_bq", "L0_xattn_Wv",
        "L0_xattn_bv", "L0_xattn_Wck", "L0_xattn_bck", "L0_xattn_Wcq", "L0_xattn_bcq", "L0_xattn_Wcv", "L0_xattn_bcv",
        "L0_xattn_Wp", "L0_xattn_bp", "L0_ffn_Wg", "L0_ffn_bg", "L0_ffn_W1", "L0_ffn_b1", "L0_ffn_W2", "L0_ffn_b2",
        "L1_xattn_Wq", "L1_xattn_bq", "L1_xattn_Wk", "L1_xattn_bk", "L1_xattn_Wv", "L1_xattn_bv", "L1_ffn_W_fc",
        "L1_ffn_ln_w", "L1_ffn_ln_b", "L1_ffn_W_proj"]


def kernel(**inputs):
    import numpy as _np
    import concourse.bacc as _bacc
    from concourse import mybir as _mybir
    from concourse.bass_utils import run_bass_kernel_spmd as _run

    nc = _bacc.Bacc("TRN2", target_bir_lowering=False, num_devices=1)
    arrays, args = {}, []
    for name in _INS:
        a = _np.ascontiguousarray(inputs[name])
        arrays[f"in_{name}_dram"] = a
        args.append(nc.dram_tensor(f"in_{name}_dram", a.shape, _mybir.dt.from_np(a.dtype), kind="ExternalInput").ap())
    out = nc.dram_tensor("out_0_dram", (B, T, C), _mybir.dt.float32, kind="ExternalOutput").ap()
    flamingo(nc, *args, out)
    r = _run(nc, [arrays], core_ids=[0])
    return r.results[0]["out_0_dram"]
```

```python
from contextlib import ExitStack

import concourse.bass as bass
from concourse import mybir

F32 = mybir.dt.float32
F16 = mybir.dt.float16
BF16 = mybir.dt.bfloat16
ALU = mybir.AluOpType
ACT = mybir.ActivationFunctionType
AX = mybir.AxisListType

P = 128
B, T, C = 8, 256, 128
CC = 64
H, D = 16, 8
E, F = 8, 512
TT = T // P
FC = F // P
SH = 4
SLOT = P // SH
ONES = 3 * D
LN_EPS = 1e-5
MASKED = -1e30
SHIFT_MAX = 60000.0

PER_BATCH = dict(
    x_in=16, ctx_in=16,
    a_stats=TT, a_mv=TT, a_var=1, a_rstd=1, a_xn=TT, a_tr=1, a_ctx_tr=1, a_xT=1, a_cT=1,
    stack_ps=4, stack_hi=4, stack=4, qm_self=H, qm_cross=H, v_ps=1, v_pad=2,
    max_ps=14, max_out=14, maxT_ps=2, shift=2, shift_self_in=16, shift_cross_in=16,
    score_ps=14, probs=14, probs_masked=6, pv=14,
    o_sb=2, oT_ps=1, o_rec=1, o_num=1, y=1, yT_ps=1, yT=1, wp_ps=1, xb=1, x1=1,
    b_stats=TT, b_mv=TT, b_var=1, b_rstd=1, b_xn=TT, b_tr=1, b_xT=1,
    gate_ps=1, gate=17, gate_e=1, gate_w=1, wT_ps=1, wT=1, b2_ps=1,
    h_ps=E, h=E, y_ps=E, acc=2 * E + 1,
    ctxb_in=16,
    c_stats=TT, c_mv=TT, c_var=1, c_rstd=1, c_xn=TT, c_tr=1, c_xT=1, cb_tr=1, cb_cT=1,
    q1_ps=1, q1=1, v1_ps=1, v1=1, s1_ps=1, s1_max=1, p1=2, p1T_ps=1, p1T=1, s1_rec=1, s1_scale=1, o1_ps=1, x3=2,
    d_stats=TT, d_mv=TT, d_var=1, d_rstd=1, d_xn=TT, d_tr=1, d_xT=1,
    f_ps=1, f=1, g_stats=TT, g_mv=TT, g_var=1, g_rstd=1, z=TT, zT_ps=1, zT=1, f2_ps=1, x3b=1, xo=1, out=16,
)


def schedule():
    first = ([("stacks", 1), ("values_in",), ("stacks", 2), ("mask", 0, 0), ("mask", 0, 1), ("stacks", 3), ("mask", 0, 2),
              ("mask", 0, 3), ("mask", 1, 0), ("mask", 1, 1)]
             + [("max_unit", u) for u in range(6)] + [("turn_max", 0), ("mask", 1, 2), ("mask", 1, 3)]
             + [("max_unit", u) for u in range(6, 14)] + [("turn_max", 1)])
    experts = [("hidden", 0), ("turn_gate",), ("hidden", 1), ("expert_bias",)]
    for e in range(E):
        experts += [("expert", e)] + [("hidden", e + 2)] * (e + 2 < E)
    second = [("score", 0), ("score", 1)]
    for u in range(14):
        second += [("value", u)] + [("score", u + 2)] * (u + 2 < 14)
    second += [("turn_out",), ("turn_y",), ("project",)]
    rest = [("att_norm",), ("att_turn",), ("att_qk",), ("att_v",), ("att_score",), ("att_turn_p",), ("att_out",), ("ffn_norm",),
            ("ffn_turn",), ("ffn_hidden",), ("ffn_turn_z",), ("ffn_out",)]

    def merge(a, b):
        out, k = [], 0
        for n, step in enumerate(a):
            out.append(("A", *step))
            while k < len(b) and (k + 1) * len(a) <= (n + 1) * len(b):
                out.append(("B", *b[k]))
                k += 1
        return out + [("B", *step) for step in b[k:]]

    head = [("A", "load"), ("B", "load_ctx"), ("B", "exp_norm"), ("A", "norm"), ("B", "exp_turn"), ("A", "turn"), ("B", "gate"),
            ("A", "stacks", 0)]
    return head + merge(first, experts) + merge(second, rest)


SCHEDULE = schedule()
SETUP = ["w_in", "ctxw_in", "w1_in", "w2_in", "raw_zero", "ctxw_zero", "consts", "masks", "cen_ps", "cen", "bias_in", "expand",
         "ones_in", "gates", "fold", "bp_in", "lnw_in", "wf_in", "absum", "gamma_ps", "gamma", "tern", "ternT_ps", "ternT",
         "cb_ps", "cb", "zeros", "link",
         "pool_passed", "dve_passed"]


def flamingo(nc, x, ctx_512, g_xattn, g_ffn, L0_xattn_Wk, L0_xattn_bk, L0_xattn_Wq, L0_xattn_bq, L0_xattn_Wv, L0_xattn_bv,
             L0_xattn_Wck, L0_xattn_bck, L0_xattn_Wcq, L0_xattn_bcq, L0_xattn_Wcv, L0_xattn_bcv, L0_xattn_Wp, L0_xattn_bp,
             L0_ffn_Wg, L0_ffn_bg, L0_ffn_W1, L0_ffn_b1, L0_ffn_W2, L0_ffn_b2, L1_xattn_Wq, L1_xattn_bq, L1_xattn_Wk,
             L1_xattn_bk, L1_xattn_Wv, L1_xattn_bv, L1_ffn_W_fc, L1_ffn_ln_w, L1_ffn_ln_b, L1_ffn_W_proj, out):
    with ExitStack() as ctx:
        def sb(name, shape, dt=F32):
            return ctx.enter_context(nc.sbuf_tensor(name, shape, dt))

        def row(ap):
            return ap.rearrange("(a n) -> a n", a=1)

        sems = {name: ctx.enter_context(nc.semaphore("s_" + name)) for name in [*PER_BATCH, *SETUP]}

        ident = sb("ident", [P, P])
        identb = sb("identb", [P, P], BF16)
        causal = sb("causal", [P, P], BF16)
        center = sb("center", [P, P])
        raw = sb("raw", [P, 6, P])
        cw = sb("cw", [P, 6, P])
        cxw = sb("cxw", [P, 4, P])
        w1raw = sb("w1raw", [P, E * F])
        w1 = sb("w1", [P, E, FC, P])
        w2 = sb("w2", [P, E, FC, P])
        b2 = sb("b2", [P, P])
        wstack = sb("wstack", [P, 4, H // SH, SH, SLOT])
        lo_q = sb("lo_q", [P, 1])
        lo_k = sb("lo_k", [P, 1])
        head_mask = sb("head_mask", [P, SH])
        low8 = sb("low8", [P, 2, SH])
        wp = sb("wp", [P, P])
        bp = sb("bp", [P, P])
        graw = sb("graw", [P, 4])
        gates = sb("gates", [P, 4])
        onesrow = sb("onesrow", [1, H])
        spare = sb("spare", [P, 1])
        rank = sb("rank", [P, E])
        minus_half = sb("minus_half", [P, TT])
        eps = sb("eps", [P, TT])
        wfc_raw = sb("wfc_raw", [P, FC, P])
        wpr_raw = sb("wpr_raw", [P, F])
        absum = sb("absum", [P, 2])
        ones = sb("ones", [P, P])
        thr = sb("thr", [P, 2, 2])
        tern = sb("tern", [P, 2, F])
        tneg = sb("tneg", [P, F])
        wfcT = sb("wfcT", [P, F])
        wprT = sb("wprT", [P, FC, P])
        wprT0 = sb("wprT0", [P, FC, P])
        lnw = sb("lnw", [P, FC])
        lnwg = sb("lnwg", [P, FC])
        lnb = sb("lnb", [P, FC])
        lnbb = sb("lnbb", [P, FC, P])
        cb = sb("cb", [P, P])

        xin = sb("xin", [P, TT, C])
        cin = sb("cin", [P, TT, P])
        xn = {k: sb("xn_" + k, [P, TT, C]) for k in "abcd"}
        stats = {k: sb("stats_" + k, [P, TT, 6]) for k in "abcdg"}
        mv = {k: sb("mv_" + k, [P, TT, 2]) for k in "abcdg"}
        var = {k: sb("var_" + k, [P, TT]) for k in "abcdg"}
        rstd = {k: sb("rstd_" + k, [P, TT]) for k in "abcdg"}
        xT = {k: sb("xT_" + k, [P, T]) for k in "abcd"}
        cT = sb("cT", [P, T])
        hi = sb("hi", [P, 4, H // SH, T], F16)
        stack = sb("stack", [P, 4, H // SH, T], F16)
        qm = sb("qm", [P, 2 * H, T], F16)
        vpad = sb("vpad", [P, 2, TT, H, 32])
        smax = sb("smax", [P, 2, TT, H])
        shift = sb("shift", [H, 2, T], F16)
        probs = [sb(f"probs{n}", [P, 1024]) for n in range(3)]
        o_sb = sb("o_sb", [P, 2, 2, T])
        o_rec = sb("o_rec", [P, 2 * TT, H, 1])
        o_num = sb("o_num", [P, 2 * TT, H, D])
        y = sb("y", [P, TT, C])
        yT = sb("yT", [P, T])
        xb = sb("xb", [P, TT, C])
        x1 = sb("x1", [P, TT, C])
        gt = sb("gt", [P, 12, TT, E])
        gs = sb("gs", [P, 8, TT, 1])
        gw = sb("gw", [P, TT, P])
        wT = sb("wT", [P, T])
        h = [sb(f"h{n}", [P, FC, T]) for n in range(2)]
        acc = sb("acc", [P, TT, C])
        cinb = sb("cinb", [P, TT, P])
        cTb = sb("cTb", [P, T])
        q1 = sb("q1", [P, 2, T])
        v1 = sb("v1", [P, TT, C])
        s1max = sb("s1max", [P, TT])
        s1sum = sb("s1sum", [P, TT])
        s1rec = sb("s1rec", [P, TT])
        s1scale = sb("s1scale", [P, TT])
        p1 = sb("p1", [P, TT, T])
        p1T = sb("p1T", [P, TT, T])
        x3 = sb("x3", [P, TT, C])
        x3b = sb("x3b", [P, TT, C])
        fh = sb("fh", [P, TT, F])
        z = sb("z", [P, TT, F])
        zT = sb("zT", [P, FC, T])
        xo = sb("xo", [P, TT, C])

        ps = ctx.enter_context(nc.psum_tensor("ps", [P, 8, 512], F32))
        WK = [ps[:, 0:2, :].rearrange("p a n -> p (a n)"), ps[:, 2:4, :].rearrange("p a n -> p (a n)")]
        HB = ps[:, 4:6, :].rearrange("p a n -> p (a n)")
        PO = ps[:, 6, :]
        MS = ps[:, 7, :]

        def count(name, b, k=None):
            return b * PER_BATCH[name] + (PER_BATCH[name] if k is None else k)

        def before(name, b):
            return b * PER_BATCH[name]

        MAX_UNITS = [("s0", n) for n in range(2)] + [("s1", n) for n in range(4)] + [("c", n) for n in range(8)]
        GROUPS = [[8 * r + 2 * j + s for j in range(4)] for r in range(2) for s in range(2)]
        EXP_UNITS = ([(0, 0, [(hd, j * T, 0, T) for j, hd in enumerate(g)]) for g in GROUPS]
                     + [(0, 1, [(hd, (4 * k + j) * P, P, P) for k in range(2) for j, hd in enumerate(GROUPS[2 * u + k])])
                        for u in range(2)]
                     + [(1, kb, [(hd, j * T, 0, T) for j, hd in enumerate(g)]) for kb in range(2) for g in GROUPS])

        block = ctx.enter_context(nc.Block())

        def run(steps, loop):
            def work(ahead, behind):
                for track, name, *k in SCHEDULE:
                    b = ahead if track == "A" else behind
                    if b is not None and name in steps:
                        steps[name](b, *k)

            work(0, None)
            work(1, 0)
            with loop(1, B - 1) as b:
                work(b + 1, b)
            work(None, B - 1)

        @block.sync
        def _(sp):
            sp.wait_ge(sems["raw_zero"], 1)
            for n, w in enumerate([L0_xattn_Wq, L0_xattn_Wk, L0_xattn_Wcq, L0_xattn_Wv, L1_xattn_Wq]):
                sp.dma_start(raw[:, n, :], w).then_inc(sems["w_in"], 16)
            sp.dma_start(raw[:, 5, 0:E], L0_ffn_Wg).then_inc(sems["w_in"], 16)
            sp.dma_start(w1raw[:].rearrange("p (e f) -> p e f", e=E), L0_ffn_W1.rearrange("e d f -> d e f")).then_inc(sems["w1_in"], 16)
            sp.wait_ge(sems["ctxw_zero"], 1)
            for n, (w, b) in enumerate([(L0_xattn_Wck, L0_xattn_bck), (L0_xattn_Wcv, L0_xattn_bcv),
                                        (L1_xattn_Wk, L1_xattn_bk), (L1_xattn_Wv, L1_xattn_bv)]):
                sp.dma_start(cxw[0:CC, n, :], w).then_inc(sems["ctxw_in"], 16)
                sp.dma_start(cxw[CC:CC + 1, n, :], row(b)).then_inc(sems["ctxw_in"], 16)
            sp.dma_start(wp[:], L0_xattn_Wp).then_inc(sems["bp_in"], 16)
            sp.dma_start(bp[:], row(L0_xattn_bp).broadcast_to([P, C])).then_inc(sems["bp_in"], 16)
            sp.dma_start(graw[:, 0:2], row(g_xattn).broadcast_to([P, 2])).then_inc(sems["bp_in"], 16)
            sp.dma_start(graw[:, 2:4], row(g_ffn).broadcast_to([P, 2])).then_inc(sems["bp_in"], 16)
            sp.dma_start(w2[:], L0_ffn_W2.rearrange("e (c h) d -> h e c d", h=P)).then_inc(sems["w2_in"], 16)
            sp.dma_start(b2[0:E, :], L0_ffn_b2).then_inc(sems["w2_in"], 16)
            sp.dma_start(wfc_raw[:], L1_ffn_W_fc.rearrange("(c h) d -> h c d", h=P)).then_inc(sems["wf_in"], 16)
            sp.dma_start(wpr_raw[:], L1_ffn_W_proj).then_inc(sems["wf_in"], 16)
            with nc.allow_non_contiguous_dma(reason="512 values"):
                sp.dma_start(lnw[:], L1_ffn_ln_w.rearrange("(c h) -> h c", h=P)).then_inc(sems["lnw_in"], 16)
                sp.dma_start(lnb[:], L1_ffn_ln_b.rearrange("(c h) -> h c", h=P)).then_inc(sems["lnw_in"], 16)
            sp.wait_ge(sems["cen"], 10)
            for n, b in enumerate([L0_xattn_bq, L0_xattn_bk, L0_xattn_bcq, L0_xattn_bv, L1_xattn_bq]):
                sp.dma_start(cw[P - 1:P, n, :], row(b)).then_inc(sems["bias_in"], 16)
            sp.dma_start(cw[P - 1:P, 5, 0:E], row(L0_ffn_bg)).then_inc(sems["bias_in"], 16)
            sp.dma_start(w1[P - 1:P, :, :, :].rearrange("p e c f -> p (e c f)"),
                         L0_ffn_b1.rearrange("(a e) f -> a (e f)", a=1)).then_inc(sems["bias_in"], 16)
            sp.wait_ge(sems["expand"], 13)
            sp.wait_ge(sems["consts"], 1)
            with nc.allow_non_contiguous_dma(reason="16 values"):
                for r, op in ((P - 1, 1), (CC, 3)):
                    sp.dma_start(wstack[r:r + 1, op, :, :, ONES:ONES + 1].rearrange("p o g s -> p (o g s)"),
                                 onesrow[:]).then_inc(sems["ones_in"], 16)
            sp.wait_ge(sems["zeros"], 1)
            def load(b):
                sp.wait_ge(sems["a_xn"], before("a_xn", b))
                sp.wait_ge(sems["xb"], before("xb", b))
                sp.dma_start(xin[:], x[b].rearrange("(t p) c -> p t c", p=P)).then_inc(sems["x_in"], 16)
                sp.wait_ge(sems["a_ctx_tr"], before("a_ctx_tr", b))
                sp.dma_start(cin[:, :, 0:CC], ctx_512[b].rearrange("(t p) c -> p t c", p=P)).then_inc(sems["ctx_in"], 16)

            def load_ctx(b):
                sp.wait_ge(sems["cb_tr"], before("cb_tr", b))
                sp.dma_start(cinb[:, :, 0:CC], ctx_512[b].rearrange("(t p) c -> p t c", p=P)).then_inc(sems["ctxb_in"], 16)

            def turn_max(b, kind):
                sp.wait_ge(sems["shift"], count("shift", b, kind + 1))
                sp.dma_start(qm[ONES:ONES + 1, kind * H:(kind + 1) * H, :], shift[:, kind, :])\
                    .then_inc(sems[("shift_self_in", "shift_cross_in")[kind]], 16)

            def ffn_out(b):
                sp.wait_ge(sems["xo"], count("xo", b))
                sp.dma_start(out[b].rearrange("(t p) c -> p t c", p=P), xo[:]).then_inc(sems["out"], 16)

            run(dict(load=load, load_ctx=load_ctx, turn_max=turn_max, ffn_out=ffn_out), sp.Fori)
            sp.wait_ge(sems["out"], 16 * B)

        @block.gpsimd
        def _(pool):
            g = nc.gpsimd
            g.memset(raw[:, 5, :], 0.0)
            g.memset(b2[:], 0.0).then_inc(sems["raw_zero"], 1)
            g.memset(cxw[:], 0.0).then_inc(sems["ctxw_zero"], 1)
            linked = [0]

            def link(ins):
                linked[0] += 1
                ins.then_inc(sems["masks"], 1)
                pool.wait_ge(sems["masks"], linked[0])

            g.memset(onesrow[:], 1.0).then_inc(sems["consts"], 1)
            g.memset(ones[:], 1.0)
            g.memset(minus_half[:], -0.5)
            g.memset(eps[:], LN_EPS)
            for e in range(E):
                g.memset(rank[:, e:e + 1], float(E - e))
            link(g.memset(ident[:], 0.0))
            link(g.affine_select(out=ident[:], in_=ident[:], compare_op=ALU.not_equal, fill=1.0, base=0,
                                 pattern=[[-1, P]], channel_multiplier=1))
            link(g.tensor_copy(identb[:], ident[:]))
            link(g.affine_select(out=center[:], in_=ident[:], compare_op=ALU.not_equal, fill=-1.0, base=-(P - 1),
                                 pattern=[[0, P]], channel_multiplier=1))
            link(g.memset(center[:, P - 1:P], 0.0))
            link(g.memset(causal[:], 0.0))
            link(g.affine_select(out=causal[:], in_=causal[:], compare_op=ALU.is_ge, fill=MASKED, base=0,
                                 pattern=[[-1, P]], channel_multiplier=1))
            for t, first, rows in ((head_mask[:], 0, SLOT), (low8[:, 0, :], 2 * D, D), (low8[:, 1, :], D, D)):
                link(g.memset(t, 1.0))
                link(g.affine_select(out=t, in_=t, compare_op=ALU.is_ge, fill=0.0, base=-first,
                                     pattern=[[-SLOT, SH]], channel_multiplier=1))
                link(g.affine_select(out=t, in_=t, compare_op=ALU.is_ge, fill=0.0, base=first + rows - 1,
                                     pattern=[[SLOT, SH]], channel_multiplier=-1))
            g.memset(cin[:], 0.0)
            g.memset(cinb[:], 0.0)
            g.memset(vpad[:], 0.0)
            for k in "abc":
                g.memset(xn[k][:, :, C - 1:C], 1.0)
            link(g.memset(gw[:], 0.0))
            g.memset(cin[:, :, CC:CC + 1], 1.0)
            g.memset(cinb[:, :, CC:CC + 1], 1.0)
            for s in range(2):
                g.memset(vpad[:].rearrange("p k t (j s) c -> p (k t j) s c", s=2)[:, :, s, 16 * s + D:16 * s + D + 1], 1.0)
            link(g.memset(tneg[:], 0.0))
            g.memset(spare[:], 0.0).then_inc(sems["zeros"], 1)

            def variance(k, b):
                pool.wait_ge(sems[k + "_mv"], count(k + "_mv", b))
                g.tensor_tensor(var[k][:], mv[k][:, :, 1], eps[:], ALU.add).then_inc(sems[k + "_var"], 1)
                pool.wait_ge(sems[k + "_var"], count(k + "_var", b))
                g.tensor_tensor(rstd[k][:], var[k][:], minus_half[:], ALU.pow).then_inc(sems[k + "_rstd"], 1)

            def norm(b):
                variance("a", b)
                pool.wait_ge(sems["x_in"], count("x_in", b))
                pool.wait_ge(sems["x1"], before("x1", b))
                g.tensor_tensor(xb[:], xin[:], bp[:].rearrange("p (a c) -> p a c", a=1).broadcast_to([P, TT, C]),
                                ALU.add).then_inc(sems["xb"], 1)

            def score(b, u):
                if u >= 6:
                    return
                pool.wait_ge(sems["probs"], count("probs", b, u + 1))
                pool.sem_inc(sems["pool_passed"], 1)
                p = probs[u % 3][:]
                if u < 4:
                    p = p.rearrange("p (h q) -> p h q", q=T)[:, :, 0:P]
                else:
                    p = p.rearrange("p (h q) -> p h q", q=P)
                g.affine_select(out=p, in_=p, compare_op=ALU.is_ge, fill=0.0, base=0,
                                pattern=[[0, 4 if u < 4 else 8], [1, P]], channel_multiplier=-1).then_inc(sems["probs_masked"], 1)

            def ffn_norm(b):
                variance("d", b)
                pool.wait_ge(sems["x3"], count("x3", b))
                g.tensor_tensor(x3b[:], x3[:], cb[:].rearrange("p (a c) -> p a c", a=1).broadcast_to([P, TT, C]),
                                ALU.add).then_inc(sems["x3b"], 1)

            run(dict(norm=norm, score=score, exp_norm=lambda b: variance("b", b), att_norm=lambda b: variance("c", b),
                     ffn_norm=ffn_norm, ffn_hidden=lambda b: variance("g", b)), pool.Fori)

        @block.tensor
        def _(pe):
            mm = nc.tensor.matmul
            pe.wait_ge(sems["masks"], 7)
            pe.wait_ge(sems["w1_in"], 16)
            for e in range(E):
                mm(ps[:, e, :], center[:], w1raw[:, e * F:(e + 1) * F], start=True, stop=True).then_inc(sems["cen_ps"], 1)
            pe.wait_ge(sems["w_in"], 96)
            pe.wait_ge(sems["cen"], 2)
            r = raw[:].rearrange("p n c -> p (n c)")
            mm(ps[:, 0, :], center[:], r[:, 0:512], start=True, stop=True).then_inc(sems["cen_ps"], 1)
            mm(ps[:, 1, 0:256], center[:], r[:, 512:768], start=True, stop=True).then_inc(sems["cen_ps"], 1)
            pe.wait_ge(sems["absum"], 2)
            pe.wait_ge(sems["cen"], 3)
            mm(ps[:, 2, 0:2], ones[:], absum[:], start=True, stop=True).then_inc(sems["gamma_ps"], 1)
            pe.wait_ge(sems["tern"], 4)
            pe.wait_ge(sems["cen"], 8)
            for m in range(2):
                for c in range(FC):
                    t = nc.tensor.transpose(ps[:, 4 + m, c * P:(c + 1) * P], tern[:, m, c * P:(c + 1) * P], ident[:])
                t.then_inc(sems["ternT_ps"], 1)
            pe.wait_ge(sems["ternT"], 2)
            pe.wait_ge(sems["fold"], 4)
            pe.wait_ge(sems["gamma"], 2)
            for c in range(FC):
                t = mm(ps[:, 3, 0:P], lnbb[:, c, :], wprT0[:, c, :], start=(c == 0), stop=(c == FC - 1))
            t.then_inc(sems["cb_ps"], 1)
            pe.wait_ge(sems["bias_in"], 112)
            pe.wait_ge(sems["ones_in"], 32)
            pe.wait_ge(sems["ctxw_in"], 128)
            pe.wait_ge(sems["w2_in"], 32)
            pe.wait_ge(sems["cen"], 10)
            pe.wait_ge(sems["cb"], 1)
            pe.wait_ge(sems["zeros"], 1)
            pe.wait_ge(sems["fold"], 9)

            def transposes(dst, src, need_name, b, done):
                pe.wait_ge(sems[need_name], count(need_name, b))
                for t in range(TT):
                    ins = nc.tensor.transpose(dst[:, t * P:(t + 1) * P], src[:, t, :], ident[:])
                ins.then_inc(sems[done], 1)

            def turn(b):
                pe.wait_ge(sems["x1"], before("x1", b))
                transposes(PO[:, 0:T], xn["a"], "a_xn", b, "a_tr")
                transposes(PO[:, T:2 * T], cin, "ctx_in", b, "a_ctx_tr")

            def stacks(b, op):
                if op == 0:
                    pe.wait_ge(sems["a_xT"], count("a_xT", b))
                    pe.wait_ge(sems["o_num"], before("o_num", b))
                    pe.wait_ge(sems["probs"], before("probs", b))
                if op == 3:
                    pe.wait_ge(sems["a_cT"], count("a_cT", b))
                if op >= 2:
                    pe.wait_ge(sems["stack"], count("stack", b, op - 1))
                for n in range(H // SH):
                    ins = mm(WK[op % 2][:, n * T:(n + 1) * T], wstack[:, op, n, :, :].rearrange("p g s -> p (g s)"),
                             (cT if op == 3 else xT["a"])[:], start=True, stop=True)
                ins.then_inc(sems["stack_ps"], 1)

            def values_in(b):
                pe.wait_ge(sems["a_cT"], count("a_cT", b))
                for t in range(TT):
                    mm(PO[:, t * P:(t + 1) * P], xT["a"][:, t * P:(t + 1) * P], cw[:, 3, :], start=True, stop=True)
                for t in range(TT):
                    ins = mm(PO[:, T + t * P:T + (t + 1) * P], cT[:, t * P:(t + 1) * P], cxw[:, 1, :], start=True, stop=True)
                ins.then_inc(sems["v_ps"], 1)

            def max_unit(b, u):
                kind, n = MAX_UNITS[u]
                wk = WK[u % 2]
                if u < 2:
                    pe.wait_ge(sems["stack"], count("stack", b))
                else:
                    pe.wait_ge(sems["max_out"], count("max_out", b, u - 1))
                if kind == "s0":
                    for half in range(2):
                        for k in range(4):
                            hd = 8 * n + 4 * half + k
                            pe.wait_ge(sems["qm_self"], count("qm_self", b, hd + 1))
                            mm(wk[:, (4 * half + k) * P:(4 * half + k + 1) * P], qm[:, hd, 0:P],
                               stack[:, 1, hd // SH, 0:P], start=(k == 0), stop=False, skip_group_check=True)
                        ins = mm(wk[:, half * 512:(half + 1) * 512].rearrange("p (k n) -> p k n", k=4), identb[:],
                                 causal[:].rearrange("p (a n) -> p a n", a=1).broadcast_to([P, 4, P]),
                                 start=False, stop=True, skip_group_check=True)
                elif kind == "s1":
                    for half in range(2):
                        for k in range(2):
                            hd = 4 * n + 2 * half + k
                            at = half * 512 + k * T
                            mm(wk[:, at:at + T], qm[:, hd, P:T], stack[:, 1, hd // SH, :], start=(k == 0), stop=False,
                               skip_group_check=True)
                        ins = mm(wk[:, half * 512:(half + 1) * 512].rearrange("p (k n) -> p k n", k=2)[:, :, P:T], identb[:],
                                 causal[:].rearrange("p (a n) -> p a n", a=1).broadcast_to([P, 2, P]),
                                 start=False, stop=True, skip_group_check=True)
                else:
                    for k in range(4):
                        hd = 4 * (n % 4) + k
                        t = n // 4
                        if t == 0:
                            pe.wait_ge(sems["qm_cross"], count("qm_cross", b, hd + 1))
                        ins = mm(wk[:, k * T:(k + 1) * T], qm[:, H + hd, t * P:(t + 1) * P], stack[:, 3, hd // SH, :],
                                 start=True, stop=True)
                ins.then_inc(sems["max_ps"], 1)

            def turn_max(b, kind):
                pe.wait_ge(sems["max_out"], count("max_out", b, (6, 14)[kind]))
                pe.wait_ge(sems["v_pad"], count("v_pad", b))
                if kind:
                    pe.wait_ge(sems["shift"], count("shift", b, 1))
                for t in range(TT):
                    ins = nc.tensor.transpose(PO[0:H, kind * T + t * P:kind * T + (t + 1) * P], smax[:, kind, t, :], ident[:])
                ins.then_inc(sems["maxT_ps"], 1)

            def score(b, u):
                kind, kb, parts = EXP_UNITS[u]
                if u == 0:
                    pe.wait_ge(sems["shift_self_in"], count("shift_self_in", b))
                if u == 6:
                    pe.wait_ge(sems["shift_cross_in"], count("shift_cross_in", b))
                if u < 2:
                    pe.wait_ge(sems["max_out"], count("max_out", b))
                else:
                    pe.wait_ge(sems["probs"], count("probs", b, u - 1))
                for hd, at, q0, nq in parts:
                    ins = mm(WK[u % 2][:, at:at + nq], stack[:, 1 + 2 * kind, hd // SH, kb * P:(kb + 1) * P],
                             qm[:, kind * H + hd, q0:q0 + nq], start=True, stop=True)
                ins.then_inc(sems["score_ps"], 1)

            def value(b, u):
                kind, kb, parts = EXP_UNITS[u]
                if u < 6:
                    pe.wait_ge(sems["probs_masked"], count("probs_masked", b, u + 1))
                else:
                    pe.wait_ge(sems["probs"], count("probs", b, u + 1))
                if u == 0:
                    pe.wait_ge(sems["shift"], count("shift", b))
                if u == 6:
                    pe.wait_ge(sems["o_sb"], count("o_sb", b, 1))
                for hd, at, q0, nq in parts:
                    j, col = hd % 8 // 2, hd // 8 * T + q0
                    ins = mm(PO[32 * j:32 * j + 32, col:col + nq], vpad[:, kind, kb, hd, :],
                             probs[u % 3][:, at:at + nq], start=(u in (0, 6)), stop=(u in (5, 13)), skip_group_check=True)
                ins.then_inc(sems["pv"], 1)

            def turn_out(b):
                pe.wait_ge(sems["o_sb"], count("o_sb", b))
                for n in range(4 * TT):
                    kind, t, half = n // 4, n // 2 % 2, n % 2
                    ins = nc.tensor.transpose(WK[0][:, n * P:(n + 1) * P], o_sb[:, kind, half, t * P:(t + 1) * P], ident[:])
                ins.then_inc(sems["oT_ps"], 1)

            def turn_y(b):
                transposes(PO[:, 0:T], y, "y", b, "yT_ps")

            def project(b):
                pe.wait_ge(sems["yT"], count("yT", b))
                for t in range(TT):
                    ins = mm(PO[:, t * P:(t + 1) * P], yT[:, t * P:(t + 1) * P], wp[:], start=True, stop=True)
                ins.then_inc(sems["wp_ps"], 1)

            def exp_turn(b):
                pe.wait_ge(sems["xo"], before("xo", b))
                transposes(MS[:, 0:T], xn["b"], "b_xn", b, "b_tr")

            def gate(b):
                pe.wait_ge(sems["b_xT"], count("b_xT", b))
                for t in range(TT):
                    ins = mm(MS[:, t * P:(t + 1) * P], xT["b"][:, t * P:(t + 1) * P], cw[:, 5, :], start=True, stop=True)
                ins.then_inc(sems["gate_ps"], 1)

            def hidden(b, e):
                if e:
                    pe.wait_ge(sems["h"], count("h", b, e))
                else:
                    pe.wait_ge(sems["zT"], before("zT", b))
                for c in range(FC):
                    ins = mm(HB[:, c * T:(c + 1) * T], w1[:, e, c, :], xT["b"][:], start=True, stop=True)
                ins.then_inc(sems["h_ps"], 1)

            def turn_gate(b):
                transposes(MS[:, 0:T], gw, "gate_w", b, "wT_ps")

            def expert_bias(b):
                pe.wait_ge(sems["wT"], count("wT", b))
                for t in range(TT):
                    ins = mm(MS[:, t * P:(t + 1) * P], wT[:, t * P:(t + 1) * P], b2[:], start=True, stop=True)
                ins.then_inc(sems["b2_ps"], 1)

            def expert(b, e):
                pe.wait_ge(sems["h"], count("h", b, e + 1))
                pe.wait_ge(sems["acc"], count("acc", b, 2 * e + 1))
                for t in range(TT):
                    for c in range(FC):
                        ins = mm(MS[:, t * P:(t + 1) * P], h[e % 2][:, c, t * P:(t + 1) * P], w2[:, e, c, :],
                                 start=(c == 0), stop=(c == FC - 1))
                ins.then_inc(sems["y_ps"], 1)

            def att_turn(b):
                pe.wait_ge(sems["acc"], count("acc", b))
                transposes(MS[:, 0:T], xn["c"], "c_xn", b, "c_tr")
                transposes(MS[:, T:2 * T], cinb, "ctxb_in", b, "cb_tr")

            def att_qk(b):
                pe.wait_ge(sems["c_xT"], count("c_xT", b))
                pe.wait_ge(sems["cb_cT"], count("cb_cT", b))
                mm(MS[:, 0:T], cw[:, 4, :], xT["c"][:], start=True, stop=True)
                mm(MS[:, T:2 * T], cxw[:, 2, :], cTb[:], start=True, stop=True).then_inc(sems["q1_ps"], 1)

            def att_v(b):
                pe.wait_ge(sems["q1"], count("q1", b))
                for t in range(TT):
                    ins = mm(MS[:, t * P:(t + 1) * P], cTb[:, t * P:(t + 1) * P], cxw[:, 3, :], start=True, stop=True)
                ins.then_inc(sems["v1_ps"], 1)

            def att_score(b):
                pe.wait_ge(sems["h"], count("h", b))
                for t in range(TT):
                    ins = mm(HB[:, t * T:(t + 1) * T], q1[:, 0, t * P:(t + 1) * P], q1[:, 1, :], start=True, stop=True)
                ins.then_inc(sems["s1_ps"], 1)

            def att_turn_p(b):
                pe.wait_ge(sems["p1"], count("p1", b))
                pe.wait_ge(sems["v1"], count("v1", b))
                for kb in range(TT):
                    for t in range(TT):
                        ins = nc.tensor.transpose(MS[:, kb * T + t * P:kb * T + (t + 1) * P], p1[:, t, kb * P:(kb + 1) * P], ident[:])
                ins.then_inc(sems["p1T_ps"], 1)

            def att_out(b):
                pe.wait_ge(sems["p1T"], count("p1T", b))
                for t in range(TT):
                    for kb in range(TT):
                        ins = mm(MS[:, t * P:(t + 1) * P], p1T[:, kb, t * P:(t + 1) * P], v1[:, kb, :], start=(kb == 0), stop=(kb == TT - 1))
                ins.then_inc(sems["o1_ps"], 1)

            def ffn_turn(b):
                pe.wait_ge(sems["x3"], count("x3", b))
                transposes(MS[:, 0:T], xn["d"], "d_xn", b, "d_tr")

            def ffn_hidden(b):
                pe.wait_ge(sems["d_xT"], count("d_xT", b))
                for t in range(TT):
                    ins = mm(HB[:, t * F:(t + 1) * F], xT["d"][:, t * P:(t + 1) * P], wfcT[:], start=True, stop=True)
                ins.then_inc(sems["f_ps"], 1)

            def ffn_turn_z(b):
                pe.wait_ge(sems["z"], count("z", b))
                for c in range(FC):
                    for t in range(TT):
                        ins = nc.tensor.transpose(HB[:, c * T + t * P:c * T + (t + 1) * P], z[:, t, c * P:(c + 1) * P], ident[:])
                ins.then_inc(sems["zT_ps"], 1)

            def ffn_out(b):
                pe.wait_ge(sems["zT"], count("zT", b))
                for t in range(TT):
                    for c in range(FC):
                        ins = mm(MS[:, t * P:(t + 1) * P], zT[:, c, t * P:(t + 1) * P], wprT[:, c, :], start=(c == 0), stop=(c == FC - 1))
                ins.then_inc(sems["f2_ps"], 1)

            run(dict(turn=turn, stacks=stacks, values_in=values_in, max_unit=max_unit, turn_max=turn_max, score=score, value=value,
                     turn_out=turn_out, turn_y=turn_y, project=project, exp_turn=exp_turn, gate=gate, hidden=hidden,
                     turn_gate=turn_gate, expert_bias=expert_bias, expert=expert, att_turn=att_turn, att_qk=att_qk, att_v=att_v,
                     att_score=att_score, att_turn_p=att_turn_p, att_out=att_out, ffn_turn=ffn_turn, ffn_hidden=ffn_hidden,
                     ffn_turn_z=ffn_turn_z, ffn_out=ffn_out), pe.Fori)

        @block.scalar
        def _(act):
            sc = nc.scalar
            act.wait_ge(sems["bp_in"], 64)
            sc.activation(gates[:], graw[:], ACT.Tanh).then_inc(sems["gates"], 1)
            for e in range(0, E, 2):
                act.wait_ge(sems["cen_ps"], e + 2)
                for k in range(2):
                    sc.copy(w1[:, e + k, :, :].rearrange("p c f -> p (c f)"), ps[:, e + k, :]).then_inc(sems["cen"], 1)
            act.wait_ge(sems["cen_ps"], 10)
            c6 = cw[:].rearrange("p n c -> p (n c)")
            sc.copy(c6[:, 0:512], ps[:, 0, :]).then_inc(sems["cen"], 1)
            sc.copy(c6[:, 512:768], ps[:, 1, 0:256]).then_inc(sems["cen"], 1)
            def turn(b):
                act.wait_ge(sems["a_ctx_tr"], count("a_ctx_tr", b))
                act.wait_ge(sems["v_ps"], before("v_ps", b))
                sc.copy(xT["a"][:], PO[:, 0:T]).then_inc(sems["a_xT"], 1)
                sc.copy(cT[:], PO[:, T:2 * T]).then_inc(sems["a_cT"], 1)

            def stacks(b, op):
                if op == 0:
                    act.wait_ge(sems["stack"], before("stack", b))
                act.wait_ge(sems["stack_ps"], count("stack_ps", b, op + 1))
                sc.copy(hi[:, op, :, :].rearrange("p o t -> p (o t)"), WK[op % 2]).then_inc(sems["stack_hi"], 1)

            def values_in(b):
                act.wait_ge(sems["v_ps"], count("v_ps", b))
                act.wait_ge(sems["pv"], before("pv", b))
                for s in range(2):
                    dst = vpad[:].rearrange("p k t (j s) c -> p s (k t j) c", s=2)[:, s, :, 16 * s:16 * s + D]
                    sc.copy(dst, PO.rearrange("p (n s d) -> p s n d", s=2, d=D)[:, s]).then_inc(sems["v_pad"], 1)

            def score(b, u):
                act.wait_ge(sems["score_ps"], count("score_ps", b, u + 1))
                if u >= 3:
                    act.wait_ge(sems["pv"], count("pv", b, u - 2))
                sc.activation(probs[u % 3][:], WK[u % 2], ACT.Exp, scale=D ** -0.5).then_inc(sems["probs"], 1)

            def value(b, u):
                if u not in (5, 13):
                    return
                kind = int(u == 13)
                act.wait_ge(sems["pv"], count("pv", b, u + 1))
                act.wait_ge(sems["oT_ps"], before("oT_ps", b))
                sc.copy(o_sb[:, kind, :, :].rearrange("p r t -> p (r t)"), PO).then_inc(sems["o_sb"], 1)

            def turn_y(b):
                act.wait_ge(sems["yT_ps"], count("yT_ps", b))
                sc.copy(yT[:], PO[:, 0:T]).then_inc(sems["yT"], 1)

            def exp_turn(b):
                act.wait_ge(sems["b_tr"], count("b_tr", b))
                sc.copy(xT["b"][:], MS[:, 0:T]).then_inc(sems["b_xT"], 1)

            def gate(b):
                act.wait_ge(sems["gate"], count("gate", b, 2))
                sc.activation(gt[:, 1, :, :], gt[:, 0, :, :], ACT.Exp).then_inc(sems["gate_e"], 1)

            def turn_gate(b):
                act.wait_ge(sems["wT_ps"], count("wT_ps", b))
                sc.copy(wT[:], MS[:, 0:T]).then_inc(sems["wT"], 1)

            def hidden(b, e):
                act.wait_ge(sems["h_ps"], count("h_ps", b, e + 1))
                if e >= 2:
                    act.wait_ge(sems["y_ps"], count("y_ps", b, e - 1))
                sc.activation(h[e % 2][:].rearrange("p c t -> p (c t)"), HB, ACT.Gelu_apprx_tanh).then_inc(sems["h"], 1)

            def att_turn(b):
                act.wait_ge(sems["cb_tr"], count("cb_tr", b))
                sc.copy(xT["c"][:], MS[:, 0:T]).then_inc(sems["c_xT"], 1)
                sc.copy(cTb[:], MS[:, T:2 * T]).then_inc(sems["cb_cT"], 1)

            def att_qk(b):
                act.wait_ge(sems["q1_ps"], count("q1_ps", b))
                sc.copy(q1[:].rearrange("p a t -> p (a t)"), MS).then_inc(sems["q1"], 1)

            def att_v(b):
                act.wait_ge(sems["v1_ps"], count("v1_ps", b))
                sc.copy(v1[:].rearrange("p t c -> p (t c)"), MS[:, 0:T]).then_inc(sems["v1"], 1)

            def att_score(b):
                act.wait_ge(sems["s1_max"], count("s1_max", b))
                for t in range(TT):
                    sc.activation(p1[:, t, :], HB[:, t * T:(t + 1) * T], ACT.Exp, bias=s1max[:, t:t + 1],
                                  accum_out=s1sum[:, t:t + 1]).then_inc(sems["p1"], 1)

            def att_turn_p(b):
                act.wait_ge(sems["p1T_ps"], count("p1T_ps", b))
                sc.copy(p1T[:].rearrange("p k t -> p (k t)"), MS).then_inc(sems["p1T"], 1)

            def ffn_turn(b):
                act.wait_ge(sems["d_tr"], count("d_tr", b))
                sc.copy(xT["d"][:], MS[:, 0:T]).then_inc(sems["d_xT"], 1)

            def ffn_hidden(b):
                act.wait_ge(sems["f_ps"], count("f_ps", b))
                sc.activation(fh[:].rearrange("p t f -> p (t f)"), HB, ACT.Gelu).then_inc(sems["f"], 1)

            def ffn_turn_z(b):
                act.wait_ge(sems["zT_ps"], count("zT_ps", b))
                sc.copy(zT[:].rearrange("p c t -> p (c t)"), HB).then_inc(sems["zT"], 1)

            run(dict(turn=turn, stacks=stacks, values_in=values_in, score=score, value=value, turn_y=turn_y, exp_turn=exp_turn,
                     gate=gate, turn_gate=turn_gate, hidden=hidden, att_turn=att_turn, att_qk=att_qk, att_v=att_v,
                     att_score=att_score, att_turn_p=att_turn_p, ffn_turn=ffn_turn, ffn_hidden=ffn_hidden,
                     ffn_turn_z=ffn_turn_z), act.Fori)

        @block.vector
        def _(dve):
            v = nc.vector
            dve.wait_ge(sems["masks"], 16)
            v.tensor_reduce(lo_q[:], low8[:, 0, :], AX.X, ALU.add, negate=True)
            v.tensor_reduce(lo_k[:], low8[:, 1, :], AX.X, ALU.add, negate=True).then_inc(sems["gamma"], 1)
            v.memset(wstack[:], 0.0).then_inc(sems["expand"], 1)
            dve.wait_ge(sems["wf_in"], 32)
            v.tensor_reduce(absum[:, 0:1], wfc_raw[:].rearrange("p c d -> p (c d)"), AX.X, ALU.add,
                            apply_absolute_value=True).then_inc(sems["absum"], 1)
            v.tensor_reduce(absum[:, 1:2], wpr_raw[:], AX.X, ALU.add, apply_absolute_value=True).then_inc(sems["absum"], 1)
            dve.wait_ge(sems["gates"], 1)
            v.tensor_scalar(wp[:], wp[:], gates[:, 0:1], None, ALU.mult).then_inc(sems["fold"], 1)
            v.tensor_scalar(bp[:], bp[:], gates[:, 0:1], None, ALU.mult).then_inc(sems["fold"], 1)
            dve.wait_ge(sems["lnw_in"], 32)
            v.tensor_scalar(lnwg[:], lnw[:], gates[:, 3:4], None, ALU.mult).then_inc(sems["fold"], 1)
            dve.wait_ge(sems["masks"], 18)
            v.tensor_copy(lnbb[:], lnb[:].rearrange("p (c a) -> p c a", a=1).broadcast_to([P, FC, P])).then_inc(sems["fold"], 1)
            dve.wait_ge(sems["gamma_ps"], 1)
            v.tensor_scalar(thr[:, 0, :], ps[:, 2, 0:2], 0.5 / (F * C), 0.5e-6, ALU.mult, ALU.add).then_inc(sems["gamma"], 1)
            dve.wait_ge(sems["gamma"], 2)
            v.tensor_scalar(thr[:, 1, :], thr[:, 0, :], -1.0, None, ALU.mult).then_inc(sems["link"], 1)
            dve.wait_ge(sems["link"], 1)
            for m, w in enumerate((wfc_raw[:].rearrange("p c d -> p (c d)"), wpr_raw[:])):
                v.tensor_scalar(tneg[:], w, thr[:, 1, m:m + 1], None, ALU.is_lt).then_inc(sems["tern"], 1)
                dve.wait_ge(sems["tern"], 2 * m + 1)
                v.scalar_tensor_tensor(out=tern[:, m, :], in0=w, scalar=thr[:, 0, m:m + 1], in1=tneg[:], op0=ALU.is_gt,
                                       op1=ALU.subtract).then_inc(sems["tern"], 1)
                dve.wait_ge(sems["tern"], 2 * m + 2)
            dve.wait_ge(sems["ternT_ps"], 2)
            v.tensor_copy(wfcT[:], ps[:, 4, :]).then_inc(sems["ternT"], 1)
            v.tensor_copy(wprT0[:].rearrange("p c d -> p (c d)"), ps[:, 5, :]).then_inc(sems["ternT"], 1)
            dve.wait_ge(sems["ternT"], 2)
            dve.wait_ge(sems["fold"], 3)
            for c in range(FC):
                v.tensor_scalar(wprT[:, c, :], wprT0[:, c, :], lnwg[:, c:c + 1], None, ALU.mult).then_inc(sems["fold"], 1)
            dve.wait_ge(sems["expand"], 1)
            dve.wait_ge(sems["bias_in"], 112)
            dve.wait_ge(sems["ctxw_in"], 128)
            for op, w in enumerate((cw[:, 0, :], cw[:, 1, :], cw[:, 2, :], cxw[:, 0, :])):
                for r in range(3):
                    v.tensor_copy(wstack[:, op, :, :, r * D:(r + 1) * D].rearrange("p o g d -> p (o g) d"),
                                  w.rearrange("p (h d) -> p h d", d=D)).then_inc(sems["expand"], 1)
            v.memset(qm[0:1, 0, 0:1], 0.0).then_inc(sems["fold"], 1)
            dve.wait_ge(sems["cb_ps"], 1)
            v.tensor_scalar(cb[:], ps[:, 3, 0:P], gates[:, 3:4], None, ALU.mult).then_inc(sems["cb"], 1)
            dve.wait_ge(sems["zeros"], 1)

            def statistics(k, src, b):
                for t in range(TT):
                    v.bn_stats(stats[k][:, t, :], src[:, t, :]).then_inc(sems[k + "_stats"], 1)
                for t in range(TT):
                    dve.wait_ge(sems[k + "_stats"], count(k + "_stats", b, t + 1))
                    dve.sem_inc(sems["dve_passed"], 1)
                    v.bn_aggr(mv[k][:, t, :], stats[k][:, t, :]).then_inc(sems[k + "_mv"], 1)

            def normalise(k, src, dst, width, done, b):
                dve.wait_ge(sems[k + "_rstd"], count(k + "_rstd", b))
                for t in range(TT):
                    v.tensor_scalar(dst[:, t, 0:width], src[:, t, 0:width], mv[k][:, t, 0:1], rstd[k][:, t:t + 1],
                                    ALU.subtract, ALU.mult).then_inc(sems[done], 1)

            def norm(b):
                dve.wait_ge(sems["x_in"], count("x_in", b))
                statistics("a", xin, b)
                dve.wait_ge(sems["a_tr"], before("a_tr", b))
                normalise("a", xin, xn["a"], C - 1, "a_xn", b)

            def stacks(b, op):
                if op == 0:
                    dve.wait_ge(sems["score_ps"], before("score_ps", b))
                dve.wait_ge(sems["stack_hi"], count("stack_hi", b, op + 1))
                v.scalar_tensor_tensor(out=stack[:, op, :, :].rearrange("p o t -> p (o t)"),
                                       in0=hi[:, op, :, :].rearrange("p o t -> p (o t)"), scalar=(lo_k if op % 2 else lo_q)[:, 0:1],
                                       in1=WK[op % 2], op0=ALU.mult, op1=ALU.add).then_inc(sems["stack"], 1)

            def mask(b, kind, part):
                dve.wait_ge(sems["stack"], count("stack", b, 2 * kind + 1))
                for n in range(4 * part, 4 * part + 4):
                    v.tensor_scalar(qm[:, kind * H + n, :], stack[:, 2 * kind, n // SH, :], head_mask[:, n % SH:n % SH + 1], None,
                                    ALU.mult).then_inc(sems[("qm_self", "qm_cross")[kind]], 1)

            def max_unit(b, u):
                kind, n = MAX_UNITS[u]
                if u == 0:
                    dve.wait_ge(sems["maxT_ps"], before("maxT_ps", b))
                dve.wait_ge(sems["max_ps"], count("max_ps", b, u + 1))
                wk = WK[u % 2]
                if kind == "s0":
                    o, i = smax[:, 0, 0, 8 * n:8 * n + 8], wk.rearrange("p (h k) -> p h k", k=P)
                elif kind == "s1":
                    o, i = smax[:, 0, 1, 4 * n:4 * n + 4], wk.rearrange("p (h k) -> p h k", k=T)
                else:
                    o, i = smax[:, 1, n // 4, 4 * (n % 4):4 * (n % 4) + 4], wk.rearrange("p (h k) -> p h k", k=T)
                v.tensor_reduce(o, i, AX.X, ALU.max).then_inc(sems["max_out"], 1)

            def turn_max(b, kind):
                dve.wait_ge(sems["maxT_ps"], count("maxT_ps", b, kind + 1))
                name = ("shift_self_in", "shift_cross_in")[kind]
                dve.wait_ge(sems[name], before(name, b))
                v.tensor_scalar(shift[:, kind, :], PO[0:H, kind * T:(kind + 1) * T], -1.0, -SHIFT_MAX, ALU.mult,
                                ALU.max).then_inc(sems["shift"], 1)

            def turn_out(b):
                dve.wait_ge(sems["oT_ps"], count("oT_ps", b))
                o = WK[0].rearrange("p (n h r) -> p n h r", n=2 * TT, r=16)
                v.reciprocal(o_rec[:], o[:, :, :, D:D + 1]).then_inc(sems["o_rec"], 1)
                dve.wait_ge(sems["o_rec"], count("o_rec", b))
                v.tensor_tensor(o_num[:], o[:, :, :, 0:D], o_rec[:].broadcast_to([P, 2 * TT, H, D]), ALU.mult)\
                    .then_inc(sems["o_num"], 1)
                dve.wait_ge(sems["o_num"], count("o_num", b))
                dve.wait_ge(sems["yT_ps"], before("yT_ps", b))
                v.tensor_tensor(y[:], o_num[:, 0:TT].rearrange("p t h d -> p t (h d)"),
                                o_num[:, TT:2 * TT].rearrange("p t h d -> p t (h d)"), ALU.add).then_inc(sems["y"], 1)

            def project(b):
                dve.wait_ge(sems["wp_ps"], count("wp_ps", b))
                dve.wait_ge(sems["xb"], count("xb", b))
                v.tensor_tensor(x1[:], PO[:, 0:T].rearrange("p (t c) -> p t c", t=TT), xb[:], ALU.add).then_inc(sems["x1"], 1)

            def exp_norm(b):
                dve.wait_ge(sems["x1"], count("x1", b))
                statistics("b", x1, b)
                dve.wait_ge(sems["b_tr"], before("b_tr", b))
                normalise("b", x1, xn["b"], C - 1, "b_xn", b)

            def gate(b):
                dve.wait_ge(sems["gate_ps"], count("gate_ps", b))
                dve.wait_ge(sems["wT_ps"], before("wT_ps", b))
                lg = MS[:, 0:T].rearrange("p (t e) -> p t e", t=TT)[:, :, 0:E]
                step = [0]

                def gate(ins):
                    step[0] += 1
                    ins.then_inc(sems["gate"], 1)
                    dve.wait_ge(sems["gate"], count("gate", b, step[0]))

                def wide(n):
                    return gs[:, n, :, :].broadcast_to([P, TT, E])

                rk = rank[:].rearrange("p (a e) -> p a e", a=1).broadcast_to([P, TT, E])
                gate(v.tensor_reduce(gs[:, 0, :, 0], lg, AX.X, ALU.max))
                gate(v.tensor_tensor(gt[:, 0], lg, wide(0), ALU.subtract))
                gate(v.scalar_tensor_tensor(out=gt[:, 4], in0=gt[:, 0], scalar=0.0, in1=rk, op0=ALU.is_equal, op1=ALU.mult))
                gate(v.tensor_reduce(gs[:, 2, :, 0], gt[:, 4], AX.X, ALU.max))
                gate(v.tensor_tensor(gt[:, 5], rk, wide(2), ALU.is_equal))
                gate(v.scalar_tensor_tensor(out=gt[:, 7], in0=gt[:, 5], scalar=MASKED, in1=gt[:, 0], op0=ALU.mult, op1=ALU.add))
                gate(v.tensor_reduce(gs[:, 1, :, 0], gt[:, 7], AX.X, ALU.max))
                gate(v.tensor_tensor(gt[:, 3], gt[:, 7], wide(1), ALU.is_equal))
                gate(v.tensor_tensor(gt[:, 4], gt[:, 3], rk, ALU.mult))
                gate(v.tensor_reduce(gs[:, 3, :, 0], gt[:, 4], AX.X, ALU.max))
                gate(v.tensor_tensor(gt[:, 6], rk, wide(3), ALU.is_equal))
                gate(v.tensor_tensor(gt[:, 8], gt[:, 5], gt[:, 6], ALU.add))
                dve.wait_ge(sems["gate_e"], count("gate_e", b))
                gate(v.tensor_tensor(gt[:, 9], gt[:, 1], gt[:, 8], ALU.mult))
                gate(v.tensor_reduce(gs[:, 4, :, 0], gt[:, 9], AX.X, ALU.add))
                gate(v.tensor_reduce(gs[:, 5, :, 0], gt[:, 1], AX.X, ALU.add))
                gate(v.scalar_tensor_tensor(out=gs[:, 6], in0=gs[:, 5], scalar=1e-8, in1=gs[:, 4], op0=ALU.mult, op1=ALU.add))
                gate(v.reciprocal(gs[:, 7], gs[:, 6]))
                v.scalar_tensor_tensor(out=gw[:, :, 0:E], in0=gt[:, 9], scalar=gates[:, 2:3], in1=wide(7), op0=ALU.mult,
                                       op1=ALU.mult).then_inc(sems["gate_w"], 1)

            def expert_bias(b):
                dve.wait_ge(sems["b2_ps"], count("b2_ps", b))
                dve.wait_ge(sems["x3"], before("x3", b))
                v.tensor_tensor(acc[:], MS[:, 0:T].rearrange("p (t c) -> p t c", t=TT), x1[:], ALU.add).then_inc(sems["acc"], 1)

            def expert(b, e):
                dve.wait_ge(sems["y_ps"], count("y_ps", b, e + 1))
                dve.wait_ge(sems["acc"], count("acc", b, 2 * e + 1))
                for t in range(TT):
                    v.scalar_tensor_tensor(out=acc[:, t, :], in0=MS[:, t * P:(t + 1) * P], scalar=gw[:, t, e:e + 1], in1=acc[:, t, :],
                                           op0=ALU.mult, op1=ALU.add).then_inc(sems["acc"], 1)

            def att_norm(b):
                dve.wait_ge(sems["acc"], count("acc", b))
                statistics("c", acc, b)
                dve.wait_ge(sems["c_tr"], before("c_tr", b))
                normalise("c", acc, xn["c"], C - 1, "c_xn", b)

            def att_score(b):
                dve.wait_ge(sems["s1_ps"], count("s1_ps", b))
                v.tensor_reduce(s1max[:], HB[:, 0:TT * T].rearrange("p (t k) -> p t k", t=TT), AX.X, ALU.max, negate=True)\
                    .then_inc(sems["s1_max"], 1)

            def att_out(b):
                dve.wait_ge(sems["p1"], count("p1", b))
                v.reciprocal(s1rec[:], s1sum[:]).then_inc(sems["s1_rec"], 1)
                dve.wait_ge(sems["s1_rec"], count("s1_rec", b))
                v.tensor_scalar(s1scale[:], s1rec[:], gates[:, 1:2], None, ALU.mult).then_inc(sems["s1_scale"], 1)
                dve.wait_ge(sems["s1_scale"], count("s1_scale", b))
                dve.wait_ge(sems["o1_ps"], count("o1_ps", b))
                dve.wait_ge(sems["x3b"], before("x3b", b))
                for t in range(TT):
                    v.scalar_tensor_tensor(out=x3[:, t, :], in0=MS[:, t * P:(t + 1) * P], scalar=s1scale[:, t:t + 1],
                                           in1=acc[:, t, :], op0=ALU.mult, op1=ALU.add).then_inc(sems["x3"], 1)

            def ffn_norm(b):
                dve.wait_ge(sems["x3"], count("x3", b))
                statistics("d", x3, b)
                dve.wait_ge(sems["d_tr"], before("d_tr", b))
                normalise("d", x3, xn["d"], C, "d_xn", b)

            def ffn_hidden(b):
                dve.wait_ge(sems["f"], count("f", b))
                statistics("g", fh, b)
                dve.wait_ge(sems["zT_ps"], before("zT_ps", b))
                normalise("g", fh, z, F, "z", b)

            def ffn_out(b):
                dve.wait_ge(sems["f2_ps"], count("f2_ps", b))
                dve.wait_ge(sems["x3b"], count("x3b", b))
                dve.wait_ge(sems["out"], before("out", b))
                v.tensor_tensor(xo[:], MS[:, 0:T].rearrange("p (t c) -> p t c", t=TT), x3b[:], ALU.add).then_inc(sems["xo"], 1)

            run(dict(norm=norm, stacks=stacks, mask=mask, max_unit=max_unit, turn_max=turn_max, turn_out=turn_out, project=project,
                     exp_norm=exp_norm, gate=gate, expert_bias=expert_bias, expert=expert, att_norm=att_norm,
                     att_score=att_score, att_out=att_out, ffn_norm=ffn_norm, ffn_hidden=ffn_hidden, ffn_out=ffn_out), dve.Fori)


_INS = ["x", "ctx_512", "g_xattn", "g_ffn", "L0_xattn_Wk", "L0_xattn_bk", "L0_xattn_Wq", "L0_xattn_bq", "L0_xattn_Wv",
        "L0_xattn_bv", "L0_xattn_Wck", "L0_xattn_bck", "L0_xattn_Wcq", "L0_xattn_bcq", "L0_xattn_Wcv", "L0_xattn_bcv",
        "L0_xattn_Wp", "L0_xattn_bp", "L0_ffn_Wg", "L0_ffn_bg", "L0_ffn_W1", "L0_ffn_b1", "L0_ffn_W2", "L0_ffn_b2",
        "L1_xattn_Wq", "L1_xattn_bq", "L1_xattn_Wk", "L1_xattn_bk", "L1_xattn_Wv", "L1_xattn_bv", "L1_ffn_W_fc",
        "L1_ffn_ln_w", "L1_ffn_ln_b", "L1_ffn_W_proj"]


def kernel(**inputs):
    import numpy as _np
    import concourse.bacc as _bacc
    from concourse import mybir as _mybir
    from concourse.bass_utils import run_bass_kernel_spmd as _run

    nc = _bacc.Bacc("TRN2", target_bir_lowering=False, num_devices=1)
    arrays, args = {}, []
    for name in _INS:
        a = _np.ascontiguousarray(inputs[name])
        arrays[f"in_{name}_dram"] = a
        args.append(nc.dram_tensor(f"in_{name}_dram", a.shape, _mybir.dt.from_np(a.dtype), kind="ExternalInput").ap())
    out = nc.dram_tensor("out_0_dram", (B, T, C), _mybir.dt.float32, kind="ExternalOutput").ap()
    flamingo(nc, *args, out)
    r = _run(nc, [arrays], core_ids=[0])
    return r.results[0]["out_0_dram"]
```

```python
from contextlib import ExitStack

import concourse.bass as bass
from concourse import mybir

F32 = mybir.dt.float32
F16 = mybir.dt.float16
BF16 = mybir.dt.bfloat16
ALU = mybir.AluOpType
ACT = mybir.ActivationFunctionType
AX = mybir.AxisListType

P = 128
B, T, C = 8, 256, 128
CC = 64
H, D = 16, 8
E, F = 8, 512
TT = T // P
FC = F // P
SH = 4
HBUF = 3
SLOT = P // SH
ONES = 3 * D
LN_EPS = 1e-5
MASKED = -1e30
SHIFT_MAX = 60000.0
SCALE = 64.0

PER_BATCH = dict(
    x_in=16, ctx_in=16,
    a_stats=TT, a_mv=TT, a_var=1, a_rstd=1, a_xn=TT, a_tr=1, a_ctx_tr=1, a_xh=1, a_xl=1,
    stack_ps=4, stack_hi=4, stack=4, qm_self=H, qm_cross=H, v_ps=1, v_pad=2,
    max_ps=14, max_out=14, maxT_ps=2, shift=2, shift_self_in=16, shift_cross_in=16,
    score_ps=14, probs=14, probs_masked=6, pv=14,
    o_sb=2, oT_ps=1, o_rec=1, o_num=1, y=1, yT_ps=1, yT=1, wp_ps=1, xb=1, x1=1,
    b_stats=TT, b_mv=TT, b_var=1, b_rstd=1, b_xn=TT, b_tr=1, b_xT=1, b_xh=1, b_xl=1,
    gate_ps=1, gate=17, gate_e=1, gate_w=1, wT_ps=1, wT=1, b2_ps=1,
    h_ps=E, h=E, h_hi=E, h_lo=E, y_ps=E, acc=2 * E + 1,
    ctxb_in=16,
    c_stats=TT, c_mv=TT, c_var=1, c_rstd=1, c_xn=TT, c_tr=1, c_xT=1, cb_tr=1, cb_cT=1,
    q1_ps=1, q1=1, kv_ps=1, kv=1, s1_ps=1, s1_max=1, p1=2, p1T_ps=1, p1T=1, s1_rec=1, s1_scale=1, o1_ps=1, x3=2,
    d_stats=TT, d_mv=TT, d_var=1, d_rstd=1, d_xn=TT, d_tr=1, d_xh=1, d_xl=1,
    f_ps=1, f=1, g_stats=TT, g_mv=TT, g_var=1, g_rstd=1, z=TT, zT_ps=1, zT=1, f2_ps=1, x3b=1, xo=1, out=16,
)


def steps(text):
    return [tuple(int(w) if w.isdigit() else w for w in step.split()) for step in text.split(";")]


FIRST = steps("""
    P spread; P loads; P ones_row; A turn; P weights; P fold_gates; A split 0; A stacks 0; A split 1; A mask 0 0;
    A stacks 1; A values_in; A stacks 2; A mask 0 1; A stacks 3; A split 2; A split 3; A mask 0 2; A mask 0 3; P w1 0;
    P w1 1; A mask 1 0; A maxima 0; A maxima 1; A max_unit 0; A max_unit 1; A maxima 2; A maxima 3; P w1 2;
    A maxima 4; A maxima 5; A max_unit 2; N load; A max_unit 3; A mask 1 1; A mask 1 2; A mask 1 3; A max_unit 4;
    A max_unit 5; A maxima 6; P w1 3; A maxima 7; A maxima 8; A max_unit 6; P w1 4; A turn_max 0; A max_unit 7;
    A maxima 9; A maxima 10; A max_unit 8; P w1 5; A max_unit 9; A max_unit 10; A maxima 11; A maxima 12;
    A max_unit 11; P w1 6; A maxima 13; A max_unit 12; A max_unit 13; P w1 7; A turn_max 1; A score 0; A score 1;
    A value 0; P gamma; A score 2; A value 1; A score 3; A value 2; P ternary; A score 4; A value 3; A score 5;
    P turn_ternary; A value 4; A score 6; A value 5; N norm; A score 7; P fold_ln; P fold_b2; P w2 0; A value 6;
    A score 8; A value 7; A score 9; A value 8; A score 10; A value 9; A score 11; A value 10; P w2 1; A score 12;
    A value 11; A score 13; A value 12; P w2 2; A value 13; P w2 3; A turn_out; P w2 4; P w2 5; P w2 6; A turn_y;
    A project; P w2 7
""")
SCHEDULE = steps("""
    B load_ctx; B exp_norm; A turn; B att_ctx; B low 0; B low 1; B exp_turn; A stacks 0; B gate; A split 0; A split 1;
    A stacks 1; B hidden 0; A mask 0 0; A mask 0 1; A split 2; B turn_gate; A split 3; A values_in; A stacks 2;
    A stacks 3; B hidden 1; A mask 0 2; B expert_bias; B hidden 2; A max_unit 0; A mask 0 3; A max_unit 1; B expert 0;
    A mask 1 0; A maxima 0; A maxima 1; B add 0; A maxima 2; B low 2; A max_unit 2; A maxima 3; B add 1; B hidden 3;
    A maxima 4; A maxima 5; A mask 1 1; A max_unit 3; A mask 1 2; B expert 1; B low 3; B add 2; A mask 1 3;
    A max_unit 4; A max_unit 5; A maxima 6; B low 4; A maxima 7; N load; A maxima 8; B add 3; A maxima 9; A maxima 10;
    B low 5; B hidden 4; B expert 2; A max_unit 6; B add 4; A turn_max 0; A max_unit 7; B hidden 5; B expert 3;
    A maxima 11; A max_unit 8; B hidden 6; B low 6; A max_unit 9; A maxima 12; A max_unit 10; A maxima 13; B expert 4;
    B add 5; B low 7; A max_unit 11; A max_unit 12; B hidden 7; A max_unit 13; B expert 5; A turn_max 1; A score 0;
    B expert 6; A score 1; B add 6; B expert 7; B add 7; A value 0; B att_norm; A score 2; A value 1; A score 3;
    B att_turn; A value 2; B att_q; A score 4; A value 3; A score 5; B att_score; A value 4; A score 6; N norm;
    B att_turn_p; A value 5; A score 7; B att_out; A value 6; A score 8; A value 7; A score 9; A value 8; A score 10;
    A value 9; B ffn_norm; B ffn_turn; A score 11; B ffn_hidden; A value 10; A score 12; A value 11; A score 13;
    A value 12; A value 13; B ffn_turn_z; A turn_out; B ffn_out; A turn_y; A project
""")
SETUP = ["w_in", "b_in", "ctxw_in", "l1w_in", "b_track_w_in", "w1_in", "w2_in", "raw_zero", "brow_zero", "ctxw_zero", "consts", "masks", "sel", "cin_ready", "b_track_ready",
         "v_ready", "cen_ps", "w_hi", "w_lo", "cw", "expand", "ones_set", "gates", "fold", "bp_in", "lnw_in", "wf_in", "absum",
         "gamma_ps", "gamma", "tern", "ternT_ps", "ternT", "wprT", "cb_ps", "cb", "w1_ps", "w1_hi", "w1_lo", "w2_hi", "w2_lo",
         "pool_passed", "dve_passed"]


def flamingo(nc, x, ctx_512, g_xattn, g_ffn, L0_xattn_Wk, L0_xattn_bk, L0_xattn_Wq, L0_xattn_bq, L0_xattn_Wv, L0_xattn_bv,
             L0_xattn_Wck, L0_xattn_bck, L0_xattn_Wcq, L0_xattn_bcq, L0_xattn_Wcv, L0_xattn_bcv, L0_xattn_Wp, L0_xattn_bp,
             L0_ffn_Wg, L0_ffn_bg, L0_ffn_W1, L0_ffn_b1, L0_ffn_W2, L0_ffn_b2, L1_xattn_Wq, L1_xattn_bq, L1_xattn_Wk,
             L1_xattn_bk, L1_xattn_Wv, L1_xattn_bv, L1_ffn_W_fc, L1_ffn_ln_w, L1_ffn_ln_b, L1_ffn_W_proj, out):
    with ExitStack() as ctx:
        def sb(name, shape, dt=F32):
            return ctx.enter_context(nc.sbuf_tensor(name, shape, dt))

        def row(ap):
            return ap.rearrange("(a n) -> a n", a=1)

        sems = {name: ctx.enter_context(nc.semaphore("s_" + name)) for name in [*PER_BATCH, *SETUP]}

        ident = sb("ident", [P, P])
        identb = sb("identb", [P, P], BF16)
        causal = sb("causal", [P, P], BF16)
        center = sb("center", [P, P])
        raw = sb("raw", [P, 6, P])
        brow = sb("brow", [P, P])
        brow_b = sb("brow_b", [E, P])
        b1row = sb("b1row", [P, F])
        sel = sb("sel", [E, E, P])
        cw = sb("cw", [P, 2, P])
        cxw = sb("cxw", [P, 4, P])
        w_hi = sb("w_hi", [P, 6, P], F16)
        w_lo = sb("w_lo", [P, 6, P], F16)
        staging = sb("staging", [P, E * F])
        w1_hi = sb("w1_hi", [P, E, FC, P], F16)
        w1_lo = sb("w1_lo", [P, E, FC, P], F16)
        w2_hi = sb("w2_hi", [P, E, FC, P], F16)
        w2_lo = sb("w2_lo", [P, E, FC, P], F16)
        b2 = sb("b2", [P, P])
        wstack_hi = sb("wstack_hi", [P, 4, H // SH, SH, SLOT], F16)
        wstack_lo = sb("wstack_lo", [P, 4, H // SH, SH, SLOT], F16)
        lo_q = sb("lo_q", [P, 1])
        lo_k = sb("lo_k", [P, 1])
        head_mask = sb("head_mask", [P, SH])
        low8 = sb("low8", [P, 2, SH])
        wp = sb("wp", [P, P])
        bp = sb("bp", [P, P])
        graw = sb("graw", [P, 4])
        gates = sb("gates", [P, 4])
        gate_scale = sb("gate_scale", [P, 1])
        rank = sb("rank", [P, E])
        minus_half = sb("minus_half", [P, TT])
        eps = sb("eps", [P, TT])
        absum = sb("absum", [P, 2])
        ones = sb("ones", [P, P])
        thr = sb("thr", [P, 2, 2])
        wfcT = sb("wfcT", [P, F], F16)
        wprT = sb("wprT", [P, FC, P])
        lnw = sb("lnw", [P, FC])
        lnwg = sb("lnwg", [P, FC])
        lnb = sb("lnb", [P, FC])
        cb = sb("cb", [P, P])

        xin = sb("xin", [P, TT, C])
        cin = sb("cin", [P, TT, P])
        xn = {k: sb("xn_" + k, [P, TT, C]) for k in "abcd"}
        stats = {k: sb("stats_" + k, [P, TT, 6]) for k in "abcdg"}
        mv = {k: sb("mv_" + k, [P, TT, 2]) for k in "abcdg"}
        var = {k: sb("var_" + k, [P, TT]) for k in "abcdg"}
        rstd = {k: sb("rstd_" + k, [P, TT]) for k in "abcdg"}
        xT = {k: sb("xT_" + k, [P, T]) for k in "bc"}
        xh = {k: sb("xh_" + k, [P, 2 * T if k == "a" else T], F16) for k in "abd"}
        xl = {k: sb("xl_" + k, [P, 2 * T if k == "a" else T], F16) for k in "abd"}
        hi = sb("hi", [P, 4, H // SH, T], F16)
        stack = sb("stack", [P, 4, H // SH, T], F16)
        qm = sb("qm", [P, 2 * H, T], F16)
        vpad = sb("vpad", [P, 2, TT, H, 32])
        smax = sb("smax", [P, 2, TT, H])
        shift = sb("shift", [H, 2, T], F16)
        probs = [sb(f"probs{n}", [P, 1024]) for n in range(3)]
        o_sb = sb("o_sb", [P, 2, 2, T])
        o_rec = sb("o_rec", [P, 2 * TT, H, 1])
        o_num = sb("o_num", [P, 2 * TT, H, D])
        y = sb("y", [P, TT, C])
        yT = sb("yT", [P, T])
        xb = sb("xb", [P, TT, C])
        x1 = sb("x1", [P, TT, C])
        gt = sb("gt", [P, 12, TT, E])
        gs = sb("gs", [P, 8, TT, 1])
        gw = sb("gw", [P, TT, P])
        wT = sb("wT", [P, T])
        h = [sb(f"h{n}", [P, FC, T]) for n in range(HBUF)]
        h_hi = [sb(f"h_hi{n}", [P, FC, T], F16) for n in range(HBUF)]
        h_lo = [sb(f"h_lo{n}", [P, FC, T], F16) for n in range(HBUF)]
        acc = sb("acc", [P, TT, C])
        cinb = sb("cinb", [P, TT, P])
        cTb = sb("cTb", [P, T])
        q1 = sb("q1", [P, T])
        kv1 = sb("kv1", [P, 2 * T])
        s1max = sb("s1max", [P, TT])
        s1sum = sb("s1sum", [P, TT])
        s1rec = sb("s1rec", [P, TT])
        s1scale = sb("s1scale", [P, TT])
        p1 = sb("p1", [P, TT, T])
        p1T = sb("p1T", [P, TT, T])
        x3 = sb("x3", [P, TT, C])
        x3b = sb("x3b", [P, TT, C])
        fh = sb("fh", [P, TT, F])
        z = sb("z", [P, TT, F])
        zT = sb("zT", [P, FC, T])
        xo = sb("xo", [P, TT, C])
        wfc_raw = fh[:, 0, :].rearrange("p (c d) -> p c d", d=P)
        wpr_raw = fh[:, 1, :]
        tern = z
        tneg = zT[:, 0:2, :].rearrange("p c t -> p (c t)")
        lnbb = zT[:, 2:4, :].rearrange("p c t -> p (c t)").rearrange("p (c d) -> p c d", d=P)
        wprT0 = p1[:].rearrange("p a t -> p (a t)").rearrange("p (c d) -> p c d", d=P)

        ps = ctx.enter_context(nc.psum_tensor("ps", [P, 8, 512], F32))
        WK = [ps[:, 0:2, :].rearrange("p a n -> p (a n)"), ps[:, 2:4, :].rearrange("p a n -> p (a n)")]
        HB = ps[:, 4:6, :].rearrange("p a n -> p (a n)")
        PO = ps[:, 6, :]
        MS = ps[:, 7, :]

        def count(name, b, k=None):
            return b * PER_BATCH[name] + (PER_BATCH[name] if k is None else k)

        def before(name, b):
            return b * PER_BATCH[name]

        MAX_UNITS = [("s0", n) for n in range(2)] + [("s1", n) for n in range(4)] + [("c", n) for n in range(8)]
        GROUPS = [[8 * r + 2 * j + s for j in range(4)] for r in range(2) for s in range(2)]
        EXP_UNITS = ([(0, 0, [(hd, j * T, 0, T) for j, hd in enumerate(g)]) for g in GROUPS]
                     + [(0, 1, [(hd, (4 * k + j) * P, P, P) for k in range(2) for j, hd in enumerate(GROUPS[2 * u + k])])
                        for u in range(2)]
                     + [(1, kb, [(hd, j * T, 0, T) for j, hd in enumerate(g)]) for kb in range(2) for g in GROUPS])

        block = ctx.enter_context(nc.Block())

        def run(steps, loop):
            def work(schedule, n, a, b, p=None):
                for name, step, *k in schedule:
                    batch = dict(N=n, A=a, B=b, P=p)[name]
                    if batch is not None and step in steps:
                        steps[step](batch, *k)

            work(FIRST, 0, None, None)
            work(FIRST, 1, 0, None, 0)
            work(SCHEDULE, 2, 1, 0)
            with loop(1, B - 2) as b:
                work(SCHEDULE, b + 2, b + 1, b)
            work(SCHEDULE, None, B - 1, B - 2)
            work(SCHEDULE, None, None, B - 1)

        @block.sync
        def _(sp):
            def load(b):
                sp.wait_ge(sems["a_xn"], before("a_xn", b))
                sp.wait_ge(sems["xb"], before("xb", b))
                sp.dma_start(xin[:], x[b].rearrange("(t p) c -> p t c", p=P)).then_inc(sems["x_in"], 16)
                sp.wait_ge(sems["a_ctx_tr"], before("a_ctx_tr", b))
                sp.wait_ge(sems["cin_ready"], 1)
                sp.dma_start(cin[:, :, 0:CC], ctx_512[b].rearrange("(t p) c -> p t c", p=P)).then_inc(sems["ctx_in"], 16)

            for n, w in enumerate([L0_xattn_Wq, L0_xattn_Wk, L0_xattn_Wcq, L0_xattn_Wv]):
                sp.dma_start(raw[:, n, :], w).then_inc(sems["w_in"], 16)
            sp.wait_ge(sems["brow_zero"], 1)
            for n, b in enumerate([L0_xattn_bq, L0_xattn_bk, L0_xattn_bcq, L0_xattn_bv]):
                sp.dma_start(brow[n:n + 1, :], row(b)).then_inc(sems["b_in"], 16)

            def loads(_):
                sp.wait_ge(sems["raw_zero"], 1)
                sp.dma_start(raw[:, 4, :], L1_xattn_Wq).then_inc(sems["b_track_w_in"], 16)
                sp.dma_start(raw[:, 5, 0:E], L0_ffn_Wg).then_inc(sems["b_track_w_in"], 16)
                sp.dma_start(brow_b[4:5, :], row(L1_xattn_bq)).then_inc(sems["b_track_w_in"], 16)
                sp.dma_start(brow_b[5:6, 0:E], row(L0_ffn_bg)).then_inc(sems["b_track_w_in"], 16)
                sp.dma_start(graw[:, 0:2], row(g_xattn).broadcast_to([P, 2])).then_inc(sems["bp_in"], 16)
                sp.dma_start(graw[:, 2:4], row(g_ffn).broadcast_to([P, 2])).then_inc(sems["bp_in"], 16)
                sp.dma_start(bp[:], row(L0_xattn_bp).broadcast_to([P, C])).then_inc(sems["bp_in"], 16)
                sp.dma_start(wp[:], L0_xattn_Wp).then_inc(sems["bp_in"], 16)
                sp.dma_start(b1row[0:E, :], L0_ffn_b1).then_inc(sems["w1_in"], 16)
                sp.dma_start(staging[:].rearrange("p (e f) -> p e f", e=E), L0_ffn_W1.rearrange("e d f -> d e f"))\
                    .then_inc(sems["w1_in"], 16)
                sp.dma_start(wfc_raw, L1_ffn_W_fc.rearrange("(c h) d -> h c d", h=P)).then_inc(sems["wf_in"], 16)
                sp.dma_start(wpr_raw, L1_ffn_W_proj).then_inc(sems["wf_in"], 16)
                sp.dma_start(b2[0:E, :], L0_ffn_b2).then_inc(sems["wf_in"], 16)
                for n, (w, b) in ((2, (L1_xattn_Wk, L1_xattn_bk)), (3, (L1_xattn_Wv, L1_xattn_bv))):
                    sp.dma_start(cxw[0:CC, n, :], w).then_inc(sems["l1w_in"], 16)
                    sp.dma_start(cxw[CC:CC + 1, n, :], row(b)).then_inc(sems["l1w_in"], 16)
                with nc.allow_non_contiguous_dma(reason="512 values"):
                    sp.dma_start(lnw[:], L1_ffn_ln_w.rearrange("(c h) -> h c", h=P)).then_inc(sems["lnw_in"], 16)
                    sp.dma_start(lnb[:], L1_ffn_ln_b.rearrange("(c h) -> h c", h=P)).then_inc(sems["lnw_in"], 16)

            def gamma(_):
                sp.wait_ge(sems["w1_ps"], E)
                sp.dma_start(staging[:].rearrange("p (e c d) -> p e c d", e=E, c=FC),
                             L0_ffn_W2.rearrange("e (c h) d -> h e c d", h=P)).then_inc(sems["w2_in"], 16)

            def load_ctx(b):
                sp.wait_ge(sems["b_track_ready"], 1)
                sp.wait_ge(sems["cb_tr"], before("cb_tr", b))
                sp.dma_start(cinb[:, :, 0:CC], ctx_512[b].rearrange("(t p) c -> p t c", p=P)).then_inc(sems["ctxb_in"], 16)

            def turn_max(b, kind):
                sp.wait_ge(sems["shift"], count("shift", b, kind + 1))
                sp.dma_start(qm[ONES:ONES + 1, kind * H:(kind + 1) * H, :], shift[:, kind, :])\
                    .then_inc(sems[("shift_self_in", "shift_cross_in")[kind]], 16)

            def ffn_out(b):
                sp.wait_ge(sems["xo"], count("xo", b))
                sp.dma_start(out[b].rearrange("(t p) c -> p t c", p=P), xo[:]).then_inc(sems["out"], 16)

            run(dict(load=load, load_ctx=load_ctx, turn_max=turn_max, ffn_out=ffn_out, loads=loads, gamma=gamma), sp.Fori)
            sp.wait_ge(sems["out"], 16 * B)

        @block.gpsimd
        def _(pool):
            g = nc.gpsimd
            g.memset(cxw[:], 0.0).then_inc(sems["ctxw_zero"], 1)
            g.memset(brow[:], 0.0).then_inc(sems["brow_zero"], 1)
            linked = [0]

            def link(ins):
                linked[0] += 1
                ins.then_inc(sems["masks"], 1)
                pool.wait_ge(sems["masks"], linked[0])

            g.memset(cin[:], 0.0)
            g.memset(minus_half[:], -0.5)
            g.memset(xn["a"][:, :, C - 1:C], 1.0)
            g.memset(eps[:], LN_EPS)
            link(g.memset(ident[:], 0.0))
            g.memset(cin[:, :, CC:CC + 1], 1.0).then_inc(sems["cin_ready"], 1)
            link(g.affine_select(out=ident[:], in_=ident[:], compare_op=ALU.not_equal, fill=1.0, base=0,
                                 pattern=[[-1, P]], channel_multiplier=1))
            link(g.affine_select(out=center[:], in_=ident[:], compare_op=ALU.not_equal, fill=-1.0, base=-(P - 1),
                                 pattern=[[0, P]], channel_multiplier=1))
            link(g.memset(center[:, P - 1:P], 0.0))
            link(g.memset(sel[:], 0.0))
            g.affine_select(out=sel[:, :, P - 1:P], in_=sel[:, :, P - 1:P], compare_op=ALU.not_equal, fill=1.0, base=0,
                            pattern=[[-1, E]], channel_multiplier=1).then_inc(sems["sel"], 1)
            for t, first, rows in ((low8[:, 0, :], 2 * D, D), (low8[:, 1, :], D, D), (head_mask[:], 0, SLOT)):
                link(g.memset(t, 1.0))
                link(g.affine_select(out=t, in_=t, compare_op=ALU.is_ge, fill=0.0, base=-first,
                                     pattern=[[-SLOT, SH]], channel_multiplier=1))
                link(g.affine_select(out=t, in_=t, compare_op=ALU.is_ge, fill=0.0, base=first + rows - 1,
                                     pattern=[[SLOT, SH]], channel_multiplier=-1))
            link(g.tensor_copy(identb[:], ident[:]))
            link(g.memset(causal[:], 0.0))
            link(g.affine_select(out=causal[:], in_=causal[:], compare_op=ALU.is_ge, fill=MASKED, base=0,
                                 pattern=[[-1, P]], channel_multiplier=1))
            link(g.memset(vpad[:], 0.0))
            for s in range(2):
                g.memset(vpad[:].rearrange("p k t (j s) c -> p (k t j) s c", s=2)[:, :, s, 16 * s + D:16 * s + D + 1], 1.0)\
                    .then_inc(sems["v_ready"], 1)
            g.memset(raw[:, 5, :], 0.0)
            g.memset(brow_b[:], 0.0)
            g.memset(b2[:], 0.0).then_inc(sems["raw_zero"], 1)

            def first_constants(_):
                g.memset(ones[:], 1.0).then_inc(sems["consts"], 1)
                for e in range(E):
                    g.memset(rank[:, e:e + 1], float(E - e))
                for k in "bc":
                    g.memset(xn[k][:, :, C - 1:C], 1.0)
                link(g.memset(cinb[:], 0.0))
                g.memset(cinb[:, :, CC:CC + 1], 1.0)
                g.memset(gw[:], 0.0).then_inc(sems["b_track_ready"], 1)

            def variance(k, b):
                pool.wait_ge(sems[k + "_mv"], count(k + "_mv", b))
                g.tensor_tensor(var[k][:], mv[k][:, :, 1], eps[:], ALU.add).then_inc(sems[k + "_var"], 1)
                pool.wait_ge(sems[k + "_var"], count(k + "_var", b))
                g.tensor_tensor(rstd[k][:], var[k][:], minus_half[:], ALU.pow).then_inc(sems[k + "_rstd"], 1)

            def ones_row(_):
                pool.wait_ge(sems["expand"], 26)
                for op_k, p in ((1, P - 1), (3, CC)):
                    o = wstack_hi[:, op_k, :, :, ONES]
                    g.affine_select(out=o, in_=o, compare_op=ALU.not_equal, fill=SCALE, base=-p,
                                    pattern=[[0, H // SH], [0, SH]], channel_multiplier=1).then_inc(sems["ones_set"], 1)

            def turn(b):
                pool.wait_ge(sems["x_in"], count("x_in", b))
                pool.wait_ge(sems["fold"], 2)
                pool.wait_ge(sems["x1"], before("x1", b))
                g.tensor_tensor(xb[:], xin[:], bp[:].rearrange("p (a c) -> p a c", a=1).broadcast_to([P, TT, C]),
                                ALU.add).then_inc(sems["xb"], 1)

            def score(b, u):
                if u >= 6:
                    return
                pool.wait_ge(sems["probs"], count("probs", b, u + 1))
                pool.sem_inc(sems["pool_passed"], 1)
                p = probs[u % 3][:]
                if u < 4:
                    p = p.rearrange("p (h q) -> p h q", q=T)[:, :, 0:P]
                else:
                    p = p.rearrange("p (h q) -> p h q", q=P)
                g.affine_select(out=p, in_=p, compare_op=ALU.is_ge, fill=0.0, base=0,
                                pattern=[[0, 4 if u < 4 else 8], [1, P]], channel_multiplier=-1).then_inc(sems["probs_masked"], 1)

            def low(b, e):
                pool.wait_ge(sems["h_hi"], count("h_hi", b, e + 1))
                if e >= HBUF:
                    pool.wait_ge(sems["y_ps"], count("y_ps", b, e + 1 - HBUF))
                g.tensor_tensor(h_lo[e % HBUF][:], h[e % HBUF][:], h_hi[e % HBUF][:], ALU.subtract).then_inc(sems["h_lo"], 1)

            def ffn_norm(b):
                variance("d", b)
                pool.wait_ge(sems["cb"], 1)
                pool.wait_ge(sems["x3"], count("x3", b))
                g.tensor_tensor(x3b[:], x3[:], cb[:].rearrange("p (a c) -> p a c", a=1).broadcast_to([P, TT, C]),
                                ALU.add).then_inc(sems["x3b"], 1)

            run(dict(norm=lambda b: variance("a", b), turn=turn, ones_row=ones_row, gamma=first_constants, score=score, low=low, exp_norm=lambda b: variance("b", b), att_norm=lambda b: variance("c", b),
                     ffn_norm=ffn_norm, ffn_hidden=lambda b: variance("g", b)), pool.Fori)

        @block.tensor
        def _(pe):
            mm = nc.tensor.matmul
            pe.wait_ge(sems["masks"], 4)
            pe.wait_ge(sems["sel"], 1)
            pe.wait_ge(sems["w_in"], 64)
            pe.wait_ge(sems["b_in"], 64)

            def centre(o, n):
                mm(o, center[:], raw[:, n, :], start=True, stop=False)
                return mm(o, sel[:, n, :], (brow[0:E, :] if n < 4 else brow_b[:]), start=False, stop=True)

            for n in range(4):
                centre(ps[:, 0, n * P:(n + 1) * P], n).then_inc(sems["cen_ps"], 1)

            def weights(_):
                pe.wait_ge(sems["b_track_w_in"], 64)
                for n in (4, 5):
                    centre(MS[:, (n - 4) * P:(n - 3) * P], n).then_inc(sems["cen_ps"], 1)

            def w1_step(_, e):
                if e == 0:
                    pe.wait_ge(sems["w1_in"], 32)
                if e >= 2:
                    pe.wait_ge(sems["w1_lo"], e - 1)
                mm(ps[:, 4 + e % 2, :], center[:], staging[:, e * F:(e + 1) * F], start=True, stop=False)
                mm(ps[:, 4 + e % 2, :], sel[:, e, :], b1row[0:E, :], start=False, stop=True).then_inc(sems["w1_ps"], 1)

            def gamma(_):
                pe.wait_ge(sems["consts"], 1)
                pe.wait_ge(sems["absum"], 2)
                pe.wait_ge(sems["cw"], 1)
                mm(MS[:, 0:2], ones[:], absum[:], start=True, stop=True).then_inc(sems["gamma_ps"], 1)

            def turn_ternary(_):
                pe.wait_ge(sems["tern"], 4)
                pe.wait_ge(sems["w1_lo"], E)
                for m in range(2):
                    for c in range(FC):
                        t = nc.tensor.transpose(ps[:, 4 + m, c * P:(c + 1) * P], tern[:, m, c * P:(c + 1) * P], ident[:])
                    t.then_inc(sems["ternT_ps"], 1)

            def fold_ln(_):
                pe.wait_ge(sems["ternT"], 2)
                pe.wait_ge(sems["fold"], 4)
                pe.wait_ge(sems["gamma"], 5)
                for c in range(FC):
                    t = mm(MS[:, 0:P], lnbb[:, c, :], wprT0[:, c, :], start=(c == 0), stop=(c == FC - 1))
                t.then_inc(sems["cb_ps"], 1)

            PARTS = ((0, 0), (1, 0), (0, 1))

            def transposes(dst, src, need_name, b, done):
                pe.wait_ge(sems[need_name], count(need_name, b))
                for t in range(TT):
                    ins = nc.tensor.transpose(dst[:, t * P:(t + 1) * P], src[:, t, :], ident[:])
                ins.then_inc(sems[done], 1)

            def turn(b):
                pe.wait_ge(sems["x1"], before("x1", b))
                transposes(PO[:, 0:T], xn["a"], "a_xn", b, "a_tr")
                transposes(PO[:, T:2 * T], cin, "ctx_in", b, "a_ctx_tr")

            def stacks(b, op):
                if op == 0:
                    pe.wait_ge(sems["expand"], 26)
                    pe.wait_ge(sems["ones_set"], 2)
                    pe.wait_ge(sems["a_xl"], count("a_xl", b))
                    pe.wait_ge(sems["o_num"], before("o_num", b))
                    pe.wait_ge(sems["probs"], before("probs", b))
                if op >= 2:
                    pe.wait_ge(sems["stack"], count("stack", b, op - 1))
                at = T if op == 3 else 0
                for n in range(H // SH):
                    for i, (pw, px) in enumerate(PARTS):
                        w, xs = (wstack_hi, wstack_lo)[pw], (xh["a"], xl["a"])[px]
                        ins = mm(WK[op % 2][:, n * T:(n + 1) * T], w[:, op, n, :, :].rearrange("p g s -> p (g s)"),
                                 xs[:, at:at + T], start=(i == 0), stop=(i == 2))
                ins.then_inc(sems["stack_ps"], 1)

            def values_in(b):
                pe.wait_ge(sems["a_xl"], count("a_xl", b))
                for t in range(2 * TT):
                    for i, (pw, px) in enumerate(PARTS):
                        ins = mm(PO[:, t * P:(t + 1) * P], (xh["a"], xl["a"])[px][:, t * P:(t + 1) * P],
                                 (w_hi, w_lo)[pw][:, 3 if t < TT else 5, :], start=(i == 0), stop=(i == 2))
                ins.then_inc(sems["v_ps"], 1)

            def max_unit(b, u):
                kind, n = MAX_UNITS[u]
                wk = WK[u % 2]
                if u < 2:
                    pe.wait_ge(sems["masks"], 17)
                    pe.wait_ge(sems["stack"], count("stack", b))
                else:
                    pe.wait_ge(sems["max_out"], count("max_out", b, u - 1))
                if kind == "s0":
                    for half in range(2):
                        for k in range(4):
                            hd = 8 * n + 4 * half + k
                            pe.wait_ge(sems["qm_self"], count("qm_self", b, hd + 1))
                            mm(wk[:, (4 * half + k) * P:(4 * half + k + 1) * P], qm[:, hd, 0:P],
                               stack[:, 1, hd // SH, 0:P], start=(k == 0), stop=False, skip_group_check=True)
                        ins = mm(wk[:, half * 512:(half + 1) * 512].rearrange("p (k n) -> p k n", k=4), identb[:],
                                 causal[:].rearrange("p (a n) -> p a n", a=1).broadcast_to([P, 4, P]),
                                 start=False, stop=True, skip_group_check=True)
                elif kind == "s1":
                    for half in range(2):
                        for k in range(2):
                            hd = 4 * n + 2 * half + k
                            at = half * 512 + k * T
                            mm(wk[:, at:at + T], qm[:, hd, P:T], stack[:, 1, hd // SH, :], start=(k == 0), stop=False,
                               skip_group_check=True)
                        ins = mm(wk[:, half * 512:(half + 1) * 512].rearrange("p (k n) -> p k n", k=2)[:, :, P:T], identb[:],
                                 causal[:].rearrange("p (a n) -> p a n", a=1).broadcast_to([P, 2, P]),
                                 start=False, stop=True, skip_group_check=True)
                else:
                    for k in range(4):
                        hd = 4 * (n % 4) + k
                        t = n // 4
                        if t == 0:
                            pe.wait_ge(sems["qm_cross"], count("qm_cross", b, hd + 1))
                        ins = mm(wk[:, k * T:(k + 1) * T], qm[:, H + hd, t * P:(t + 1) * P], stack[:, 3, hd // SH, :],
                                 start=True, stop=True)
                ins.then_inc(sems["max_ps"], 1)

            def turn_max(b, kind):
                pe.wait_ge(sems["max_out"], count("max_out", b, (6, 14)[kind]))
                pe.wait_ge(sems["v_pad"], count("v_pad", b))
                if kind:
                    pe.wait_ge(sems["shift"], count("shift", b, 1))
                for t in range(TT):
                    ins = nc.tensor.transpose(PO[0:H, kind * T + t * P:kind * T + (t + 1) * P], smax[:, kind, t, :], ident[:])
                ins.then_inc(sems["maxT_ps"], 1)

            def score(b, u):
                kind, kb, parts = EXP_UNITS[u]
                if u == 0:
                    pe.wait_ge(sems["shift_self_in"], count("shift_self_in", b))
                if u == 6:
                    pe.wait_ge(sems["shift_cross_in"], count("shift_cross_in", b))
                if u < 2:
                    pe.wait_ge(sems["max_out"], count("max_out", b))
                else:
                    pe.wait_ge(sems["probs"], count("probs", b, u - 1))
                for hd, at, q0, nq in parts:
                    ins = mm(WK[u % 2][:, at:at + nq], stack[:, 1 + 2 * kind, hd // SH, kb * P:(kb + 1) * P],
                             qm[:, kind * H + hd, q0:q0 + nq], start=True, stop=True)
                ins.then_inc(sems["score_ps"], 1)

            def value(b, u):
                kind, kb, parts = EXP_UNITS[u]
                if u < 6:
                    pe.wait_ge(sems["probs_masked"], count("probs_masked", b, u + 1))
                else:
                    pe.wait_ge(sems["probs"], count("probs", b, u + 1))
                if u == 0:
                    pe.wait_ge(sems["shift"], count("shift", b))
                if u == 6:
                    pe.wait_ge(sems["o_sb"], count("o_sb", b, 1))
                for hd, at, q0, nq in parts:
                    j, col = hd % 8 // 2, hd // 8 * T + q0
                    ins = mm(PO[32 * j:32 * j + 32, col:col + nq], vpad[:, kind, kb, hd, :],
                             probs[u % 3][:, at:at + nq], start=(u in (0, 6)), stop=(u in (5, 13)), skip_group_check=True)
                ins.then_inc(sems["pv"], 1)

            def turn_out(b):
                pe.wait_ge(sems["o_sb"], count("o_sb", b))
                for n in range(4 * TT):
                    kind, t, half = n // 4, n // 2 % 2, n % 2
                    ins = nc.tensor.transpose(WK[0][:, n * P:(n + 1) * P], o_sb[:, kind, half, t * P:(t + 1) * P], ident[:])
                ins.then_inc(sems["oT_ps"], 1)

            def turn_y(b):
                transposes(PO[:, 0:T], y, "y", b, "yT_ps")

            def project(b):
                pe.wait_ge(sems["fold"], 1)
                pe.wait_ge(sems["yT"], count("yT", b))
                for t in range(TT):
                    ins = mm(PO[:, t * P:(t + 1) * P], yT[:, t * P:(t + 1) * P], wp[:], start=True, stop=True)
                ins.then_inc(sems["wp_ps"], 1)

            def exp_turn(b):
                pe.wait_ge(sems["b_track_ready"], 1)
                pe.wait_ge(sems["cb"], 1)
                pe.wait_ge(sems["xo"], before("xo", b))
                transposes(MS[:, 0:T], xn["b"], "b_xn", b, "b_tr")

            def gate(b):
                pe.wait_ge(sems["b_xh"], count("b_xh", b))
                for t in range(TT):
                    ins = mm(MS[:, t * P:(t + 1) * P], xT["b"][:, t * P:(t + 1) * P], cw[:, 1, :], start=True, stop=True)
                ins.then_inc(sems["gate_ps"], 1)

            def hidden(b, e):
                if e:
                    pe.wait_ge(sems["h"], count("h", b, e))
                else:
                    pe.wait_ge(sems["kv"], count("kv", b))
                    pe.wait_ge(sems["w1_lo"], E)
                    pe.wait_ge(sems["ternT"], 2)
                    pe.wait_ge(sems["b_xl"], count("b_xl", b))
                    pe.wait_ge(sems["zT"], before("zT", b))
                for c in range(FC):
                    for i, (pw, px) in enumerate(PARTS):
                        ins = mm(HB[:, c * T:(c + 1) * T], (w1_hi, w1_lo)[pw][:, e, c, :], (xh["b"], xl["b"])[px][:],
                                 start=(i == 0), stop=(i == 2))
                ins.then_inc(sems["h_ps"], 1)

            def turn_gate(b):
                transposes(MS[:, 0:T], gw, "gate_w", b, "wT_ps")

            def expert_bias(b):
                pe.wait_ge(sems["fold"], 5)
                pe.wait_ge(sems["wT"], count("wT", b))
                for t in range(TT):
                    ins = mm(MS[:, t * P:(t + 1) * P], wT[:, t * P:(t + 1) * P], b2[:], start=True, stop=True)
                ins.then_inc(sems["b2_ps"], 1)

            def expert(b, e):
                pe.wait_ge(sems["w2_lo"], E)
                pe.wait_ge(sems["h_lo"], count("h_lo", b, e + 1))
                pe.wait_ge(sems["acc"], count("acc", b, 2 * e + 1))
                for t in range(TT):
                    for c in range(FC):
                        for i, (pw, px) in enumerate(PARTS):
                            ins = mm(MS[:, t * P:(t + 1) * P], (h_hi, h_lo)[px][e % HBUF][:, c, t * P:(t + 1) * P],
                                     (w2_hi, w2_lo)[pw][:, e, c, :], start=(c == 0 and i == 0), stop=(c == FC - 1 and i == 2))
                ins.then_inc(sems["y_ps"], 1)

            def att_ctx(b):
                pe.wait_ge(sems["zT"], before("zT", b))
                transposes(ps[:, 4, 0:T], cinb, "ctxb_in", b, "cb_tr")
                pe.wait_ge(sems["cb_cT"], count("cb_cT", b))
                pe.wait_ge(sems["l1w_in"], 64)
                mm(ps[:, 5, 0:T], cxw[:, 2, :], cTb[:], start=True, stop=True)
                for t in range(TT):
                    ins = mm(ps[:, 5, T + t * P:T + (t + 1) * P], cTb[:, t * P:(t + 1) * P], cxw[:, 3, :], start=True, stop=True)
                ins.then_inc(sems["kv_ps"], 1)

            def att_turn(b):
                pe.wait_ge(sems["acc"], count("acc", b))
                transposes(MS[:, 0:T], xn["c"], "c_xn", b, "c_tr")

            def att_q(b):
                pe.wait_ge(sems["c_xT"], count("c_xT", b))
                mm(MS[:, 0:T], cw[:, 0, :], xT["c"][:], start=True, stop=True).then_inc(sems["q1_ps"], 1)

            def att_score(b):
                pe.wait_ge(sems["h"], count("h", b))
                pe.wait_ge(sems["q1"], count("q1", b))
                for t in range(TT):
                    ins = mm(HB[:, t * T:(t + 1) * T], q1[:, t * P:(t + 1) * P], kv1[:, 0:T], start=True, stop=True)
                ins.then_inc(sems["s1_ps"], 1)

            def att_turn_p(b):
                pe.wait_ge(sems["p1"], count("p1", b))
                for kb in range(TT):
                    for t in range(TT):
                        ins = nc.tensor.transpose(MS[:, kb * T + t * P:kb * T + (t + 1) * P], p1[:, t, kb * P:(kb + 1) * P], ident[:])
                ins.then_inc(sems["p1T_ps"], 1)

            def att_out(b):
                pe.wait_ge(sems["p1T"], count("p1T", b))
                for t in range(TT):
                    for kb in range(TT):
                        ins = mm(MS[:, t * P:(t + 1) * P], p1T[:, kb, t * P:(t + 1) * P], kv1[:, T + kb * P:T + (kb + 1) * P], start=(kb == 0), stop=(kb == TT - 1))
                ins.then_inc(sems["o1_ps"], 1)

            def ffn_turn(b):
                pe.wait_ge(sems["x3"], count("x3", b))
                transposes(MS[:, 0:T], xn["d"], "d_xn", b, "d_tr")

            def ffn_hidden(b):
                pe.wait_ge(sems["d_xl"], count("d_xl", b))
                for t in range(TT):
                    mm(HB[:, t * F:(t + 1) * F], xh["d"][:, t * P:(t + 1) * P], wfcT[:], start=True, stop=False)
                    ins = mm(HB[:, t * F:(t + 1) * F], xl["d"][:, t * P:(t + 1) * P], wfcT[:], start=False, stop=True)
                ins.then_inc(sems["f_ps"], 1)

            def ffn_turn_z(b):
                pe.wait_ge(sems["z"], count("z", b))
                for c in range(FC):
                    for t in range(TT):
                        ins = nc.tensor.transpose(HB[:, c * T + t * P:c * T + (t + 1) * P], z[:, t, c * P:(c + 1) * P], ident[:])
                ins.then_inc(sems["zT_ps"], 1)

            def ffn_out(b):
                pe.wait_ge(sems["wprT"], FC)
                pe.wait_ge(sems["zT"], count("zT", b))
                for t in range(TT):
                    for c in range(FC):
                        ins = mm(MS[:, t * P:(t + 1) * P], zT[:, c, t * P:(t + 1) * P], wprT[:, c, :], start=(c == 0), stop=(c == FC - 1))
                ins.then_inc(sems["f2_ps"], 1)

            run(dict(turn=turn, stacks=stacks, values_in=values_in, max_unit=max_unit, turn_max=turn_max, score=score, value=value,
                     turn_out=turn_out, turn_y=turn_y, project=project, exp_turn=exp_turn, gate=gate, hidden=hidden,
                     turn_gate=turn_gate, expert_bias=expert_bias, expert=expert, att_turn=att_turn, att_ctx=att_ctx, att_q=att_q,
                     att_score=att_score, att_turn_p=att_turn_p, att_out=att_out, ffn_turn=ffn_turn, ffn_hidden=ffn_hidden,
                     ffn_turn_z=ffn_turn_z, ffn_out=ffn_out, weights=weights, w1=w1_step, gamma=gamma, turn_ternary=turn_ternary,
                     fold_ln=fold_ln), pe.Fori)

        @block.scalar
        def _(act):
            sc = nc.scalar
            act.wait_ge(sems["ctxw_zero"], 1)
            for n, (w, b) in enumerate([(L0_xattn_Wck, L0_xattn_bck), (L0_xattn_Wcv, L0_xattn_bcv)]):
                act.dma_start(cxw[0:CC, n, :], w).then_inc(sems["ctxw_in"], 16)
                act.dma_start(cxw[CC:CC + 1, n, :], row(b)).then_inc(sems["ctxw_in"], 16)
            act.wait_ge(sems["ctxw_in"], 64)
            sc.activation(w_hi[:, 4:6, :].rearrange("p n c -> p (n c)"), cxw[:, 0:2, :].rearrange("p n c -> p (n c)"), ACT.Copy,
                          scale=SCALE).then_inc(sems["w_hi"], 1)
            act.wait_ge(sems["cen_ps"], 4)
            sc.activation(w_hi[:, 0:4, :].rearrange("p n c -> p (n c)"), ps[:, 0, :], ACT.Copy, scale=SCALE)\
                .then_inc(sems["w_hi"], 1)

            def weights(_):
                act.wait_ge(sems["cen_ps"], 6)
                sc.copy(cw[:].rearrange("p n c -> p (n c)"), MS[:, 0:2 * P]).then_inc(sems["cw"], 1)

            def fold_gates(_):
                act.wait_ge(sems["bp_in"], 64)
                sc.activation(gates[:], graw[:], ACT.Tanh).then_inc(sems["gates"], 1)

            def w1_step(_, e):
                act.wait_ge(sems["w1_ps"], e + 1)
                sc.activation(w1_hi[:, e, :, :].rearrange("p c f -> p (c f)"), ps[:, 4 + e % 2, :], ACT.Copy, scale=SCALE)\
                    .then_inc(sems["w1_hi"], 1)

            def w2_step(_, e):
                act.wait_ge(sems["w2_in"], 16)
                sc.activation(w2_hi[:, e, :, :].rearrange("p c f -> p (c f)"), staging[:, e * F:(e + 1) * F], ACT.Copy, scale=SCALE)\
                    .then_inc(sems["w2_hi"], 1)

            def turn(b):
                act.wait_ge(sems["a_ctx_tr"], count("a_ctx_tr", b))
                act.wait_ge(sems["v_ps"], before("v_ps", b))
                act.wait_ge(sems["stack_ps"], before("stack_ps", b))
                sc.copy(xh["a"][:], PO).then_inc(sems["a_xh"], 1)

            def stacks(b, op):
                if op == 0:
                    act.wait_ge(sems["gamma"], 4)
                    act.wait_ge(sems["stack"], before("stack", b))
                act.wait_ge(sems["stack_ps"], count("stack_ps", b, op + 1))
                sc.activation(hi[:, op, :, :].rearrange("p o t -> p (o t)"), WK[op % 2], ACT.Copy,
                              scale=(lo_k if op % 2 else lo_q)[:, 0:1]).then_inc(sems["stack_hi"], 1)

            def values_in(b):
                act.wait_ge(sems["v_ps"], count("v_ps", b))
                act.wait_ge(sems["pv"], before("pv", b))
                act.wait_ge(sems["v_ready"], 2)
                for s in range(2):
                    dst = vpad[:].rearrange("p k t (j s) c -> p s (k t j) c", s=2)[:, s, :, 16 * s:16 * s + D]
                    sc.activation(dst, PO.rearrange("p (n s d) -> p s n d", s=2, d=D)[:, s], ACT.Copy, scale=1 / SCALE)\
                        .then_inc(sems["v_pad"], 1)

            def score(b, u):
                act.wait_ge(sems["score_ps"], count("score_ps", b, u + 1))
                if u >= 3:
                    act.wait_ge(sems["pv"], count("pv", b, u - 2))
                sc.activation(probs[u % 3][:], WK[u % 2], ACT.Exp, scale=D ** -0.5).then_inc(sems["probs"], 1)

            def value(b, u):
                if u not in (5, 13):
                    return
                kind = int(u == 13)
                act.wait_ge(sems["pv"], count("pv", b, u + 1))
                act.wait_ge(sems["oT_ps"], before("oT_ps", b))
                sc.copy(o_sb[:, kind, :, :].rearrange("p r t -> p (r t)"), PO).then_inc(sems["o_sb"], 1)

            def turn_y(b):
                act.wait_ge(sems["yT_ps"], count("yT_ps", b))
                sc.copy(yT[:], PO[:, 0:T]).then_inc(sems["yT"], 1)

            def exp_turn(b):
                act.wait_ge(sems["b_tr"], count("b_tr", b))
                sc.copy(xT["b"][:], MS[:, 0:T]).then_inc(sems["b_xT"], 1)
                sc.copy(xh["b"][:], MS[:, 0:T]).then_inc(sems["b_xh"], 1)

            def gate(b):
                act.wait_ge(sems["gate"], count("gate", b, 2))
                sc.activation(gt[:, 1, :, :], gt[:, 0, :, :], ACT.Exp).then_inc(sems["gate_e"], 1)

            def turn_gate(b):
                act.wait_ge(sems["wT_ps"], count("wT_ps", b))
                sc.copy(wT[:], MS[:, 0:T]).then_inc(sems["wT"], 1)

            def hidden(b, e):
                act.wait_ge(sems["h_ps"], count("h_ps", b, e + 1))
                if e >= HBUF:
                    act.wait_ge(sems["h_lo"], count("h_lo", b, e + 1 - HBUF))
                    act.wait_ge(sems["y_ps"], count("y_ps", b, e + 1 - HBUF))
                sc.activation(h[e % HBUF][:].rearrange("p c t -> p (c t)"), HB, ACT.Gelu_apprx_tanh, scale=1 / SCALE)\
                    .then_inc(sems["h"], 1)
                act.wait_ge(sems["h"], count("h", b, e + 1))
                sc.copy(h_hi[e % HBUF][:].rearrange("p c t -> p (c t)"), h[e % HBUF][:].rearrange("p c t -> p (c t)"))\
                    .then_inc(sems["h_hi"], 1)

            def att_ctx(b):
                act.wait_ge(sems["cb_tr"], count("cb_tr", b))
                sc.copy(cTb[:], ps[:, 4, 0:T]).then_inc(sems["cb_cT"], 1)
                act.wait_ge(sems["kv_ps"], count("kv_ps", b))
                sc.copy(kv1[:], ps[:, 5, :]).then_inc(sems["kv"], 1)

            def att_turn(b):
                act.wait_ge(sems["c_tr"], count("c_tr", b))
                sc.copy(xT["c"][:], MS[:, 0:T]).then_inc(sems["c_xT"], 1)

            def att_q(b):
                act.wait_ge(sems["q1_ps"], count("q1_ps", b))
                sc.copy(q1[:], MS[:, 0:T]).then_inc(sems["q1"], 1)

            def att_score(b):
                act.wait_ge(sems["s1_max"], count("s1_max", b))
                for t in range(TT):
                    sc.activation(p1[:, t, :], HB[:, t * T:(t + 1) * T], ACT.Exp, bias=s1max[:, t:t + 1],
                                  accum_out=s1sum[:, t:t + 1]).then_inc(sems["p1"], 1)

            def att_turn_p(b):
                act.wait_ge(sems["p1T_ps"], count("p1T_ps", b))
                sc.copy(p1T[:].rearrange("p k t -> p (k t)"), MS).then_inc(sems["p1T"], 1)

            def ffn_turn(b):
                act.wait_ge(sems["d_tr"], count("d_tr", b))
                sc.copy(xh["d"][:], MS[:, 0:T]).then_inc(sems["d_xh"], 1)

            def ffn_hidden(b):
                act.wait_ge(sems["f_ps"], count("f_ps", b))
                sc.activation(fh[:].rearrange("p t f -> p (t f)"), HB, ACT.Gelu).then_inc(sems["f"], 1)

            def ffn_turn_z(b):
                act.wait_ge(sems["zT_ps"], count("zT_ps", b))
                sc.copy(zT[:].rearrange("p c t -> p (c t)"), HB).then_inc(sems["zT"], 1)

            run(dict(turn=turn, stacks=stacks, values_in=values_in, score=score, value=value, turn_y=turn_y, exp_turn=exp_turn,
                     gate=gate, turn_gate=turn_gate, hidden=hidden, att_turn=att_turn, att_ctx=att_ctx, att_q=att_q,
                     att_score=att_score, att_turn_p=att_turn_p, ffn_turn=ffn_turn, ffn_hidden=ffn_hidden,
                     ffn_turn_z=ffn_turn_z, weights=weights, fold_gates=fold_gates, w1=w1_step,
                     w2=w2_step), act.Fori)

        @block.vector
        def _(dve):
            v = nc.vector
            v.memset(wstack_hi[:], 0.0).then_inc(sems["expand"], 1)
            v.memset(wstack_lo[:], 0.0).then_inc(sems["expand"], 1)
            dve.wait_ge(sems["masks"], 11)
            v.tensor_reduce(lo_q[:], low8[:, 0, :], AX.X, ALU.add, negate=True).then_inc(sems["gamma"], 1)
            v.tensor_reduce(lo_k[:], low8[:, 1, :], AX.X, ALU.add, negate=True).then_inc(sems["gamma"], 1)
            dve.wait_ge(sems["gamma"], 2)
            v.tensor_scalar(lo_q[:], lo_q[:], 1 / SCALE, None, ALU.mult).then_inc(sems["gamma"], 1)
            v.tensor_scalar(lo_k[:], lo_k[:], 1 / SCALE, None, ALU.mult).then_inc(sems["gamma"], 1)

            def spread(_):
                dve.wait_ge(sems["w_hi"], 1)
                v.scalar_tensor_tensor(out=w_lo[:, 4:6, :], in0=cxw[:, 0:2, :], scalar=SCALE, in1=w_hi[:, 4:6, :], op0=ALU.mult,
                                       op1=ALU.subtract).then_inc(sems["w_lo"], 1)
                dve.wait_ge(sems["w_hi"], 2)
                v.scalar_tensor_tensor(out=w_lo[:, 0:4, :], in0=ps[:, 0, :].rearrange("p (n c) -> p n c", n=4), scalar=SCALE,
                                       in1=w_hi[:, 0:4, :], op0=ALU.mult, op1=ALU.subtract).then_inc(sems["w_lo"], 1)
                dve.wait_ge(sems["w_lo"], 2)
                dve.wait_ge(sems["expand"], 2)
                for op, n in enumerate((0, 1, 2, 4)):
                    for r in range(3):
                        for dst, w in ((wstack_hi, w_hi), (wstack_lo, w_lo)):
                            v.tensor_copy(dst[:, op, :, :, r * D:(r + 1) * D].rearrange("p o g d -> p (o g) d"),
                                          w[:, n, :].rearrange("p (h d) -> p h d", d=D)).then_inc(sems["expand"], 1)

            def fold_gates(_):
                dve.wait_ge(sems["gates"], 1)
                v.tensor_scalar(wp[:], wp[:], gates[:, 0:1], None, ALU.mult).then_inc(sems["fold"], 1)
                v.tensor_scalar(bp[:], bp[:], gates[:, 0:1], None, ALU.mult).then_inc(sems["fold"], 1)

            def w1_step(_, e):
                dve.wait_ge(sems["w1_hi"], e + 1)
                v.scalar_tensor_tensor(out=w1_lo[:, e, :, :].rearrange("p c f -> p (c f)"), in0=ps[:, 4 + e % 2, :], scalar=SCALE,
                                       in1=w1_hi[:, e, :, :].rearrange("p c f -> p (c f)"), op0=ALU.mult, op1=ALU.subtract)\
                    .then_inc(sems["w1_lo"], 1)

            def w2_step(_, e):
                dve.wait_ge(sems["w2_hi"], e + 1)
                v.scalar_tensor_tensor(out=w2_lo[:, e, :, :].rearrange("p c f -> p (c f)"), in0=staging[:, e * F:(e + 1) * F],
                                       scalar=SCALE, in1=w2_hi[:, e, :, :].rearrange("p c f -> p (c f)"), op0=ALU.mult,
                                       op1=ALU.subtract).then_inc(sems["w2_lo"], 1)

            def gamma(_):
                dve.wait_ge(sems["wf_in"], 48)
                v.tensor_reduce(absum[:, 0:1], wfc_raw.rearrange("p c d -> p (c d)"), AX.X, ALU.add,
                                apply_absolute_value=True).then_inc(sems["absum"], 1)
                v.tensor_reduce(absum[:, 1:2], wpr_raw, AX.X, ALU.add, apply_absolute_value=True).then_inc(sems["absum"], 1)

            def ternary(_):
                dve.wait_ge(sems["gamma_ps"], 1)
                v.tensor_scalar(thr[:, 0, :], MS[:, 0:2], 0.5 / (F * C), 0.5e-6, ALU.mult, ALU.add).then_inc(sems["gamma"], 1)
                dve.wait_ge(sems["gamma"], 5)
                v.tensor_scalar(thr[:, 1, :], thr[:, 0, :], -1.0, None, ALU.mult).then_inc(sems["gamma"], 1)
                dve.wait_ge(sems["gamma"], 6)
                for m, w in enumerate((wfc_raw.rearrange("p c d -> p (c d)"), wpr_raw)):
                    v.tensor_scalar(tneg, w, thr[:, 1, m:m + 1], None, ALU.is_lt).then_inc(sems["tern"], 1)
                    dve.wait_ge(sems["tern"], 2 * m + 1)
                    v.scalar_tensor_tensor(out=tern[:, m, :], in0=w, scalar=thr[:, 0, m:m + 1], in1=tneg, op0=ALU.is_gt,
                                           op1=ALU.subtract).then_inc(sems["tern"], 1)
                    dve.wait_ge(sems["tern"], 2 * m + 2)

            def turn_ternary(_):
                dve.wait_ge(sems["lnw_in"], 32)
                v.tensor_scalar(lnwg[:], lnw[:], gates[:, 3:4], None, ALU.mult).then_inc(sems["fold"], 1)
                v.tensor_copy(lnbb, lnb[:].rearrange("p (c a) -> p c a", a=1).broadcast_to([P, FC, P])).then_inc(sems["fold"], 1)
                dve.wait_ge(sems["ternT_ps"], 2)
                v.tensor_copy(wfcT[:], ps[:, 4, :]).then_inc(sems["ternT"], 1)
                v.tensor_copy(wprT0.rearrange("p c d -> p (c d)"), ps[:, 5, :]).then_inc(sems["ternT"], 1)
                dve.wait_ge(sems["ternT"], 2)
                dve.wait_ge(sems["fold"], 3)
                for c in range(FC):
                    v.tensor_scalar(wprT[:, c, :], wprT0[:, c, :], lnwg[:, c:c + 1], None, ALU.mult).then_inc(sems["wprT"], 1)

            def fold_ln(_):
                dve.wait_ge(sems["cb_ps"], 1)
                v.tensor_scalar(cb[:], MS[:, 0:P], gates[:, 3:4], None, ALU.mult).then_inc(sems["cb"], 1)

            def fold_b2(_):
                v.tensor_scalar(b2[:], b2[:], SCALE, None, ALU.mult).then_inc(sems["fold"], 1)
                v.tensor_scalar(gate_scale[:], gates[:, 2:3], 1 / SCALE, None, ALU.mult).then_inc(sems["fold"], 1)

            def statistics(k, src, b):
                for t in range(TT):
                    v.bn_stats(stats[k][:, t, :], src[:, t, :]).then_inc(sems[k + "_stats"], 1)
                for t in range(TT):
                    dve.wait_ge(sems[k + "_stats"], count(k + "_stats", b, t + 1))
                    dve.sem_inc(sems["dve_passed"], 1)
                    v.bn_aggr(mv[k][:, t, :], stats[k][:, t, :]).then_inc(sems[k + "_mv"], 1)

            def normalise(k, src, dst, width, done, b):
                dve.wait_ge(sems[k + "_rstd"], count(k + "_rstd", b))
                for t in range(TT):
                    v.tensor_scalar(dst[:, t, 0:width], src[:, t, 0:width], mv[k][:, t, 0:1], rstd[k][:, t:t + 1],
                                    ALU.subtract, ALU.mult).then_inc(sems[done], 1)

            def norm(b):
                dve.wait_ge(sems["x_in"], count("x_in", b))
                statistics("a", xin, b)
                dve.wait_ge(sems["a_tr"], before("a_tr", b))
                normalise("a", xin, xn["a"], C - 1, "a_xn", b)

            def turn(b):
                dve.wait_ge(sems["a_xh"], count("a_xh", b))
                v.tensor_tensor(xl["a"][:], PO, xh["a"][:], ALU.subtract).then_inc(sems["a_xl"], 1)

            def split(b, op):
                if op == 0:
                    dve.wait_ge(sems["score_ps"], before("score_ps", b))
                dve.wait_ge(sems["stack_hi"], count("stack_hi", b, op + 1))
                v.scalar_tensor_tensor(out=stack[:, op, :, :].rearrange("p o t -> p (o t)"),
                                       in0=WK[op % 2], scalar=1 / SCALE, in1=hi[:, op, :, :].rearrange("p o t -> p (o t)"),
                                       op0=ALU.mult, op1=ALU.add).then_inc(sems["stack"], 1)

            def mask(b, kind, part):
                dve.wait_ge(sems["masks"], 14)
                dve.wait_ge(sems["stack"], count("stack", b, 2 * kind + 1))
                for n in range(4 * part, 4 * part + 4):
                    v.tensor_scalar(qm[:, kind * H + n, :], stack[:, 2 * kind, n // SH, :], head_mask[:, n % SH:n % SH + 1], None,
                                    ALU.mult).then_inc(sems[("qm_self", "qm_cross")[kind]], 1)

            def maxima(b, u):
                kind, n = MAX_UNITS[u]
                if u == 0:
                    dve.wait_ge(sems["maxT_ps"], before("maxT_ps", b))
                dve.wait_ge(sems["max_ps"], count("max_ps", b, u + 1))
                wk = WK[u % 2]
                if kind == "s0":
                    o, i = smax[:, 0, 0, 8 * n:8 * n + 8], wk.rearrange("p (h k) -> p h k", k=P)
                elif kind == "s1":
                    o, i = smax[:, 0, 1, 4 * n:4 * n + 4], wk.rearrange("p (h k) -> p h k", k=T)
                else:
                    o, i = smax[:, 1, n // 4, 4 * (n % 4):4 * (n % 4) + 4], wk.rearrange("p (h k) -> p h k", k=T)
                v.tensor_reduce(o, i, AX.X, ALU.max).then_inc(sems["max_out"], 1)

            def turn_max(b, kind):
                dve.wait_ge(sems["maxT_ps"], count("maxT_ps", b, kind + 1))
                name = ("shift_self_in", "shift_cross_in")[kind]
                dve.wait_ge(sems[name], before(name, b))
                v.tensor_scalar(shift[:, kind, :], PO[0:H, kind * T:(kind + 1) * T], -1.0, -SHIFT_MAX, ALU.mult,
                                ALU.max).then_inc(sems["shift"], 1)

            def turn_out(b):
                dve.wait_ge(sems["oT_ps"], count("oT_ps", b))
                o = WK[0].rearrange("p (n h r) -> p n h r", n=2 * TT, r=16)
                v.reciprocal(o_rec[:], o[:, :, :, D:D + 1]).then_inc(sems["o_rec"], 1)
                dve.wait_ge(sems["o_rec"], count("o_rec", b))
                v.tensor_tensor(o_num[:], o[:, :, :, 0:D], o_rec[:].broadcast_to([P, 2 * TT, H, D]), ALU.mult)\
                    .then_inc(sems["o_num"], 1)
                dve.wait_ge(sems["o_num"], count("o_num", b))
                dve.wait_ge(sems["yT_ps"], before("yT_ps", b))
                v.tensor_tensor(y[:], o_num[:, 0:TT].rearrange("p t h d -> p t (h d)"),
                                o_num[:, TT:2 * TT].rearrange("p t h d -> p t (h d)"), ALU.add).then_inc(sems["y"], 1)

            def project(b):
                dve.wait_ge(sems["wp_ps"], count("wp_ps", b))
                dve.wait_ge(sems["xb"], count("xb", b))
                v.tensor_tensor(x1[:], PO[:, 0:T].rearrange("p (t c) -> p t c", t=TT), xb[:], ALU.add).then_inc(sems["x1"], 1)

            def exp_norm(b):
                dve.wait_ge(sems["b_track_ready"], 1)
                dve.wait_ge(sems["x1"], count("x1", b))
                statistics("b", x1, b)
                dve.wait_ge(sems["b_tr"], before("b_tr", b))
                normalise("b", x1, xn["b"], C - 1, "b_xn", b)

            def gate(b):
                dve.wait_ge(sems["gate_ps"], count("gate_ps", b))
                dve.wait_ge(sems["wT_ps"], before("wT_ps", b))
                lg = MS[:, 0:T].rearrange("p (t e) -> p t e", t=TT)[:, :, 0:E]
                step = [0]

                def gate(ins):
                    step[0] += 1
                    ins.then_inc(sems["gate"], 1)
                    dve.wait_ge(sems["gate"], count("gate", b, step[0]))

                def wide(n):
                    return gs[:, n, :, :].broadcast_to([P, TT, E])

                rk = rank[:].rearrange("p (a e) -> p a e", a=1).broadcast_to([P, TT, E])
                gate(v.tensor_reduce(gs[:, 0, :, 0], lg, AX.X, ALU.max))
                gate(v.tensor_tensor(gt[:, 0], lg, wide(0), ALU.subtract))
                gate(v.scalar_tensor_tensor(out=gt[:, 4], in0=gt[:, 0], scalar=0.0, in1=rk, op0=ALU.is_equal, op1=ALU.mult))
                gate(v.tensor_reduce(gs[:, 2, :, 0], gt[:, 4], AX.X, ALU.max))
                gate(v.tensor_tensor(gt[:, 5], rk, wide(2), ALU.is_equal))
                gate(v.scalar_tensor_tensor(out=gt[:, 7], in0=gt[:, 5], scalar=MASKED, in1=gt[:, 0], op0=ALU.mult, op1=ALU.add))
                gate(v.tensor_reduce(gs[:, 1, :, 0], gt[:, 7], AX.X, ALU.max))
                gate(v.tensor_tensor(gt[:, 3], gt[:, 7], wide(1), ALU.is_equal))
                gate(v.tensor_tensor(gt[:, 4], gt[:, 3], rk, ALU.mult))
                gate(v.tensor_reduce(gs[:, 3, :, 0], gt[:, 4], AX.X, ALU.max))
                gate(v.tensor_tensor(gt[:, 6], rk, wide(3), ALU.is_equal))
                gate(v.tensor_tensor(gt[:, 8], gt[:, 5], gt[:, 6], ALU.add))
                dve.wait_ge(sems["fold"], 6)
                dve.wait_ge(sems["gate_e"], count("gate_e", b))
                gate(v.tensor_tensor(gt[:, 9], gt[:, 1], gt[:, 8], ALU.mult))
                gate(v.tensor_reduce(gs[:, 4, :, 0], gt[:, 9], AX.X, ALU.add))
                gate(v.tensor_reduce(gs[:, 5, :, 0], gt[:, 1], AX.X, ALU.add))
                gate(v.scalar_tensor_tensor(out=gs[:, 6], in0=gs[:, 5], scalar=1e-8, in1=gs[:, 4], op0=ALU.mult, op1=ALU.add))
                gate(v.reciprocal(gs[:, 7], gs[:, 6]))
                v.scalar_tensor_tensor(out=gw[:, :, 0:E], in0=gt[:, 9], scalar=gate_scale[:, 0:1], in1=wide(7), op0=ALU.mult,
                                       op1=ALU.mult).then_inc(sems["gate_w"], 1)

            def expert_bias(b):
                dve.wait_ge(sems["b2_ps"], count("b2_ps", b))
                dve.wait_ge(sems["x3"], before("x3", b))
                v.tensor_tensor(acc[:], MS[:, 0:T].rearrange("p (t c) -> p t c", t=TT), x1[:], ALU.add).then_inc(sems["acc"], 1)

            def exp_turn(b):
                dve.wait_ge(sems["b_xh"], count("b_xh", b))
                v.tensor_tensor(xl["b"][:], xT["b"][:], xh["b"][:], ALU.subtract).then_inc(sems["b_xl"], 1)

            def add(b, e):
                dve.wait_ge(sems["y_ps"], count("y_ps", b, e + 1))
                dve.wait_ge(sems["acc"], count("acc", b, 2 * e + 1))
                for t in range(TT):
                    v.scalar_tensor_tensor(out=acc[:, t, :], in0=MS[:, t * P:(t + 1) * P], scalar=gw[:, t, e:e + 1], in1=acc[:, t, :],
                                           op0=ALU.mult, op1=ALU.add).then_inc(sems["acc"], 1)

            def att_norm(b):
                dve.wait_ge(sems["acc"], count("acc", b))
                statistics("c", acc, b)
                dve.wait_ge(sems["c_tr"], before("c_tr", b))
                normalise("c", acc, xn["c"], C - 1, "c_xn", b)

            def att_score(b):
                dve.wait_ge(sems["s1_ps"], count("s1_ps", b))
                v.tensor_reduce(s1max[:], HB[:, 0:TT * T].rearrange("p (t k) -> p t k", t=TT), AX.X, ALU.max, negate=True)\
                    .then_inc(sems["s1_max"], 1)

            def att_out(b):
                dve.wait_ge(sems["gates"], 1)
                dve.wait_ge(sems["p1"], count("p1", b))
                v.reciprocal(s1rec[:], s1sum[:]).then_inc(sems["s1_rec"], 1)
                dve.wait_ge(sems["s1_rec"], count("s1_rec", b))
                v.tensor_scalar(s1scale[:], s1rec[:], gates[:, 1:2], None, ALU.mult).then_inc(sems["s1_scale"], 1)
                dve.wait_ge(sems["s1_scale"], count("s1_scale", b))
                dve.wait_ge(sems["o1_ps"], count("o1_ps", b))
                dve.wait_ge(sems["x3b"], before("x3b", b))
                for t in range(TT):
                    v.scalar_tensor_tensor(out=x3[:, t, :], in0=MS[:, t * P:(t + 1) * P], scalar=s1scale[:, t:t + 1],
                                           in1=acc[:, t, :], op0=ALU.mult, op1=ALU.add).then_inc(sems["x3"], 1)

            def ffn_norm(b):
                dve.wait_ge(sems["x3"], count("x3", b))
                statistics("d", x3, b)
                dve.wait_ge(sems["d_tr"], before("d_tr", b))
                normalise("d", x3, xn["d"], C, "d_xn", b)

            def ffn_turn(b):
                dve.wait_ge(sems["d_xh"], count("d_xh", b))
                v.tensor_tensor(xl["d"][:], MS[:, 0:T], xh["d"][:], ALU.subtract).then_inc(sems["d_xl"], 1)

            def ffn_hidden(b):
                dve.wait_ge(sems["f"], count("f", b))
                statistics("g", fh, b)
                dve.wait_ge(sems["zT_ps"], before("zT_ps", b))
                normalise("g", fh, z, F, "z", b)

            def ffn_out(b):
                dve.wait_ge(sems["f2_ps"], count("f2_ps", b))
                dve.wait_ge(sems["x3b"], count("x3b", b))
                dve.wait_ge(sems["out"], before("out", b))
                v.tensor_tensor(xo[:], MS[:, 0:T].rearrange("p (t c) -> p t c", t=TT), x3b[:], ALU.add).then_inc(sems["xo"], 1)

            run(dict(norm=norm, split=split, mask=mask, maxima=maxima, turn_max=turn_max, turn_out=turn_out, project=project,
                     exp_norm=exp_norm, gate=gate, expert_bias=expert_bias, add=add, att_norm=att_norm,
                     att_score=att_score, att_out=att_out, ffn_norm=ffn_norm, ffn_hidden=ffn_hidden, ffn_out=ffn_out,
                     turn=turn, spread=spread, fold_gates=fold_gates, exp_turn=exp_turn, ffn_turn=ffn_turn, w1=w1_step, w2=w2_step, gamma=gamma,
                     ternary=ternary, turn_ternary=turn_ternary, fold_ln=fold_ln, fold_b2=fold_b2), dve.Fori)


_INS = ["x", "ctx_512", "g_xattn", "g_ffn", "L0_xattn_Wk", "L0_xattn_bk", "L0_xattn_Wq", "L0_xattn_bq", "L0_xattn_Wv",
        "L0_xattn_bv", "L0_xattn_Wck", "L0_xattn_bck", "L0_xattn_Wcq", "L0_xattn_bcq", "L0_xattn_Wcv", "L0_xattn_bcv",
        "L0_xattn_Wp", "L0_xattn_bp", "L0_ffn_Wg", "L0_ffn_bg", "L0_ffn_W1", "L0_ffn_b1", "L0_ffn_W2", "L0_ffn_b2",
        "L1_xattn_Wq", "L1_xattn_bq", "L1_xattn_Wk", "L1_xattn_bk", "L1_xattn_Wv", "L1_xattn_bv", "L1_ffn_W_fc",
        "L1_ffn_ln_w", "L1_ffn_ln_b", "L1_ffn_W_proj"]


def kernel(**inputs):
    import numpy as _np
    import concourse.bacc as _bacc
    from concourse import mybir as _mybir
    from concourse.bass_utils import run_bass_kernel_spmd as _run

    nc = _bacc.Bacc("TRN2", target_bir_lowering=False, num_devices=1)
    arrays, args = {}, []
    for name in _INS:
        a = _np.ascontiguousarray(inputs[name])
        arrays[f"in_{name}_dram"] = a
        args.append(nc.dram_tensor(f"in_{name}_dram", a.shape, _mybir.dt.from_np(a.dtype), kind="ExternalInput").ap())
    out = nc.dram_tensor("out_0_dram", (B, T, C), _mybir.dt.float32, kind="ExternalOutput").ap()
    flamingo(nc, *args, out)
    r = _run(nc, [arrays], core_ids=[0])
    return r.results[0]["out_0_dram"]
```
